# Optimizing a Trainium2 kernel written in Bass

```python
import numpy as np
import jax
import jax.numpy as jnp

def _softmax(x, axis=-1):
    return jax.nn.softmax(x, axis=axis)

def _gelu(x):
    return jax.nn.gelu(x, approximate=True)

def _silu(x):
    return jax.nn.silu(x)

def _sigmoid(x):
    return jax.nn.sigmoid(x)

def _layernorm(x, axis=-1, eps=1e-05):
    m = jnp.mean(x, axis=axis, keepdims=True)
    v = jnp.var(x, axis=axis, keepdims=True)
    return (x - m) / jnp.sqrt(v + eps)

def _scatter_add(tgt, idx, src, axis=0):
    return tgt.at[idx].add(src)

def _segment_sum(src, seg, n):
    return jax.ops.segment_sum(src, seg, n)
kernel_name = 'mk_xattn_ffn_d1_seqx_r4_fed713'

def setup_inputs(seed: int=0):
    np.random.seed(seed)
    _w = jnp.asarray

    def _rec_inputs():
        import jax
        import jax.numpy as jnp
        _rk = jax.random.key(seed)
        x = -0.0005146 + 1 * jax.random.normal(jax.random.fold_in(_rk, 1), (4, 1024, 256), jnp.float32)
        _lenS = 1024 - jax.random.randint(jax.random.fold_in(_rk, 7), (4,), 0, max(1, 1024 // 4) + 1, jnp.int32)
        _lenS2 = 77 - jax.random.randint(jax.random.fold_in(_rk, 8), (4,), 0, max(1, 77 // 4) + 1, jnp.int32)
        _ctx_768P = jax.random.normal(jax.random.fold_in(_rk, 11), (4, 16, 192), jnp.float32)
        _ctx_768c = jax.random.dirichlet(jax.random.fold_in(_rk, 511), 0.3 * jnp.ones((16,), jnp.float32), (4, 77))
        _ctx_768t = jnp.einsum('bsk,bkd->bsd', _ctx_768c, _ctx_768P)
        _ctx_768t = _ctx_768t * jax.lax.rsqrt(jnp.mean(jnp.square(_ctx_768t)) + 1e-12) * 0.953939
        ctx_768 = -0.00040386 + 0.999972 * (_ctx_768t + 0.3 * jax.random.normal(jax.random.fold_in(_rk, 611), (4, 77, 192), jnp.float32))
        _validS = jnp.arange(1024)[None, :] < _lenS[:, None]
        _validS2 = jnp.arange(77)[None, :] < _lenS2[:, None]
        _causal = jnp.tril(jnp.ones((1024, 1024), dtype=bool))
        mask_BxS2_bk0 = jnp.logical_not(jnp.broadcast_to(_validS2[:, :], (4, 77)))
        return (x, ctx_768, mask_BxS2_bk0)
    x, ctx_768, mask_BxS2_bk0 = _rec_inputs()

    def _L0_xattn_setup():
        import jax, jax.numpy as jnp
        import numpy as np
        DIM_IN, DIM_LAT, DIM_HEAD = (192, 256, 64)
        INNER = max(DIM_LAT, DIM_IN)
        HEADS = INNER // DIM_HEAD
        SCALE = DIM_HEAD ** (-0.5)
        RMS_EPS = 1e-08
        LN_EPS = 1e-05

        def layernorm(x, g, b):
            mu = jnp.mean(x, axis=-1, keepdims=True)
            var = jnp.mean((x - mu) ** 2, axis=-1, keepdims=True)
            return (x - mu) * jax.lax.rsqrt(var + LN_EPS) * g + b

        def rmsnorm(x, gamma):
            norm = jnp.sqrt(jnp.sum(x * x, axis=-1, keepdims=True)) * x.shape[-1] ** (-0.5)
            return x / jnp.maximum(norm, RMS_EPS) * gamma
        key = jax.random.key(seed)
        ks = jax.random.split(key, 12)
        b, n, m = (4, 1024, 128)
        x = jax.random.normal(ks[0], (b, n, DIM_IN), jnp.float32)
        latents = jax.random.normal(ks[1], (b, m, DIM_LAT), jnp.float32)
        mask = jax.random.randint(ks[2], (b, n), 0, 2).astype(bool)
        s = lambda k, sh, fan: jax.random.normal(k, sh, jnp.float32) * fan ** (-0.5)
        return {'x': x, 'latents': latents, 'mask': mask, 'ln_x_g': jnp.ones((DIM_IN,), jnp.float32), 'ln_x_b': jnp.zeros((DIM_IN,), jnp.float32), 'ln_l_g': jnp.ones((DIM_LAT,), jnp.float32), 'ln_l_b': jnp.zeros((DIM_LAT,), jnp.float32), 'qn_g': jnp.ones((DIM_HEAD,), jnp.float32), 'kn_g': jnp.ones((DIM_HEAD,), jnp.float32), 'Wq': s(ks[3], (INNER, DIM_LAT), DIM_LAT), 'Wkv': s(ks[4], (2 * INNER, DIM_IN), DIM_IN), 'Wlkv': s(ks[5], (2 * INNER, DIM_LAT), DIM_LAT), 'Wo': s(ks[6], (DIM_LAT, INNER), INNER), 'bo': jnp.zeros((DIM_LAT,), jnp.float32)}
    _L0_xattn_all = _L0_xattn_setup()
    _L0_xattn_in = {k: v for k, v in _L0_xattn_all.items() if k in ('ln_x_g', 'ln_x_b', 'ln_l_g', 'ln_l_b', 'qn_g', 'kn_g', 'Wq', 'Wkv', 'Wlkv', 'Wo', 'bo')}
    del _L0_xattn_all

    def _L0_ffn_setup():
        import jax, jax.numpy as jnp
        import numpy as np
        B, S, H, I = (2, 512, 256, 128)
        E, K, G, TG = (64, 8, 8, 4)
        SCALE = 2.5
        CAP = 256
        key = jax.random.key(seed)
        ks = jax.random.split(key, 6)
        hidden_states = jax.random.normal(ks[0], (B, S, H), jnp.float32)
        gate_w = jax.random.normal(ks[1], (E, H), jnp.float32) * 0.02
        gate_bias = jax.random.normal(ks[2], (E,), jnp.float32) * 0.02
        w_gate = jax.random.normal(ks[3], (E, H, I), jnp.float32) * (1.0 / np.sqrt(H))
        w_up = jax.random.normal(ks[4], (E, H, I), jnp.float32) * (1.0 / np.sqrt(H))
        w_down = jax.random.normal(ks[5], (E, I, H), jnp.float32) * (1.0 / np.sqrt(I))
        return {'hidden_states': hidden_states, 'gate_w': gate_w, 'gate_bias': gate_bias, 'w_gate': w_gate, 'w_up': w_up, 'w_down': w_down}
    _L0_ffn_all = _L0_ffn_setup()
    _L0_ffn_in = {k: v for k, v in _L0_ffn_all.items() if k in ('gate_w', 'gate_bias', 'w_gate', 'w_up', 'w_down')}
    del _L0_ffn_all
    return {'x': x, 'ctx_768': ctx_768, 'mask_BxS2_bk0': mask_BxS2_bk0, 'L0_xattn_ln_x_g': _L0_xattn_in['ln_x_g'], 'L0_xattn_ln_x_b': _L0_xattn_in['ln_x_b'], 'L0_xattn_ln_l_g': _L0_xattn_in['ln_l_g'], 'L0_xattn_ln_l_b': _L0_xattn_in['ln_l_b'], 'L0_xattn_qn_g': _L0_xattn_in['qn_g'], 'L0_xattn_kn_g': _L0_xattn_in['kn_g'], 'L0_xattn_Wq': _L0_xattn_in['Wq'], 'L0_xattn_Wkv': _L0_xattn_in['Wkv'], 'L0_xattn_Wlkv': _L0_xattn_in['Wlkv'], 'L0_xattn_Wo': _L0_xattn_in['Wo'], 'L0_xattn_bo': _L0_xattn_in['bo'], 'L0_ffn_gate_w': _L0_ffn_in['gate_w'], 'L0_ffn_gate_bias': _L0_ffn_in['gate_bias'], 'L0_ffn_w_gate': _L0_ffn_in['w_gate'], 'L0_ffn_w_up': _L0_ffn_in['w_up'], 'L0_ffn_w_down': _L0_ffn_in['w_down']}

def reference(x, ctx_768, mask_BxS2_bk0, L0_xattn_ln_x_g, L0_xattn_ln_x_b, L0_xattn_ln_l_g, L0_xattn_ln_l_b, L0_xattn_qn_g, L0_xattn_kn_g, L0_xattn_Wq, L0_xattn_Wkv, L0_xattn_Wlkv, L0_xattn_Wo, L0_xattn_bo, L0_ffn_gate_w, L0_ffn_gate_bias, L0_ffn_w_gate, L0_ffn_w_up, L0_ffn_w_down):
    import jax
    import jax.numpy as jnp

    def _L0_xattn_ref(x, latents, mask, ln_x_g, ln_x_b, ln_l_g, ln_l_b, qn_g, kn_g, Wq, Wkv, Wlkv, Wo, bo):
        import jax, jax.numpy as jnp
        import numpy as np
        DIM_IN, DIM_LAT, DIM_HEAD = (192, 256, 64)
        INNER = max(DIM_LAT, DIM_IN)
        HEADS = INNER // DIM_HEAD
        SCALE = DIM_HEAD ** (-0.5)
        RMS_EPS = 1e-08
        LN_EPS = 1e-05

        def layernorm(x, g, b):
            mu = jnp.mean(x, axis=-1, keepdims=True)
            var = jnp.mean((x - mu) ** 2, axis=-1, keepdims=True)
            return (x - mu) * jax.lax.rsqrt(var + LN_EPS) * g + b

        def rmsnorm(x, gamma):
            norm = jnp.sqrt(jnp.sum(x * x, axis=-1, keepdims=True)) * x.shape[-1] ** (-0.5)
            return x / jnp.maximum(norm, RMS_EPS) * gamma
        b, n, _ = x.shape
        m = latents.shape[1]
        xn = layernorm(x, ln_x_g, ln_x_b)
        ln = layernorm(latents, ln_l_g, ln_l_b)
        q = ln @ Wq.T
        kv = jnp.concatenate([xn @ Wkv.T, ln @ Wlkv.T], axis=1)
        k, v = (kv[..., :INNER], kv[..., INNER:])
        split_heads = lambda t: t.reshape(t.shape[0], t.shape[1], HEADS, DIM_HEAD).transpose(0, 2, 1, 3)
        q, k, v = (split_heads(q), split_heads(k), split_heads(v))
        qn = rmsnorm(q, qn_g) * SCALE
        kn = rmsnorm(k, kn_g)
        attn = jnp.einsum('bhid,bhjd->bhij', qn, kn)
        full_mask = jnp.pad(mask, ((0, 0), (0, m)), constant_values=True)
        attn = jnp.where(full_mask[:, None, None, :], attn, -jnp.finfo(attn.dtype).max)
        attn = jax.nn.softmax(attn, axis=-1)
        out = jnp.einsum('bhij,bhjd->bhid', attn, v)
        out = out.transpose(0, 2, 1, 3).reshape(b, m, INNER)
        return out @ Wo.T + bo

    def _L0_ffn_ref(hidden_states, gate_w, gate_bias, w_gate, w_up, w_down):
        import jax, jax.numpy as jnp
        import numpy as np
        B, S, H, I = (2, 512, 256, 128)
        E, K, G, TG = (64, 8, 8, 4)
        SCALE = 2.5
        CAP = 256
        b, s, h = hidden_states.shape
        x = hidden_states.reshape(-1, h)
        n = x.shape[0]
        logits = x.astype(jnp.float32) @ gate_w.astype(jnp.float32).T
        scores = jax.nn.sigmoid(logits)
        sfc = scores + gate_bias[None, :]
        group_scores = jax.lax.top_k(sfc.reshape(n, G, E // G), 2)[0].sum(-1)
        gidx = jax.lax.top_k(group_scores, TG)[1]
        gmask = jnp.zeros((n, G), bool).at[jnp.arange(n)[:, None], gidx].set(True)
        smask = jnp.repeat(gmask, E // G, axis=1)
        tmp = jnp.where(smask, sfc, -jnp.inf)
        topk_idx = jax.lax.top_k(tmp, K)[1]
        topk_w = jnp.take_along_axis(scores, topk_idx, axis=1)
        topk_w = topk_w / (topk_w.sum(-1, keepdims=True) + 1e-20)
        topk_w = topk_w * SCALE
        e = topk_idx.reshape(-1)
        token = jnp.repeat(jnp.arange(n), K)
        oh = jax.nn.one_hot(e, E, dtype=jnp.int32)
        pos = jnp.take_along_axis(jnp.cumsum(oh, 0) - 1, e[:, None], 1)[:, 0]
        valid = pos < CAP
        pos_c = jnp.where(valid, pos, CAP)
        buf = jnp.zeros((E, CAP + 1, h), x.dtype).at[e, pos_c].set(x[token])[:, :CAP]
        g = jnp.einsum('ech,ehi->eci', buf, w_gate)
        u = jnp.einsum('ech,ehi->eci', buf, w_up)
        y = jnp.einsum('eci,eih->ech', jax.nn.silu(g) * u, w_down)
        y_slots = y[e, jnp.minimum(pos, CAP - 1)]
        w_slot = topk_w.reshape(-1) * valid.astype(topk_w.dtype)
        out = jnp.zeros((n, h), jnp.float32).at[token].add(y_slots * w_slot[:, None])
        return out.reshape(b, s, h)
    x = x + _L0_xattn_ref(ctx_768, _layernorm(x, axis=-1), mask_BxS2_bk0, L0_xattn_ln_x_g, L0_xattn_ln_x_b, L0_xattn_ln_l_g, L0_xattn_ln_l_b, L0_xattn_qn_g, L0_xattn_kn_g, L0_xattn_Wq, L0_xattn_Wkv, L0_xattn_Wlkv, L0_xattn_Wo, L0_xattn_bo)
    x = x + _L0_ffn_ref(_layernorm(x, axis=-1), L0_ffn_gate_w, L0_ffn_gate_bias, L0_ffn_w_gate, L0_ffn_w_up, L0_ffn_w_down)
    return x

_drawn_inputs = setup_inputs


def setup_inputs(seed=0):
    import zlib

    import numpy as np

    out = dict(_drawn_inputs(seed))
    spreads = {'L0_xattn_ln_x_g': (1.0, 0.6),
     'L0_xattn_ln_x_b': (0.0, 0.301),
     'L0_xattn_ln_l_g': (1.0, 0.2),
     'L0_xattn_ln_l_b': (0.0, 0.1),
     'L0_xattn_qn_g': (1.0, 0.2),
     'L0_xattn_kn_g': (1.0, 0.2),
     'L0_xattn_bo': (0.0, 0.1)}
    factors = {}
    for name, (base, spread) in spreads.items():
        noise = np.random.default_rng([zlib.crc32(name.encode()), seed]).standard_normal(out[name].shape)
        drawn = base * np.exp(spread * noise) if base else spread * noise
        out[name] = jnp.asarray(drawn.astype(out[name].dtype))
    for name, factor in factors.items():
        out[name] = (out[name] * factor).astype(out[name].dtype)
    return out
```

```python
from contextlib import ExitStack

import numpy as np

import concourse.bass as bass
from concourse import mybir

F32 = mybir.dt.float32
F32R = mybir.dt.float32r
BF16 = mybir.dt.bfloat16
U32 = mybir.dt.uint32
I32 = mybir.dt.int32
U8 = mybir.dt.uint8
ALU = mybir.AluOpType
ACT = mybir.ActivationFunctionType
AX = mybir.AxisListType

P = 128
B, S, D = 4, 1024, 256
NCTX, DCTX = 77, 192
H, DH = 4, 64
TPB = S // P
QT = 4
QW = QT * P
NKT = TPB + 1
NCP = NCTX + 1
NK = S + NCP
STEPS = [(0, 1), (2, 3), (4, 5), (6, 7), (8,)]
VW = DH + 1
E, TOPK, G, TG, CAP = 64, 8, 8, 4, 256
EG = E // G
I = 128
ROUTE_SCALE = 2.5
NTOK = B * S
DUMP = CAP
ROW = D + 1 + E
LN_EPS = 1e-5
RMS_EPS = 1e-8
BIG = 1e30
MAGIC = 0x5F3759DF
SIDE = 3
EB = 16
RING = 4


class Plan:

    def __init__(self, first, second, keys, route0, route1):
        self.tasks = []
        self.units = []
        self.steps = []
        self.blocks = []
        self.first, self.second, self.keys = first, second, keys
        self.route0, self.route1 = route0, route1
        if keys:
            self.add("stats")
        side1 = []
        if keys:
            side1 += self.key_tasks()
        if first:
            self.maxes(1, 0)
            n = len(side1)
            r = self.route_tasks(0) if route0 else []
            cuts = [0, n * 3 // 8, n * 6 // 8, n, n]
            for h in range(H):
                side = side1[cuts[h]:cuts[h + 1]]
                mine = r[len(r) * h // H:len(r) * (h + 1) // H]
                nxt = self.max_tasks(1, h + 1) if h + 1 < H else (self.max_tasks(0, 0) if second else [])
                self.block(1, h, self.mix(side, mine) + nxt if h + 1 == H else self.mix(self.mix(side, mine), nxt))
        else:
            for t in side1:
                self.add(*t)
            if second:
                self.maxes(0, 0)
        r = self.route_tasks(1) if route1 else []
        if second:
            for h in range(H):
                mine = r[len(r) * h // H:len(r) * (h + 1) // H]
                nxt = self.max_tasks(0, h + 1) if h + 1 < H else []
                self.block(0, h, self.mix(mine, nxt))
        else:
            for t in r:
                self.add(*t)

    def mix(self, a, b):
        out, i, j = [], 0, 0
        while i < len(a) or j < len(b):
            if j >= len(b) or (i < len(a) and i * len(b) <= j * len(a)):
                out.append(a[i])
                i += 1
            else:
                out.append(b[j])
                j += 1
        return out

    def add(self, kind, *args):
        if kind in ("ln_turn", "qk", "v", "q_turn", "k_turn", "max", "max_ctx", "qb", "proj", "hn_turn", "logits",
                    "pos"):
            self.units.append((kind, *args))
        if kind == "scores":
            self.steps.append(args)
            if args[2] == 0:
                self.blocks.append(args[:2])
        self.tasks.append((kind, *args))

    def key_tasks(self):
        out = [("z", 0), ("ln_turn", 0)]
        for j in range(NKT):
            if j + 1 < NKT:
                out.append(("z", j + 1))
            out += [("qk", j), ("v", j)]
            if j + 1 < NKT:
                out.append(("ln_turn", j + 1))
            if j >= 2 and j % 2 == 0:
                out += self.turn_tasks(j // 2 - 1)
            if j % 2 == 1 or j == NKT - 1:
                out.append(("split", j // 2))
        out += self.turn_tasks((NKT - 1) // 2)
        out.append(("kv_done",))
        return out

    def turn_tasks(self, pair):
        out = []
        for j in range(2 * pair, min(2 * pair + 2, NKT)):
            if j < TPB:
                out.append(("q_turn", j))
            out.append(("k_turn", j))
        return out

    def max_tasks(self, x, h):
        out = [("max", x, h, t, half) for t in range(QT) for half in range(2)]
        return out + [("max_ctx", x, h), ("neg", x, h), ("qb", x, h)]

    def maxes(self, x, h):
        for t in self.max_tasks(x, h):
            self.add(*t)

    def route_tasks(self, x):
        out = [("proj", x, t, h) for t in range(QT) for h in range(H)]
        out.append(("hn_scale", x))
        for t in range(QT):
            out += [("hn", x, t), ("hn_turn", x, t), ("logits", x, t)]
        return out + [("top", x), ("pos", x), ("slots", x)]

    def block(self, x, h, side):
        side = list(side)
        n = len(STEPS)
        self.add("scores", x, h, 0)
        done = 0
        slots = 2 * n - 1
        at = 0
        for s in range(n):
            for kind in ("scores", "values"):
                if kind == "scores":
                    if s + 1 >= n:
                        continue
                    self.add("scores", x, h, s + 1)
                else:
                    self.add("values", x, h, s)
                at += 1
                upto = len(side) * at // slots
                for t in side[done:upto]:
                    self.add(*t)
                done = upto
        self.add("o_copy", x, h)


def build(nc, a, out):
    with ExitStack() as ctx:
        def sem(name):
            return ctx.enter_context(nc.semaphore(name))

        slot_rows = nc.dram_tensor("slot_rows", [E * CAP, ROW], F32).ap()

        first_sem = sem("loaded")
        s = {"loaded": first_sem}
        names = ["const_made", "filled", "vec_step", "pool_step", "x_loaded", "xres_loaded", "xres_based", "ctx_loaded",
                 "mask_loaded", "mask_made", "stats_done", "z_made", "unit_full", "emptied_act", "emptied_vec",
                 "summed", "normed", "hi_made", "lo_made", "head_copied0", "head_copied1", "head_copied2", "head_copied3", "neg_made", "scores_full", "probs_made",
                 "values_done", "o_copied", "x2_stored", "hn_scaled", "hn_made", "sel_made", "slots_made",
                 "rows_made",
                 "w_loaded0", "w_loaded1", "w_loaded2", "w_loaded3", "x_in0", "x_in1", "x_in2", "x_in3",
                 "rows_turned", "turned_copied", "gate_up", "silu_made", "h_made", "y_full", "y_made", "add_done"]
        for n in names:
            s[n] = sem(n)
        last = s[names[-1]]
        scattered, added = sem("scattered"), sem("added")

        def fresh():
            nc.all_engine_barrier(sems_to_clear=range(first_sem.num, last.num + 1))

        with ExitStack() as p1:
            phase1(nc, a, out, slot_rows, s, scattered, fresh, p1)
        with ExitStack() as p2:
            phase2(nc, a, out, slot_rows, s, added, fresh, p2)


def rsqrt(v, link, x, shifted, y, t):
    link(v.tensor_scalar(shifted, x.bitcast(U32), 1, None, ALU.logical_shift_right))
    link(v.tensor_scalar(y.bitcast(I32), shifted, -1.0, float(MAGIC), ALU.mult, ALU.add))
    for _ in range(3):
        link(v.scalar_tensor_tensor(t, y, -0.5, y, ALU.mult, ALU.mult))
        link(v.tensor_tensor(t, t, x, ALU.mult))
        link(v.scalar_tensor_tensor(y, t, 1.5, y, ALU.add, ALU.mult))


def phase1(nc, a, out, slot_rows, s, scattered, fresh, ctx):
    def sb(name, shape, dt=F32):
        return ctx.enter_context(nc.sbuf_tensor(name, shape, dt))

    wqkv = sb("wqkv_s", [P, 2, 3 * D])
    wkvx = sb("wkvx_s", [DCTX // 2, 2, 2 * D])
    wo = sb("wo_s", [VW, H, D + 1])
    gate = sb("gate_s", [P, 2, E])
    gate_bias = sb("gate_bias_s", [P, E])
    bo = sb("bo_s", [P, D])
    ln_g, ln_b = sb("ln_g_s", [P, 2]), sb("ln_b_s", [P, 2])
    lx_g, lx_b = sb("lx_g_s", [DCTX // 2, 2]), sb("lx_b_s", [DCTX // 2, 2])
    qk_g = sb("qk_g_s", [P, 2 * DH])
    gam = sb("gam", [P, 2 * H, DH])
    ident = sb("ident", [P, P])
    tri = sb("tri", [P, P], BF16)
    ones = sb("ones_b", [P, P], BF16)
    one_row = sb("one_row", [1, P], F32R)
    slot_base = sb("slot_base", [P, E])
    group_no = sb("group_no", [P, G])
    token_id = sb("token_id", [P, TPB])

    K = sb("K", [P, H, NK], F32R)
    Kb = sb("Kb", [VW, H, NK], F32R)
    Kn = sb("Kn", [P, H, NK], F32R)
    V = sb("V", [P, H, NKT, VW])
    Vn = sb("Vn", [P, H, NKT, VW])
    Q = [sb("Q0", [P, H, QW], F32R), sb("Q1", [P, H, QW], F32R)]
    Q1n = sb("Q1n", [P, H, QW], F32R)
    QL = [sb("QL0", [P, H, QT, VW]), sb("QL1", [P, H, QT, VW])]
    QL1n = sb("QL1n", [P, H, QT, VW])
    oT = [sb("oT0", [VW, H, QW]), sb("oT1", [VW, H, QW])]
    qbT = [sb("qbT0", [VW, QW], F32R), sb("qbT1", [VW, QW], F32R)]
    probs = sb("probs", [P, 2, 2, QW])

    xin = sb("xin", [P, TPB, D])
    xctx = sb("xctx", [NCTX, DCTX])
    xres = sb("xres", [P, QT, D])
    mask_u8 = sb("mask_u8", [NCTX, 2], U8)
    mask_bias = sb("mask_bias", [NCTX, 2])
    mask_row8 = sb("mask_row8", [1, 2, NCTX], U8)
    mask_row = sb("mask_row", [1, 2, QT, NCP], F32R)
    bn = sb("bn", [P, NKT, 6])
    mv = sb("mv", [P, NKT, 2])
    st_v, st_y, st_t, st_r = (sb(n, [P, NKT]) for n in ("st_v", "st_y", "st_t", "st_r"))
    st_i = sb("st_i", [P, NKT], U32)
    ln_s, ln_nb = sb("ln_s", [P, NKT]), sb("ln_nb", [P, NKT])
    z = sb("z", [P, 2, D])
    lnT = sb("lnT", [P, 2, 2, P])
    raw = sb("raw", [P, 4, 2 * H, DH])
    sq = sb("sq", [P, 2, 2 * H, DH])
    NR = 2 * 2 * H
    rs_v, rs_y, rs_t = (sb(n, [P, 2, NR]) for n in ("rs_v", "rs_y", "rs_t"))
    rs_i = sb("rs_i", [P, 2, NR], U32)
    st = sb("st", [P, 2, 2 * H, 2 * DH])
    mp = sb("mp", [P, QT, 3])
    mx = sb("mx", [P, QT])
    bnC, mvC = sb("bnC", [P, QT, 6]), sb("mvC", [P, QT, 2])
    c_v, c_y, c_t, c_nb = (sb(n, [P, QT]) for n in ("c_v", "c_y", "c_t", "c_nb"))
    c_i = sb("c_i", [P, QT], U32)
    rden = sb("rden", [P, 1])
    rows = [sb("rows0", [P, QT, ROW]), sb("rows1", [P, QT, ROW])]
    hnT = sb("hnT", [P, 2, 2, P])
    th = sb("th", [P, QT, E])
    sc, sfc, rep, sel, wsel, key = (sb(n, [P, QT, E]) for n in ("sc", "sfc", "rep", "sel", "wsel", "key"))
    g8 = sb("g8", [P, QT, G, 8])
    gs, gmask, pen = (sb(n, [P, QT, G]) for n in ("gs", "gmask", "pen"))
    gm8, v8, k8, adj = (sb(n, [P, QT, 8]) for n in ("gm8", "v8", "k8", "adj"))
    gi = sb("gi", [P, QT, 8], U32)
    gif = sb("gif", [P, QT, 8])
    geq = sb("geq", [P, QT, G, TG])
    selb = sb("selb", [P, QT, E], BF16)
    carry = sb("carry", [P, QT + 1, E], BF16)
    wden = sb("wden", [P, QT])
    slot_idx = [sb("slot_idx0", [P, QT, 8], U32), sb("slot_idx1", [P, QT, 8], U32)]

    ps_s = ctx.enter_context(nc.psum_tensor("ps_s", [P, 2, 2, QW], F32))
    ps_o = ctx.enter_context(nc.psum_tensor("ps_o", [P, QW], F32))
    ps_u = ctx.enter_context(nc.psum_tensor("ps_u", [P, SIDE, 512], F32))

    setup(nc, a, out, slot_rows, s, locals())
    main = locals()
    fresh()
    attend(nc, a, out, slot_rows, s, scattered, main, Plan(False, True, True, False, False), -1)
    fresh()
    with nc.Fori(0, B - 1) as b:
        attend(nc, a, out, slot_rows, s, scattered, main, Plan(True, True, True, True, True), b)
        fresh()
    attend(nc, a, out, slot_rows, s, scattered, main, Plan(True, False, False, True, True), B - 1)
    fresh()


def setup(nc, a, out, slot_rows, s, m):
    with ExitStack() as ctx:
        empty = m["probs"][:].rearrange("p a b q -> p (a b q)")[:, 0:2 * ROW].rearrange("p (t r) -> p t r", t=2)
        zero = m["xin"][:, 0:2, :]
        ctx.enter_context(nc.allow_non_contiguous_dma(reason="small constants"))
        with nc.Block() as block:
            LOADS = 11

            @block.sync
            def _(sp):
                for dst, src in ((m["wqkv"], a["wqkv"]), (m["wkvx"], a["wkvx"]), (m["gate"], a["gate"]),
                                 (m["ln_g"], a["ln_g"]), (m["ln_b"], a["ln_b"]), (m["lx_g"], a["lx_g"]),
                                 (m["lx_b"], a["lx_b"])):
                    sp.dma_start(dst[:], src).then_inc(s["loaded"], 16)
                sp.dma_start(m["gate_bias"][:], a["gate_bias"].to_broadcast([P, E])).then_inc(s["loaded"], 16)
                sp.dma_start(m["bo"][:], a["bo"].to_broadcast([P, D])).then_inc(s["loaded"], 16)
                sp.dma_start(m["qk_g"][:], a["qk_g"].to_broadcast([P, 2 * DH])).then_inc(s["loaded"], 16)
                sp.wait_ge(s["const_made"], 2)
                sp.dma_start(m["wo"][0:DH, :, 0:D], a["wo"]).then_inc(s["loaded"], 16)
                sp.wait_ge(s["const_made"], 4)
                sp.dma_start(slot_rows.rearrange("(e p t) r -> p e (t r)", p=P, t=2),
                             empty.rearrange("p t r -> p (t r)").unsqueeze(1).to_broadcast([P, E, 2 * ROW])
                             ).then_inc(s["filled"], 16)
                sp.dma_start(out[NTOK:NTOK + DUMP, :].rearrange("(p t) d -> p t d", t=2), zero
                             ).then_inc(s["filled"], 16)
                sp.wait_ge(s["loaded"], 16 * LOADS)
                sp.wait_ge(s["filled"], 32)

            @block.gpsimd
            def _(pool):
                n = 0

                def link(ins):
                    nonlocal n
                    n += 1
                    ins.then_inc(s["pool_step"], 1)
                    pool.wait_ge(s["pool_step"], n)

                link(pool.memset(m["wo"][:], 0.0))
                pool.memset(m["wo"][DH:VW, :, D:D + 1], 1.0).then_inc(s["const_made"], 2)
                pool.wait_ge(s["const_made"], 2)
                link(pool.memset(empty, 0.0))
                link(pool.iota(empty[:, :, D:D + 1], pattern=[[P, 2], [0, 1]], base=NTOK, channel_multiplier=1,
                               allow_small_or_imprecise_dtypes=True))
                pool.memset(zero, 0.0).then_inc(s["const_made"], 2)
                pool.wait_ge(s["const_made"], 4)
                link(pool.memset(m["ident"][:], 0.0))
                link(pool.affine_select(out=m["ident"][:], in_=m["ident"][:], compare_op=ALU.not_equal, fill=1.0,
                                        base=0, pattern=[[-1, P]], channel_multiplier=1))
                link(pool.memset(m["ones"][:], 1.0))
                link(pool.affine_select(out=m["tri"][:], in_=m["ones"][:], compare_op=ALU.is_gt, fill=0.0,
                                        base=0, pattern=[[1, P]], channel_multiplier=-1))
                link(pool.iota(m["slot_base"][:], pattern=[[CAP, E]], base=1, channel_multiplier=0,
                               allow_small_or_imprecise_dtypes=True))
                link(pool.iota(m["group_no"][:], pattern=[[1, G]], base=0, channel_multiplier=0,
                               allow_small_or_imprecise_dtypes=True))
                link(pool.iota(m["token_id"][:], pattern=[[P, TPB]], base=0, channel_multiplier=1,
                               allow_small_or_imprecise_dtypes=True))

            @block.vector
            def _(v):
                v.memset(m["one_row"][:].bitcast(F32), 1.0)
                v.memset(m["Kb"][DH:VW, :, :].bitcast(F32), 1.0)
                v.memset(m["V"][:], 1.0)
                v.memset(m["Vn"][:], 1.0)
                v.memset(m["mv"][:], 1.0)
                v.memset(m["raw"][:], 1.0)
                v.memset(m["sq"][:], 1.0)
                v.memset(m["carry"][:], 0.0)
                v.memset(m["QL1n"][:], 0.0)
                v.memset(m["Kn"][:].bitcast(F32), 0.0)
                v.memset(m["K"][:, :, NK - 1:NK].bitcast(F32), 0.0)
                v.memset(m["mask_row"][:].bitcast(F32), -BIG)
                v.wait_ge(s["loaded"], 16 * LOADS)
                for h in range(H):
                    v.tensor_scalar(m["gam"][:, h, :], m["qk_g"][:, 0:DH], DH ** -0.5, None, ALU.mult)
                    v.tensor_copy(m["gam"][:, H + h, :], m["qk_g"][:, DH:2 * DH])


def attend(nc, a, out, slot_rows, s, scattered, m, plan, b):
    K, Kb, Kn, V, Vn, Q, Q1n, QL, QL1n = (m[n] for n in ("K", "Kb", "Kn", "V", "Vn", "Q", "Q1n", "QL", "QL1n"))
    ps_s, ps_o, ps_u, probs, oT, qbT = (m[n] for n in ("ps_s", "ps_o", "ps_u", "probs", "oT", "qbT"))
    ident, lnT, z, st, raw, sq = (m[n] for n in ("ident", "lnT", "z", "st", "raw", "sq"))
    xin, xres, rows, hnT = (m[n] for n in ("xin", "xres", "rows", "hnT"))

    def unit_owner(u):
        return "vec" if u[0] in ("max", "max_ctx", "proj", "pos") else "act"

    units, steps, blocks = plan.units, plan.steps, plan.blocks
    unit_no = {u: i for i, u in enumerate(units)}
    step_no = {u: i for i, u in enumerate(steps)}
    block_no = {u: i for i, u in enumerate(blocks)}
    max_no = {u: i for i, u in enumerate([t[1:] for t in plan.tasks if t[0] == "qb"])}
    proj_units = [u for u in units if u[0] == "proj"]
    logit_units = [u for u in units if u[0] == "logits"]

    def bank(u):
        return ps_u[:, unit_no[u] % SIDE, :]

    def wait_full(eng, u):
        eng.wait_ge(s["unit_full"], unit_no[u] + 1)

    def count_empty(u):
        return sum(unit_owner(w) == unit_owner(u) for w in units[:unit_no[u] + 1])

    def wait_empty(eng, u):
        eng.wait_ge(s["emptied_" + unit_owner(u)], count_empty(u))

    def rows_of(j):
        return P if j < TPB else NCTX

    def q_place(j):
        return (Q[0], QL[0], j) if j < QT else (Q1n, QL1n, j - QT)

    x_dram = a["x"].rearrange("(b t p) d -> b p t d", b=B, p=P)
    out_dram = out[0:NTOK, :].rearrange("(b t p) d -> b p t d", b=B, p=P)

    def of_batch(ap, n):
        return ap[n] if isinstance(n, int) else ap[bass.ds(n, 1)][0]

    with nc.Block() as block:
        @block.sync
        def _(sp):
            if plan.keys:
                sp.dma_start(xin[:], of_batch(x_dram, b + 1)).then_inc(s["x_loaded"], 16)
                sp.dma_start(m["xctx"][:], of_batch(a["ctx"], b + 1)).then_inc(s["ctx_loaded"], 16)
            n_mask = 0
            for use, i, n in ((plan.first, 0, b), (plan.second, 1, b + 1)):
                if use:
                    n_mask += 2
                    sp.dma_start(m["mask_u8"][:, i:i + 1], of_batch(a["mask_col"], n)).then_inc(s["mask_loaded"], 16)
                    sp.dma_start(m["mask_row8"][:, i, :], of_batch(a["mask_row"], n)).then_inc(s["mask_loaded"], 16)

            def load_residual(x):
                sp.dma_start(xres[:], of_batch(x_dram, b)[:, QT * x:QT * x + QT, :]).then_inc(s["xres_loaded"], 16)

            if plan.route0:
                load_residual(0)

            def copy_head(h):
                for dst, src in ((K[:, h, :], Kn[:, h, :]), (Kb[0:DH, h, :], Kn[0:DH, h, :]),
                                 (V[:, h, :, :], Vn[:, h, :, :]), (Q[1][:, h, :], Q1n[:, h, :]),
                                 (QL[1][:, h, :, :], QL1n[:, h, :, :])):
                    sp.dma_start(dst.bitcast(F32), src.bitcast(F32)).then_inc(s[f"head_copied{h}"], 16)

            def keys_made():
                wait_empty(sp, ("k_turn", NKT - 1))
                sp.wait_ge(s["lo_made"], (NKT + 1) // 2)

            stored = 0
            for t in plan.tasks:
                if t[0] == "kv_done":
                    keys_made()
                    if not plan.first:
                        for h in range(H):
                            copy_head(h)
                if t[0] == "o_copy" and t[1] == 1 and plan.second:
                    if t[2] == 0:
                        keys_made()
                    sp.wait_ge(s["values_done"], len(STEPS) * (block_no[t[1:]] + 1))
                    copy_head(t[2])
                if t[0] == "hn_scale":
                    stored += 1
                    x = t[1]
                    wait_empty(sp, ("proj", x, QT - 1, H - 1))
                    sp.dma_start(of_batch(out_dram, b)[:, QT * x:QT * x + QT, :], xres[:]).then_inc(s["x2_stored"], 16)
                    if x == 0:
                        sp.wait_ge(s["x2_stored"], 16)
                        sp.wait_ge(s["hn_made"], QT)
                        load_residual(1)
            if stored:
                sp.wait_ge(s["x2_stored"], 16 * stored)

        @block.gpsimd
        def _(pool):
            n = 0
            def add_bias(x):
                pool.wait_ge(s["xres_loaded"], 16 * (x + 1))
                for j in range(QT):
                    pool.tensor_tensor(xres[:, j, :], xres[:, j, :], m["bo"][:], ALU.add).then_inc(s["xres_based"], 1)
                    pool.wait_ge(s["xres_based"], QT * x + j + 1)

            if plan.route0:
                add_bias(0)
            for t in plan.tasks:
                if t[0] == "slots":
                    x = t[1]
                    n += 1
                    pool.wait_ge(s["slots_made"], n)
                    pool.wait_ge(s["rows_made"], n)
                    pool.wait_ge(s["hn_made"], QT * n)
                    for q in range(QT):
                        for k in range(TOPK):
                            pool.indirect_dma_start(
                                out=slot_rows, out_offset=bass.IndirectOffsetOnAxis(
                                    ap=m["slot_idx"][x][:, q, k:k + 1], axis=0),
                                in_=rows[x][:, q, :], in_offset=None, bounds_check=E * CAP - 1,
                                oob_is_err=False).then_inc(scattered, 16)
                if t == ("hn_turn", 0, QT - 1):
                    add_bias(1)

        @block.tensor
        def _(pe):
            def free_bank(u):
                if unit_no[u] >= SIDE:
                    wait_empty(pe, units[unit_no[u] - SIDE])

            for t in plan.tasks:
                kind = t[0]
                if t in unit_no:
                    free_bank(t)
                if kind == "ln_turn":
                    j = t[1]
                    w, rj = (P, rows_of(j)) if j < TPB else (DCTX // 2, NCTX)
                    pe.wait_ge(s["z_made"], j + 1)
                    for c in range(2):
                        i = pe.transpose(bank(t)[0:w, c * P:c * P + rj], z[0:rj, j % 2, c * w:(c + 1) * w],
                                         ident[0:rj, 0:rj])
                    i.then_inc(s["unit_full"], 1)
                elif kind in ("qk", "v"):
                    j = t[1]
                    rj = rows_of(j)
                    wait_empty(pe, ("ln_turn", j))
                    w = P if j < TPB else DCTX // 2
                    if kind == "qk":
                        dst = bank(t)[0:rj, 0:2 * D] if j < TPB else bank(t)[0:rj, D:2 * D]
                    else:
                        dst = bank(t)[0:rj, 0:D]
                    for c in range(2):
                        if j < TPB:
                            rhs = m["wqkv"][:, c, 0:2 * D] if kind == "qk" else m["wqkv"][:, c, 2 * D:3 * D]
                        else:
                            rhs = m["wkvx"][:, c, 0:D] if kind == "qk" else m["wkvx"][:, c, D:2 * D]
                        i = pe.matmul(dst, lnT[0:w, j % 2, c, 0:rj], rhs, start=(c == 0), stop=(c == 1))
                    i.then_inc(s["unit_full"], 1)
                elif kind in ("q_turn", "k_turn"):
                    j = t[1]
                    rj = rows_of(j)
                    pair = j // 2
                    pe.wait_ge(s["hi_made"], pair + 1)
                    pe.wait_ge(s["lo_made"], pair + 1)
                    h0 = 0 if kind == "q_turn" else H
                    for h in range(H):
                        i = pe.transpose(bank(t)[:, h * P:h * P + rj], st[0:rj, j % 2, h0 + h, :], ident[0:rj, 0:rj])
                    i.then_inc(s["unit_full"], 1)
                elif kind in ("max", "max_ctx", "qb"):
                    x, h = t[1:3]
                    keys = K if x == 1 else Kn
                    if x == 0:
                        wait_empty(pe, ("k_turn", NKT - 1))
                    if kind == "max":
                        tile, half = t[3:5]
                        i = pe.matmul(bank(t)[:, :], Q[x][:, h, tile * P:(tile + 1) * P],
                                      keys[:, h, half * 512:(half + 1) * 512], start=True, stop=True)
                    elif kind == "max_ctx":
                        pe.wait_ge(s["mask_made"], 4 if plan.first and plan.second else 2)
                        pe.matmul(bank(t)[:, 0:QT * NCP], m["one_row"][:],
                                  m["mask_row"][:, 1 - x, :, :].rearrange("o q k -> o (q k)"), start=True, stop=False,
                                  skip_group_check=True)
                        for tile in range(QT):
                            i = pe.matmul(bank(t)[:, tile * NCP:(tile + 1) * NCP],
                                          Q[x][:, h, tile * P:(tile + 1) * P], keys[:, h, S:NK],
                                          start=False, stop=(tile == QT - 1), skip_group_check=True)
                    else:
                        pe.wait_ge(s["neg_made"], max_no[(x, h)] + 1)
                        for tile in range(QT):
                            i = pe.transpose(bank(t)[0:VW, tile * P:(tile + 1) * P], QL[x][:, h, tile, :], ident[:])
                    i.then_inc(s["unit_full"], 1)
                elif kind == "scores":
                    x, h, st_ = t[1:]
                    n = step_no[t[1:]]
                    wait_empty(pe, ("qb", x, h))
                    if x == 0:
                        pe.wait_ge(s[f"head_copied{h}"], 16 * 5)
                    if n >= 2:
                        pe.wait_ge(s["probs_made"], n - 1)
                    for i_kt, kt in enumerate(STEPS[st_]):
                        rk = rows_of(kt)
                        dst = ps_s[0:rk, n % 2, i_kt, :]
                        pe.matmul(dst, K[:, h, kt * P:kt * P + rk], Q[x][:, h, :], start=True, stop=False)
                        i = pe.matmul(dst, Kb[:, h, kt * P:kt * P + rk], qbT[max_no[(x, h)] % 2][:],
                                      start=False, stop=True)
                    i.then_inc(s["scores_full"], 1)
                elif kind == "values":
                    x, h, st_ = t[1:]
                    n = step_no[t[1:]]
                    pe.wait_ge(s["probs_made"], n + 1)
                    if st_ == 0 and block_no[(x, h)] >= 1:
                        pe.wait_ge(s["o_copied"], block_no[(x, h)])
                    for i_kt, kt in enumerate(STEPS[st_]):
                        rk = rows_of(kt)
                        i = pe.matmul(ps_o[0:VW, :], V[0:rk, h, kt, :], probs[0:rk, n % 2, i_kt, :],
                                      start=(kt == 0), stop=(kt == NKT - 1))
                    i.then_inc(s["values_done"], 1)
                elif kind == "proj":
                    x, tile, h = t[1:]
                    if x == 1:
                        pe.wait_ge(s["o_copied"], H)
                    i = pe.matmul(bank(t)[:, 0:D + 1], oT[x][:, h, tile * P:(tile + 1) * P], m["wo"][:, h, :],
                                  start=True, stop=True)
                    i.then_inc(s["unit_full"], 1)
                elif kind == "hn_turn":
                    x, tile = t[1:]
                    n = [u for u in units if u[0] == "hn_turn"].index(t)
                    pe.wait_ge(s["hn_made"], n + 1)
                    for c in range(2):
                        i = pe.transpose(bank(t)[:, c * P:(c + 1) * P], rows[x][:, tile, c * P:(c + 1) * P], ident[:])
                    i.then_inc(s["unit_full"], 1)
                elif kind == "logits":
                    n = logit_units.index(t)
                    wait_empty(pe, ("hn_turn",) + t[1:])
                    for c in range(2):
                        i = pe.matmul(bank(t)[:, 0:E], hnT[:, n % 2, c, :], m["gate"][:, c, :],
                                      start=(c == 0), stop=(c == 1))
                    i.then_inc(s["unit_full"], 1)
                elif kind == "pos":
                    n = [u for u in units if u[0] == "pos"].index(t)
                    pe.wait_ge(s["sel_made"], n + 1)
                    for tile in range(QT):
                        dst = bank(t)[:, tile * E:(tile + 1) * E]
                        pe.matmul(dst, m["tri"][:], m["selb"][:, tile, :], start=(tile == 0), stop=False,
                                  skip_group_check=True)
                        i = pe.matmul(dst, m["ones"][:], m["carry"][:, tile, :], start=False, stop=(tile == QT - 1),
                                      skip_group_check=True)
                    i.then_inc(s["unit_full"], 1)

        @block.scalar
        def _(act):
            for t in plan.tasks:
                kind = t[0]
                if kind in ("ln_turn", "qk", "v", "q_turn", "k_turn", "qb", "hn_turn", "logits"):
                    wait_full(act, t)
                if kind == "z":
                    j = t[1]
                    rj, w = rows_of(j), (D if j < TPB else DCTX)
                    act.wait_ge(s["stats_done"], 1)
                    if j >= 2:
                        wait_full(act, ("ln_turn", j - 2))
                    src = xin[:, j, :] if j < TPB else m["xctx"][:]
                    act.activation(z[0:rj, j % 2, 0:w], src, ACT.Identity, scale=m["ln_s"][0:rj, j:j + 1],
                                   bias=m["ln_nb"][0:rj, j:j + 1]).then_inc(s["z_made"], 1)
                elif kind == "ln_turn":
                    j = t[1]
                    rj = rows_of(j)
                    w = P if j < TPB else DCTX // 2
                    g_, b_ = (m["ln_g"], m["ln_b"]) if j < TPB else (m["lx_g"], m["lx_b"])
                    if j >= 2:
                        wait_full(act, ("v", j - 2))
                    for c in range(2):
                        i = act.activation(lnT[0:w, j % 2, c, 0:rj], bank(t)[0:w, c * P:c * P + rj], ACT.Identity,
                                           scale=g_[:, c:c + 1], bias=b_[:, c:c + 1])
                    i.then_inc(s["emptied_act"], 1)
                elif kind == "qk":
                    j = t[1]
                    rj = rows_of(j)
                    h0 = 0 if j < TPB else H
                    if j >= 4:
                        act.wait_ge(s["lo_made"], (j - 4) // 2 + 1)
                    if j >= 2:
                        act.wait_ge(s["summed"], j - 1)
                    src = bank(t)[0:rj, h0 * DH:2 * D]
                    act.activation(raw[0:rj, j % 4, h0:2 * H, :], src, ACT.Copy)
                    act.activation(sq[0:rj, j % 2, h0:2 * H, :], src, ACT.Square).then_inc(s["emptied_act"], 1)
                elif kind == "v":
                    j = t[1]
                    rj = rows_of(j)
                    act.activation(Vn[0:rj, :, j, 0:DH], bank(t)[0:rj, 0:D].rearrange("p (h d) -> p h d", h=H),
                                   ACT.Copy).then_inc(s["emptied_act"], 1)
                elif kind == "split":
                    pair = t[1]
                    n = min(2, NKT - 2 * pair)
                    act.wait_ge(s["normed"], pair + 1)
                    if pair >= 1:
                        wait_full(act, ("k_turn", 2 * pair - 1))
                    a0 = 2 * (pair % 2)
                    act.activation(st[:, 0:n, :, 0:DH].bitcast(F32R), raw[:, a0:a0 + n, :, :], ACT.Copy)
                    act.activation(st[:, 0:n, 0:H, DH:2 * DH].bitcast(F32R), raw[:, a0:a0 + n, 0:H, :], ACT.Copy
                                   ).then_inc(s["hi_made"], 1)
                elif kind == "q_turn":
                    j = t[1]
                    dst, _, at = q_place(j)
                    i = act.activation(dst[:, :, at * P:(at + 1) * P], bank(t).rearrange("p (h q) -> p h q", h=H),
                                       ACT.Copy)
                    i.then_inc(s["emptied_act"], 1)
                elif kind == "k_turn":
                    j = t[1]
                    rj = rows_of(j)
                    i = act.activation(Kn[:, :, j * P:j * P + rj],
                                       bank(t).rearrange("p (h q) -> p h q", h=H)[:, :, 0:rj], ACT.Copy)
                    i.then_inc(s["emptied_act"], 1)
                elif kind == "qb":
                    x, h = t[1:]
                    n = max_no[(x, h)]
                    if n >= 2:
                        act.wait_ge(s["scores_full"], step_no[blocks[n - 2] + (len(STEPS) - 1,)] + 1)
                    act.activation(qbT[n % 2][:], bank(t)[0:VW, :], ACT.Copy).then_inc(s["emptied_act"], 1)
                elif kind == "scores":
                    x, h, st_ = t[1:]
                    n = step_no[t[1:]]
                    act.wait_ge(s["scores_full"], n + 1)
                    if n >= 2:
                        act.wait_ge(s["values_done"], n - 1)
                    if len(STEPS[st_]) == 2:
                        act.activation(probs[:, n % 2, :, :], ps_s[:, n % 2, :, :], ACT.Exp
                                       ).then_inc(s["probs_made"], 1)
                    else:
                        act.wait_ge(s["mask_made"], 4 if plan.first and plan.second else 2)
                        act.activation(probs[0:NCTX, n % 2, 0, :], ps_s[0:NCTX, n % 2, 0, :], ACT.Exp,
                                       bias=m["mask_bias"][:, 1 - x:2 - x]).then_inc(s["probs_made"], 1)
                elif kind == "hn":
                    x, tile = t[1:]
                    n = [u for u in plan.tasks if u[0] == "hn_scale"].index(("hn_scale", x)) + 1
                    act.wait_ge(s["hn_scaled"], n)
                    act.activation(rows[x][:, tile, 0:D], xres[:, tile, :], ACT.Identity,
                                   scale=m["c_y"][:, tile:tile + 1], bias=m["c_nb"][:, tile:tile + 1]
                                   ).then_inc(s["hn_made"], 1)
                elif kind == "hn_turn":
                    n = [u for u in units if u[0] == "hn_turn"].index(t)
                    if n >= 2:
                        wait_full(act, logit_units[n - 2])
                    act.activation(hnT[:, n % 2, :, :], bank(t)[:, 0:2 * P].rearrange("p (c q) -> p c q", c=2),
                                   ACT.Copy).then_inc(s["emptied_act"], 1)
                elif kind == "logits":
                    x, tile = t[1:]
                    n = logit_units.index(t)
                    if tile == 0 and n:
                        act.wait_ge(s["sel_made"], n // QT)
                    act.activation(m["th"][:, tile, :], bank(t)[:, 0:E], ACT.Tanh, scale=0.5
                                   ).then_inc(s["emptied_act"], 1)

        @block.vector
        def _(v):
            n_vec = 0

            def link(ins):
                nonlocal n_vec
                n_vec += 1
                ins.then_inc(s["vec_step"], 1)
                v.wait_ge(s["vec_step"], n_vec)

            made = 0
            for use, i in ((plan.first, 0), (plan.second, 1)):
                if use:
                    v.wait_ge(s["mask_loaded"], 64 if plan.first and plan.second else 32)
                    v.tensor_scalar(m["mask_bias"][:, i:i + 1], m["mask_u8"][:, i:i + 1], BIG, -BIG, ALU.mult,
                                    ALU.add).then_inc(s["mask_made"], 1)
                    v.tensor_scalar(m["mask_row"][:, i, :, 0:NCTX],
                                    m["mask_row8"][:, i, :].unsqueeze(1).to_broadcast([1, QT, NCTX]), BIG, -BIG,
                                    ALU.mult, ALU.add).then_inc(s["mask_made"], 1)

            n_quad = n_o = 0
            for t in plan.tasks:
                kind = t[0]
                if kind in ("max", "max_ctx", "proj", "pos"):
                    wait_full(v, t)
                if kind == "stats":
                    v.wait_ge(s["x_loaded"], 16)
                    v.wait_ge(s["ctx_loaded"], 16)
                    for j in range(NKT):
                        src = xin[:, j, :] if j < TPB else m["xctx"][:]
                        i = v.bn_stats(m["bn"][0:rows_of(j), j, :], src)
                    link(i)
                    for j in range(NKT):
                        i = v.bn_aggr(m["mv"][0:rows_of(j), j, :], m["bn"][0:rows_of(j), j, :])
                    link(i)
                    mean, var = m["mv"][:, :, 0], m["mv"][:, :, 1]
                    link(v.tensor_scalar(m["st_v"][:], var, LN_EPS, None, ALU.add))
                    rsqrt(v, link, m["st_v"][:], m["st_i"][:], m["ln_s"][:], m["st_t"][:])
                    lat = slice(0, TPB)
                    link(v.tensor_tensor(m["st_v"][:, lat], m["ln_s"][:, lat], m["ln_s"][:, lat], ALU.mult))
                    link(v.tensor_tensor(m["st_v"][:, lat], m["st_v"][:, lat], var[:, lat], ALU.mult))
                    link(v.tensor_scalar(m["st_v"][:, lat], m["st_v"][:, lat], LN_EPS, None, ALU.add))
                    rsqrt(v, link, m["st_v"][:, lat], m["st_i"][:, lat], m["st_r"][:, lat], m["st_t"][:, lat])
                    link(v.tensor_tensor(m["ln_s"][:, lat], m["ln_s"][:, lat], m["st_r"][:, lat], ALU.mult))
                    v.scalar_tensor_tensor(m["ln_nb"][:], mean, -1.0, m["ln_s"][:], ALU.mult, ALU.mult
                                           ).then_inc(s["stats_done"], 1)
                elif kind == "v":
                    j = t[1]
                    wait_empty(v, ("qk", j))
                    at = 2 * H * (j % 2)
                    v.tensor_reduce(m["rs_v"][:, j // 2 % 2, at:at + 2 * H], sq[:, j % 2, :, :], AX.X, ALU.add
                                    ).then_inc(s["summed"], 1)
                elif kind == "split":
                    pair = t[1]
                    n = min(2, NKT - 2 * pair)
                    v.wait_ge(s["summed"], min(2 * pair + 2, NKT))
                    nr = n * 2 * H
                    r, y, half, shifted = (m[k][:, pair % 2, 0:nr] for k in ("rs_v", "rs_y", "rs_t", "rs_i"))
                    link(v.tensor_scalar(r, r, 1.0 / DH, RMS_EPS ** 2, ALU.mult, ALU.max))
                    rsqrt(v, link, r, shifted, y, half)
                    a0 = 2 * (pair % 2)
                    mine = raw[:, a0:a0 + n, :, :]
                    flat = mine.rearrange("p a h d -> p (a h) d")
                    link(v.tensor_tensor(flat, flat, y.unsqueeze(2).to_broadcast([P, nr, DH]), ALU.mult))
                    v.tensor_tensor(mine, mine, m["gam"][:].unsqueeze(1).to_broadcast([P, n, 2 * H, DH]), ALU.mult
                                    ).then_inc(s["normed"], 1)
                    v.wait_ge(s["hi_made"], pair + 1)
                    if 2 * pair < TPB:
                        for j in (2 * pair, 2 * pair + 1):
                            _, ql, at = q_place(j)
                            v.tensor_tensor(ql[:, :, at, 0:DH], raw[:, j % 4, 0:H, :], st[:, j % 2, 0:H, 0:DH],
                                            ALU.subtract)
                    v.tensor_tensor(st[:, 0:n, H:2 * H, DH:2 * DH], raw[:, a0:a0 + n, H:2 * H, :],
                                    st[:, 0:n, H:2 * H, 0:DH], ALU.subtract).then_inc(s["lo_made"], 1)
                elif kind == "max":
                    x, h, tile, half = t[1:]
                    v.tensor_reduce(m["mp"][:, tile, half:half + 1], bank(t)[:, :], AX.X, ALU.max
                                    ).then_inc(s["emptied_vec"], 1)
                elif kind == "max_ctx":
                    v.tensor_reduce(m["mp"][:, :, 2:3], bank(t)[:, 0:QT * NCP].rearrange("p (q k) -> p q k", q=QT),
                                    AX.X, ALU.max).then_inc(s["emptied_vec"], 1)
                elif kind == "neg":
                    x, h = t[1:]
                    wait_empty(v, ("max_ctx", x, h))
                    link(v.tensor_reduce(m["mx"][:], m["mp"][:], AX.X, ALU.max))
                    v.tensor_scalar(QL[x][:, h, :, DH:VW], m["mx"][:].unsqueeze(2), -1.0, None, ALU.mult
                                    ).then_inc(s["neg_made"], 1)
                elif kind == "o_copy":
                    x, h = t[1:]
                    n_o += 1
                    v.wait_ge(s["values_done"], len(STEPS) * n_o)
                    v.tensor_copy(oT[x][:, h, :], ps_o[0:VW, :]).then_inc(s["o_copied"], 1)
                elif kind == "proj":
                    x, tile, h = t[1:]
                    v.wait_ge(s["xres_based"], QT * x + tile + 1)
                    link(v.reciprocal(m["rden"][:], bank(t)[:, D:D + 1]))
                    i = v.scalar_tensor_tensor(xres[:, tile, :], bank(t)[:, 0:D], m["rden"][:], xres[:, tile, :],
                                               ALU.mult, ALU.add)
                    i.then_inc(s["emptied_vec"], 1)
                    wait_empty(v, t)
                    if h == H - 1:
                        link(v.bn_stats(m["bnC"][:, tile, :], xres[:, tile, :]))
                        link(v.bn_aggr(m["mvC"][:, tile, :], m["bnC"][:, tile, :]))
                elif kind == "hn_scale":
                    if n_quad:
                        v.wait_ge(s["hn_made"], QT * n_quad)
                    link(v.tensor_scalar(m["c_v"][:], m["mvC"][:, :, 1], LN_EPS, None, ALU.add))
                    rsqrt(v, link, m["c_v"][:], m["c_i"][:], m["c_y"][:], m["c_t"][:])
                    v.scalar_tensor_tensor(m["c_nb"][:], m["mvC"][:, :, 0], -1.0, m["c_y"][:], ALU.mult, ALU.mult
                                           ).then_inc(s["hn_scaled"], 1)
                elif kind == "top":
                    x = t[1]
                    n_quad += 1
                    sc, sfc, th, sel = m["sc"], m["sfc"], m["th"], m["sel"]
                    wait_empty(v, ("logits", x, QT - 1))
                    link(v.tensor_scalar(sc[:], th[:], 1.0, 0.5, ALU.add, ALU.mult))
                    link(v.tensor_tensor(sfc[:], sc[:], m["gate_bias"][:].unsqueeze(1).to_broadcast([P, QT, E]),
                                         ALU.add))
                    for q in range(QT):
                        for g in range(G):
                            i = v.max(m["g8"][:, q, g, :], sfc[:, q, g * EG:(g + 1) * EG])
                    link(i)
                    link(v.tensor_tensor(m["gs"][:], m["g8"][:, :, :, 0], m["g8"][:, :, :, 1], ALU.add))
                    for q in range(QT):
                        i = v.max(m["gm8"][:, q, :], m["gs"][:, q, :])
                    link(i)
                    for q in range(QT):
                        i = v.max_index(m["gi"][:, q, :], m["gm8"][:, q, :], m["gs"][:, q, :])
                    link(i)
                    link(v.tensor_copy(m["gif"][:], m["gi"][:]))
                    for q in range(QT):
                        i = v.tensor_tensor(m["geq"][:, q, :, :],
                                            m["group_no"][:].unsqueeze(2).to_broadcast([P, G, TG]),
                                            m["gif"][:, q, 0:TG].unsqueeze(1).to_broadcast([P, G, TG]), ALU.is_equal)
                    link(i)
                    link(v.tensor_reduce(m["gmask"][:], m["geq"][:], AX.X, ALU.add))
                    link(v.tensor_scalar(m["pen"][:], m["gmask"][:], BIG, -BIG, ALU.mult, ALU.add))
                    sfg = sfc[:].rearrange("p q (g e) -> p q g e", g=G)
                    link(v.tensor_tensor(sfg, sfg, m["gmask"][:].unsqueeze(3).to_broadcast([P, QT, G, EG]), ALU.mult))
                    link(v.tensor_tensor(sfg, sfg, m["pen"][:].unsqueeze(3).to_broadcast([P, QT, G, EG]), ALU.add))
                    for q in range(QT):
                        i = v.max(m["v8"][:, q, :], sfc[:, q, :])
                    link(i)
                    for q in range(QT):
                        i = v.match_replace(m["rep"][:, q, :], m["v8"][:, q, :], sfc[:, q, :], -3e38)
                    link(i)
                    link(v.tensor_tensor(sel[:], m["rep"][:], sfc[:], ALU.not_equal))
                    link(v.tensor_copy(m["selb"][:], sel[:]))
                    for q in range(QT - 1):
                        link(v.tensor_tensor(m["carry"][:, q + 1, :], m["carry"][:, q, :], m["selb"][:, q, :],
                                             ALU.add))
                    v.tensor_tensor(m["carry"][:, QT, :], m["carry"][:, QT - 1, :], m["selb"][:, QT - 1, :], ALU.add
                                    ).then_inc(s["sel_made"], 1)
                    link(v.tensor_tensor(m["wsel"][:], sc[:], sel[:], ALU.mult))
                    link(v.tensor_reduce(m["wden"][:], m["wsel"][:], AX.X, ALU.add))
                    link(v.tensor_scalar(m["wden"][:], m["wden"][:], 1e-20, None, ALU.add))
                    link(v.reciprocal(m["wden"][:], m["wden"][:]))
                    link(v.tensor_tensor(m["wsel"][:], m["wsel"][:], m["wden"][:].unsqueeze(2).to_broadcast([P, QT, E]),
                                         ALU.mult))
                    link(v.tensor_scalar(rows[x][:, :, D + 1:ROW], m["wsel"][:], ROUTE_SCALE, None, ALU.mult))
                    v.tensor_copy(rows[x][:, :, D:D + 1], m["token_id"][:, QT * x:QT * x + QT].unsqueeze(2)
                                  ).then_inc(s["rows_made"], 1)
                elif kind == "pos":
                    x = t[1]
                    pos = bank(t)[:, 0:QT * E].rearrange("p (q e) -> p q e", q=QT)
                    key = m["key"]
                    link(v.tensor_tensor(key[:], pos, m["slot_base"][:].unsqueeze(1).to_broadcast([P, QT, E]),
                                         ALU.add))
                    v.scalar_tensor_tensor(m["rep"][:], pos, float(CAP), m["sel"][:], ALU.is_lt, ALU.mult
                                           ).then_inc(s["emptied_vec"], 1)
                    wait_empty(v, t)
                    v.wait_ge(s["sel_made"], n_quad)
                    link(v.tensor_copy(m["carry"][:, 0, :], m["carry"][:, QT, :]))
                    link(v.tensor_tensor(key[:], key[:], m["rep"][:], ALU.mult))
                    for q in range(QT):
                        i = v.max(m["k8"][:, q, :], key[:, q, :])
                    link(i)
                    link(v.tensor_scalar(m["adj"][:], m["k8"][:], 0.0, 1e6, ALU.is_equal, ALU.mult))
                    v.scalar_tensor_tensor(m["slot_idx"][x][:], m["k8"][:], -1.0, m["adj"][:], ALU.add, ALU.add
                                           ).then_inc(s["slots_made"], 1)
                    if x == 1:
                        link(v.tensor_scalar(m["token_id"][:], m["token_id"][:], float(S), None, ALU.add))


def phase2(nc, a, out, slot_rows, s, added, fresh, ctx):
    def sb(name, shape, dt=F32):
        return ctx.enter_context(nc.sbuf_tensor(name, shape, dt))

    w = sb("w_exp", [P, RING, 3 * D])
    xr = sb("x_rows", [P, RING, 2, ROW])
    xT = sb("xT", [P, 2, 2, CAP])
    silu = sb("silu", [P, 2, CAP])
    hid = sb("hid", [P, 2, CAP])
    y = sb("y", [P, RING, 2, D])
    ids = sb("ids", [P, RING, 2], U32)
    ident = sb("ident2", [P, P])
    ps_x = ctx.enter_context(nc.psum_tensor("ps_x", [P, 2, 2, CAP], F32))
    ps_g = ctx.enter_context(nc.psum_tensor("ps_g", [P, 2, 2, CAP], F32))
    ps_y = ctx.enter_context(nc.psum_tensor("ps_y", [P, 2, 2, D], F32))
    rows_dram = slot_rows.rearrange("(e p t) r -> e p t r", p=P, t=2)

    def load(sp, e, r):
        src_w = a["wexp"][e] if isinstance(e, int) else a["wexp"][bass.ds(e, 1)][0]
        src_x = rows_dram[e] if isinstance(e, int) else rows_dram[bass.ds(e, 1)][0]
        sp.dma_start(w[:, r, :], src_w).then_inc(s[f"w_loaded{r}"], 16)
        sp.dma_start(xr[:, r, :, :], src_x).then_inc(s[f"x_in{r}"], 16)

    with nc.Block() as block:
        @block.gpsimd
        def _(pool):
            pool.memset(ident[:], 0.0).then_inc(s["pool_step"], 1)
            pool.wait_ge(s["pool_step"], 1)
            pool.affine_select(out=ident[:], in_=ident[:], compare_op=ALU.not_equal, fill=1.0,
                               base=0, pattern=[[-1, P]], channel_multiplier=1)
    fresh()
    with nc.Fori(0, E // EB) as it:
        with nc.Block() as block:
            @block.sync
            def _(sp):
                for n in range(EB):
                    if n >= RING:
                        sp.wait_ge(s["y_full"], n - RING + 1)
                        sp.wait_ge(s["y_made"], 3 * (n - RING + 1))
                    load(sp, it * EB + n, n % RING)

            @block.tensor
            def _(pe):
                def turn(n):
                    pe.wait_ge(s[f"x_in{n % RING}"], 16 * (n // RING + 1))
                    if n >= 2:
                        pe.wait_ge(s["turned_copied"], n - 1)
                    for c in range(2):
                        for t in range(2):
                            i = pe.transpose(ps_x[:, n % 2, c, t * P:(t + 1) * P],
                                             xr[:, n % RING, t, c * P:(c + 1) * P], ident[:])
                    i.then_inc(s["rows_turned"], 1)

                def gate_up(n):
                    pe.wait_ge(s[f"w_loaded{n % RING}"], 16 * (n // RING + 1))
                    pe.wait_ge(s["turned_copied"], n + 1)
                    if n >= 2:
                        pe.wait_ge(s["h_made"], n - 1)
                    for part in range(2):
                        for c in range(2):
                            k = (2 * part + c) * I
                            i = pe.matmul(ps_g[:, n % 2, part, :], w[:, n % RING, k:k + I], xT[:, n % 2, c, :],
                                          start=(c == 0), stop=(c == 1))
                    i.then_inc(s["gate_up"], 1)

                def down(n):
                    pe.wait_ge(s["h_made"], n + 1)
                    if n >= 2:
                        pe.wait_ge(s["y_made"], 3 * (n - 1))
                    for t in range(2):
                        i = pe.matmul(ps_y[:, n % 2, t, :], hid[:, n % 2, t * P:(t + 1) * P],
                                      w[:, n % RING, 4 * I:4 * I + D], start=True, stop=True)
                    i.then_inc(s["y_full"], 1)

                turn(0)
                for n in range(EB):
                    if n + 1 < EB:
                        turn(n + 1)
                    gate_up(n)
                    if n >= 1:
                        down(n - 1)
                down(EB - 1)

            @block.scalar
            def _(act):
                def copy(n):
                    act.wait_ge(s["rows_turned"], n + 1)
                    if n >= 2:
                        act.wait_ge(s["gate_up"], n - 1)
                    act.activation(xT[:, n % 2, :, :], ps_x[:, n % 2, :, :], ACT.Copy).then_inc(s["turned_copied"], 1)

                copy(0)
                for n in range(EB):
                    if n + 1 < EB:
                        copy(n + 1)
                    act.wait_ge(s["gate_up"], n + 1)
                    if n >= 2:
                        act.wait_ge(s["h_made"], n - 1)
                    act.activation(silu[:, n % 2, :], ps_g[:, n % 2, 0, :], ACT.Silu).then_inc(s["silu_made"], 1)

            @block.vector
            def _(v):
                def hidden(n):
                    v.wait_ge(s["silu_made"], n + 1)
                    if n >= 2:
                        v.wait_ge(s["y_full"], n - 1)
                    v.tensor_tensor(hid[:, n % 2, :], silu[:, n % 2, :], ps_g[:, n % 2, 1, :], ALU.mult
                                    ).then_inc(s["h_made"], 1)

                def weigh(n):
                    r = n % RING
                    v.wait_ge(s["y_full"], n + 1)
                    if n >= RING:
                        v.wait_ge(s["add_done"], n - RING + 1)
                    for t in range(2):
                        v.tensor_scalar(y[:, r, t, :], ps_y[:, n % 2, t, :], xr_w(n, t), None, ALU.mult
                                        ).then_inc(s["y_made"], 1)
                    v.tensor_copy(ids[:, r, :].unsqueeze(2), xr[:, r, :, D:D + 1]).then_inc(s["y_made"], 1)

                def xr_w(n, t):
                    c = it * EB + (D + 1 + n)
                    return xr[:, n % RING, t, bass.ds(c, 1)]

                for n in range(EB):
                    hidden(n)
                    if n >= 1:
                        weigh(n - 1)
                weigh(EB - 1)

            @block.gpsimd
            def _(pool):
                for n in range(EB):
                    r = n % RING
                    pool.wait_ge(s["y_made"], 3 * (n + 1))
                    if n:
                        pool.wait_ge(added, it * (32 * EB) + 32 * n)
                        pool.sem_inc(s["add_done"], 1)
                    for t in range(2):
                        pool.indirect_dma_start(
                            out=out, out_offset=bass.IndirectOffsetOnAxis(ap=ids[:, r, t:t + 1], axis=0),
                            in_=y[:, r, t, :], in_offset=None, bounds_check=NTOK + DUMP - 1, oob_is_err=True,
                            compute_op=ALU.add).then_inc(added, 16)

        fresh()


def kernel(x, ctx_768, mask_BxS2_bk0, L0_xattn_ln_x_g, L0_xattn_ln_x_b, L0_xattn_ln_l_g, L0_xattn_ln_l_b,
           L0_xattn_qn_g, L0_xattn_kn_g, L0_xattn_Wq, L0_xattn_Wkv, L0_xattn_Wlkv, L0_xattn_Wo, L0_xattn_bo,
           L0_ffn_gate_w, L0_ffn_gate_bias, L0_ffn_w_gate, L0_ffn_w_up, L0_ffn_w_down):
    import concourse.bacc as bacc
    from concourse.bass_utils import run_bass_kernel_spmd

    def chunks(wt, rows):
        return wt.reshape(-1, rows, wt.shape[-1]).transpose(1, 0, 2)

    arr = np.asarray
    mask = arr(mask_BxS2_bk0)
    wg = arr(L0_ffn_w_gate).reshape(E, 2, P, I).transpose(0, 2, 1, 3).reshape(E, P, 2 * I)
    wu = arr(L0_ffn_w_up).reshape(E, 2, P, I).transpose(0, 2, 1, 3).reshape(E, P, 2 * I)
    data = {
        "x": arr(x).reshape(NTOK, D),
        "ctx": arr(ctx_768),
        "mask_col": mask.reshape(B, NCTX, 1),
        "mask_row": mask.reshape(B, 1, NCTX),
        "wqkv": chunks(np.concatenate([arr(L0_xattn_Wq).T, arr(L0_xattn_Wlkv).T], axis=1), P),
        "wkvx": chunks(arr(L0_xattn_Wkv).T, DCTX // 2),
        "wo": arr(L0_xattn_Wo).T.reshape(H, DH, D).transpose(1, 0, 2),
        "gate": chunks(arr(L0_ffn_gate_w).T, P),
        "gate_bias": arr(L0_ffn_gate_bias).reshape(1, E),
        "bo": arr(L0_xattn_bo).reshape(1, D),
        "ln_g": arr(L0_xattn_ln_l_g).reshape(2, P).T,
        "ln_b": arr(L0_xattn_ln_l_b).reshape(2, P).T,
        "lx_g": arr(L0_xattn_ln_x_g).reshape(2, DCTX // 2).T,
        "lx_b": arr(L0_xattn_ln_x_b).reshape(2, DCTX // 2).T,
        "qk_g": np.concatenate([arr(L0_xattn_qn_g), arr(L0_xattn_kn_g)]).reshape(1, 2 * DH),
        "wexp": np.concatenate([wg, wu, arr(L0_ffn_w_down)], axis=2),
    }
    nc = bacc.Bacc("TRN2", target_bir_lowering=False, num_devices=1, dynamic_dma_scratch_size=4096)
    arrays, aps = {}, {}
    for name, value in data.items():
        arrays[f"in_{name}"] = np.ascontiguousarray(value)
        aps[name] = nc.dram_tensor(f"in_{name}", value.shape, mybir.dt.from_np(value.dtype),
                                   kind="ExternalInput").ap()
    out = nc.dram_tensor("out_rows", (NTOK + DUMP, D), F32, kind="ExternalOutput").ap()
    build(nc, aps, out)
    r = run_bass_kernel_spmd(nc, [arrays], core_ids=[0])
    return r.results[0]["out_rows"][:NTOK].reshape(B, S, D)
```

```python
from contextlib import ExitStack

import numpy as np

import concourse.bass as bass
from concourse import mybir

F32 = mybir.dt.float32
F32R = mybir.dt.float32r
BF16 = mybir.dt.bfloat16
U32 = mybir.dt.uint32
I32 = mybir.dt.int32
U8 = mybir.dt.uint8
ALU = mybir.AluOpType
ACT = mybir.ActivationFunctionType
AX = mybir.AxisListType

P = 128
B, S, D = 4, 1024, 256
NCTX, DCTX = 77, 192
H, DH = 4, 64
TPB = S // P
QT = 4
QW = QT * P
NKT = TPB + 1
NCP = NCTX + 1
NK = S + NCP
STEPS = [(0, 1), (2, 3), (4, 5), (6, 7), (8,)]
VW = DH + 1
E, TOPK, G, TG, CAP = 64, 8, 8, 4, 256
EG = E // G
I = 128
ROUTE_SCALE = 2.5
NTOK = B * S
DUMP = CAP
ROW = D + 1 + E
LN_EPS = 1e-5
RMS_EPS = 1e-8
BIG = 1e30
MAGIC = 0x5F3759DF
SIDE = 3
RING = 8


class Plan:

    def __init__(self, first, second, keys, route0, route1):
        self.tasks = []
        self.units = []
        self.steps = []
        self.blocks = []
        self.first, self.second, self.keys = first, second, keys
        self.route0, self.route1 = route0, route1
        key_tasks = self.key_tasks() if keys else []
        if first:
            self.maxes(1, 0)
            route = self.route_tasks(0)
            if keys:
                self.add("stats")
            for h in range(H):
                mine = self.mix(self.part(route, [0, 16, 24, 31, 31], h),
                                self.part(key_tasks, [0, 2, 12, 23, 28], h))
                if h == 0:
                    mine = [("idle",)] * 14 + mine
                if h + 1 < H:
                    self.block(1, h, self.mix(mine, self.max_tasks(1, h + 1)))
                else:
                    self.block(1, h, mine + (self.max_tasks(0, 0) if second else []))
        else:
            if keys:
                self.add("stats")
            for t in key_tasks:
                self.add(*t)
            if second:
                self.maxes(0, 0)
        route = self.route_tasks(1)
        if route1 == "project":
            route = [t for t in route if t[0] in ("proj", "store")]
        elif route1 == "rest":
            route = [t for t in route if t[0] not in ("proj", "store")]
        if not route1:
            route = []
        if second:
            for h in range(H):
                mine = self.part(route, [0, 14, 25, 31, 31], h)
                self.block(0, h, self.mix(mine, self.max_tasks(0, h + 1) if h + 1 < H else []))
        else:
            for t in route:
                self.add(*t)

    def part(self, tasks, cuts, h):
        n = len(tasks)
        return tasks[n * cuts[h] // cuts[-1]:n * cuts[h + 1] // cuts[-1]]

    def mix(self, a, b):
        out, i, j = [], 0, 0
        while i < len(a) or j < len(b):
            if j >= len(b) or (i < len(a) and i * len(b) <= j * len(a)):
                out.append(a[i])
                i += 1
            else:
                out.append(b[j])
                j += 1
        return out

    def add(self, kind, *args):
        if kind in ("ln_turn", "qk", "v", "q_turn", "k_turn", "max", "max_ctx", "qb", "proj", "hn_turn", "logits",
                    "pos"):
            self.units.append((kind, *args))
        if kind == "scores":
            self.steps.append(args)
            if args[2] == 0:
                self.blocks.append(args[:2])
        self.tasks.append((kind, *args))

    def key_tasks(self):
        out = [("z", 0), ("z", 1), ("ln_turn", 0)]
        behind = []
        for j in range(NKT):
            for t in (("qk", j), ("v", j), ("ln_turn", j + 1)):
                if t[0] == "ln_turn":
                    if j + 2 < NKT:
                        out.append(("z", j + 2))
                    if j + 1 == NKT:
                        continue
                out.append(t)
                for _ in range(2):
                    if behind:
                        out.append(behind.pop(0))
            if j % 2 == 1 or j == NKT - 1:
                pair = j // 2
                behind += [("rs", pair), ("norm", pair), ("hi", pair), ("lo", pair)]
                for k in range(2 * pair, j + 1):
                    if k < TPB:
                        behind.append(("q_turn", k))
                    behind.append(("k_turn", k))
        return out + behind + [("kv_done",)]

    def max_tasks(self, x, h):
        out = [("max", x, h, t, half) for t in range(QT) for half in range(2)]
        return out + [("max_ctx", x, h), ("neg", x, h), ("qb", x, h)]

    def maxes(self, x, h):
        for t in self.max_tasks(x, h):
            self.add(*t)

    def route_tasks(self, x):
        out = [("proj", x, t, h) for t in range(QT) for h in range(H)]
        out += [("store", x), ("hn_scale", x), ("hn", x, 0)]
        for t in range(QT):
            out.append(("hn_turn", x, t))
            if t + 1 < QT:
                out.append(("hn", x, t + 1))
            out.append(("logits", x, t))
        return out + [("gates", x), ("groups", x), ("best", x), ("pos", x), ("slots", x), ("weights", x),
                      ("scatter", x)]

    def block(self, x, h, side):
        side = list(side)
        n = len(STEPS)
        self.add("scores", x, h, 0)
        done = 0
        slots = 2 * n - 1
        at = 0
        for s in range(n):
            for kind in ("scores", "values"):
                if kind == "scores":
                    if s + 1 >= n:
                        continue
                    self.add("scores", x, h, s + 1)
                else:
                    self.add("values", x, h, s)
                at += 1
                upto = len(side) * at // slots
                for t in side[done:upto]:
                    self.add(*t)
                done = upto
        self.add("o_copy", x, h)


def build(nc, a, out):
    with ExitStack() as ctx:
        def sem(name):
            return ctx.enter_context(nc.semaphore(name))

        slot_rows = nc.dram_tensor("slot_rows", [E * CAP, ROW], F32).ap()
        odd_sum = nc.dram_tensor("odd_sum", [NTOK + DUMP, D], F32).ap()

        first_sem = sem("loaded")
        s = {"loaded": first_sem}
        names = ["const_made", "rows_free", "vec_step", "pool_step", "x_loaded", "xres_loaded", "xres_based", "ctx_loaded",
                 "mask_loaded", "mask_made", "stats_done", "z_made", "unit_full", "emptied_act", "emptied_vec",
                 "summed", "normed", "hi_made", "lo_made", "head_copied0", "head_copied1", "head_copied2", "head_copied3", "neg_made", "scores_full", "probs_made",
                 "values_done", "o_copied", "x2_stored", "hn_scaled", "hn_made", "sel_made", "slots_made",
                 "rows_made",
                 *[f"w_loaded{n}" for n in range(RING)], *[f"x_in{n}" for n in range(RING)],
                 "rows_turned", "turned_copied", "gate_up", "silu_made", "h_made", "y_full", "y_made", "add_done"]
        for n in names:
            s[n] = sem(n)
        last = s[names[-1]]
        scattered, added, filled = sem("scattered"), [sem("added_even"), sem("added_odd")], sem("filled")

        def fresh():
            nc.all_engine_barrier(sems_to_clear=range(first_sem.num, last.num + 1))

        with ExitStack() as p1:
            phase1(nc, a, out, slot_rows, odd_sum, s, scattered, filled, fresh, p1)
        with ExitStack() as p2:
            phase2(nc, a, out, slot_rows, odd_sum, s, added, fresh, p2)


def rsqrt(v, link, x, shifted, y, t):
    link(v.tensor_scalar(shifted, x.bitcast(U32), 1, None, ALU.logical_shift_right))
    link(v.tensor_scalar(y.bitcast(I32), shifted, -1.0, float(MAGIC), ALU.mult, ALU.add))
    for _ in range(3):
        link(v.scalar_tensor_tensor(t, y, -0.5, y, ALU.mult, ALU.mult))
        link(v.tensor_tensor(t, t, x, ALU.mult))
        link(v.scalar_tensor_tensor(y, t, 1.5, y, ALU.add, ALU.mult))


def phase1(nc, a, out, slot_rows, odd_sum, s, scattered, filled, fresh, ctx):
    def sb(name, shape, dt=F32):
        return ctx.enter_context(nc.sbuf_tensor(name, shape, dt))

    wqkv = sb("wqkv_s", [P, 2, 3 * D])
    wkvx = sb("wkvx_s", [DCTX // 2, 2, 2 * D])
    wo = sb("wo_s", [VW, H, D + 1])
    gate = sb("gate_s", [P, 2, E])
    gate_bias = sb("gate_bias_s", [P, E])
    bo = sb("bo_s", [P, D])
    ln_g, ln_b = sb("ln_g_s", [P, 2]), sb("ln_b_s", [P, 2])
    lx_g, lx_b = sb("lx_g_s", [DCTX // 2, 2]), sb("lx_b_s", [DCTX // 2, 2])
    qk_g = sb("qk_g_s", [P, 2 * DH])
    gam = sb("gam", [P, H, DH])
    ident = sb("ident", [P, P])
    tri = sb("tri", [P, P], BF16)
    ones = sb("ones_b", [P, P], BF16)
    one_row = sb("one_row", [1, P], F32R)
    slot_base = sb("slot_base", [P, E])
    group_no = sb("group_no", [P, G])
    token_id = sb("token_id", [P, TPB])

    K = sb("K", [P, H, NK], F32R)
    Kb = sb("Kb", [VW, H, NK], F32R)
    Kn = sb("Kn", [P, H, NK], F32R)
    V = sb("V", [P, H, NKT, VW])
    Vn = sb("Vn", [P, H, NKT, VW])
    Q = [sb("Q0", [P, H, QW], F32R), sb("Q1", [P, H, QW], F32R)]
    Q1n = sb("Q1n", [P, H, QW], F32R)
    QL = [sb("QL0", [P, H, QT, VW]), sb("QL1", [P, H, QT, VW])]
    QL1n = sb("QL1n", [P, H, QT, VW])
    oT = [sb("oT0", [VW, H, QW]), sb("oT1", [VW, H, QW])]
    qbT = [sb("qbT0", [VW, QW], F32R), sb("qbT1", [VW, QW], F32R)]
    probs = sb("probs", [P, 2, 2, QW])

    xin = sb("xin", [P, TPB, D])
    xctx = sb("xctx", [NCTX, DCTX])
    xres = sb("xres", [P, QT, D])
    mask_u8 = sb("mask_u8", [NCTX, 2], U8)
    mask_bias = sb("mask_bias", [NCTX, 2])
    mask_row8 = sb("mask_row8", [1, 2, NCTX], U8)
    mask_row = sb("mask_row", [1, 2, QT, NCP], F32R)
    bn = sb("bn", [P, NKT, 6])
    mv = sb("mv", [P, NKT, 2])
    st_v, st_y, st_t, st_r = (sb(n, [P, NKT]) for n in ("st_v", "st_y", "st_t", "st_r"))
    st_i = sb("st_i", [P, NKT], U32)
    ln_s, ln_nb = sb("ln_s", [P, NKT]), sb("ln_nb", [P, NKT])
    z = sb("z", [P, 2, D])
    lnT = sb("lnT", [P, 2, 2, P])
    raw = sb("raw", [P, 4, 2 * H, DH])
    sq = sb("sq", [P, 2, 2 * H, DH])
    NR = 2 * 2 * H
    rs_v, rs_y, rs_t = (sb(n, [P, 2, NR]) for n in ("rs_v", "rs_y", "rs_t"))
    rs_i = sb("rs_i", [P, 2, NR], U32)
    st = sb("st", [P, 2, 2 * H, 2 * DH])
    mp = sb("mp", [P, QT, 3])
    mx = sb("mx", [P, QT])
    bnC, mvC = sb("bnC", [P, QT, 6]), sb("mvC", [P, QT, 2])
    c_v, c_y, c_t, c_nb = (sb(n, [P, QT]) for n in ("c_v", "c_y", "c_t", "c_nb"))
    c_i = sb("c_i", [P, QT], U32)
    rden = sb("rden", [P, 1])
    rows = [sb("rows0", [P, QT, ROW]), sb("rows1", [P, QT, ROW])]
    hnT = sb("hnT", [P, 2, 2, P])
    th = sb("th", [P, QT, E])
    sc, sfc, rep, sel, wsel, key = (sb(n, [P, QT, E]) for n in ("sc", "sfc", "rep", "sel", "wsel", "key"))
    g8 = sb("g8", [P, QT, G, 8])
    gs, gmask, pen = (sb(n, [P, QT, G]) for n in ("gs", "gmask", "pen"))
    gm8, v8, k8, adj = (sb(n, [P, QT, 8]) for n in ("gm8", "v8", "k8", "adj"))
    gi = sb("gi", [P, QT, 8], U32)
    gif = sb("gif", [P, QT, 8])
    geq = sb("geq", [P, QT, G, TG])
    selb = sb("selb", [P, QT, E], BF16)
    carry = sb("carry", [P, QT + 1, E], BF16)
    wden = sb("wden", [P, QT])
    not_full = sb("not_full", [P, 1], I32)
    slot_idx = [sb("slot_idx0", [P, QT, 8], U32), sb("slot_idx1", [P, QT, 8], U32)]

    ps_s = ctx.enter_context(nc.psum_tensor("ps_s", [P, 2, 2, QW], F32))
    ps_o = ctx.enter_context(nc.psum_tensor("ps_o", [P, QW], F32))
    ps_u = ctx.enter_context(nc.psum_tensor("ps_u", [P, SIDE, 512], F32))

    setup(nc, a, out, slot_rows, s, locals())
    main = locals()
    fresh()
    attend(nc, a, out, slot_rows, odd_sum, s, scattered, filled, main, Plan(False, True, True, False, False), -1)
    fresh()
    with nc.Fori(0, B - 1) as b:
        attend(nc, a, out, slot_rows, odd_sum, s, scattered, filled, main, Plan(True, True, True, True, True), b)
        fresh()
    attend(nc, a, out, slot_rows, odd_sum, s, scattered, filled, main, Plan(True, False, False, True, "project"), B - 1)
    fresh()
    not_full = count_full(nc, s, main)
    fresh()
    with nc.If(not_full > 0):
        attend(nc, a, out, slot_rows, odd_sum, s, scattered, filled, main, Plan(False, False, False, False, "rest"), B - 1)
        fresh()


def count_full(nc, s, m):
    counts, few = m["ps_u"][:, 0, 0:E], m["wden"]
    with nc.Block() as block:
        @block.tensor
        def _(pe):
            pe.matmul(counts, m["ones"][:], m["carry"][:, 0, :], start=True, stop=True).then_inc(s["unit_full"], 1)

        @block.vector
        def _(v):
            v.wait_ge(s["unit_full"], 1)
            v.tensor_scalar(m["key"][:, 0, :], counts, float(CAP), None, ALU.is_lt).then_inc(s["vec_step"], 1)
            v.wait_ge(s["vec_step"], 1)
            v.tensor_reduce(few[:, 0:1], m["key"][:, 0, :], AX.X, ALU.add).then_inc(s["vec_step"], 1)
            v.wait_ge(s["vec_step"], 2)
            v.tensor_copy(m["not_full"][:], few[:, 0:1])
    return nc.values_load(m["not_full"][0:1, 0:1], min_val=0, max_val=E)


def setup(nc, a, out, slot_rows, s, m):
    with ExitStack() as ctx:
        empty = m["rows"][0][:, 0:2, :]
        ctx.enter_context(nc.allow_non_contiguous_dma(reason="small constants"))
        with nc.Block() as block:
            LOADS = 11

            @block.sync
            def _(sp):
                for dst, src in ((m["wqkv"], a["wqkv"]), (m["wkvx"], a["wkvx"]), (m["gate"], a["gate"]),
                                 (m["ln_g"], a["ln_g"]), (m["ln_b"], a["ln_b"]), (m["lx_g"], a["lx_g"]),
                                 (m["lx_b"], a["lx_b"])):
                    sp.dma_start(dst[:], src).then_inc(s["loaded"], 16)
                sp.dma_start(m["gate_bias"][:], a["gate_bias"].to_broadcast([P, E])).then_inc(s["loaded"], 16)
                sp.dma_start(m["bo"][:], a["bo"].to_broadcast([P, D])).then_inc(s["loaded"], 16)
                sp.dma_start(m["qk_g"][:], a["qk_g"].to_broadcast([P, 2 * DH])).then_inc(s["loaded"], 16)
                sp.wait_ge(s["const_made"], 2)
                sp.dma_start(m["wo"][0:DH, :, 0:D], a["wo"]).then_inc(s["loaded"], 16)
                sp.wait_ge(s["loaded"], 16 * LOADS)

            @block.gpsimd
            def _(pool):
                n = 0

                def link(ins):
                    nonlocal n
                    n += 1
                    ins.then_inc(s["pool_step"], 1)
                    pool.wait_ge(s["pool_step"], n)

                link(pool.memset(m["wo"][:], 0.0))
                pool.memset(m["wo"][DH:VW, :, D:D + 1], 1.0).then_inc(s["const_made"], 2)
                pool.wait_ge(s["const_made"], 2)
                link(pool.memset(empty, 0.0))
                link(pool.iota(empty[:, :, D:D + 1], pattern=[[P, 2], [0, 1]], base=NTOK, channel_multiplier=1,
                               allow_small_or_imprecise_dtypes=True))
                link(pool.memset(m["ident"][:], 0.0))
                link(pool.affine_select(out=m["ident"][:], in_=m["ident"][:], compare_op=ALU.not_equal, fill=1.0,
                                        base=0, pattern=[[-1, P]], channel_multiplier=1))
                link(pool.memset(m["ones"][:], 1.0))
                link(pool.affine_select(out=m["tri"][:], in_=m["ones"][:], compare_op=ALU.is_gt, fill=0.0,
                                        base=0, pattern=[[1, P]], channel_multiplier=-1))
                link(pool.iota(m["slot_base"][:], pattern=[[CAP, E]], base=1, channel_multiplier=0,
                               allow_small_or_imprecise_dtypes=True))
                link(pool.iota(m["group_no"][:], pattern=[[1, G]], base=0, channel_multiplier=0,
                               allow_small_or_imprecise_dtypes=True))
                link(pool.iota(m["token_id"][:], pattern=[[P, TPB]], base=0, channel_multiplier=1,
                               allow_small_or_imprecise_dtypes=True))

            @block.vector
            def _(v):
                v.memset(m["one_row"][:].bitcast(F32), 1.0)
                v.memset(m["Kb"][DH:VW, :, :].bitcast(F32), 1.0)
                v.memset(m["V"][:], 1.0)
                v.memset(m["Vn"][:], 1.0)
                v.memset(m["mv"][:], 1.0)
                v.memset(m["raw"][:], 1.0)
                v.memset(m["sq"][:], 1.0)
                v.memset(m["carry"][:], 0.0)
                v.memset(m["QL1n"][:], 0.0)
                v.memset(m["rows"][1][:], 0.0)
                v.memset(m["slot_idx"][1][:], 1 << 20)
                v.memset(m["Kn"][:].bitcast(F32), 0.0)
                v.memset(m["K"][:, :, NK - 1:NK].bitcast(F32), 0.0)
                v.memset(m["mask_row"][:].bitcast(F32), -BIG)
                v.wait_ge(s["loaded"], 16 * LOADS)
                for h in range(H):
                    v.scalar_tensor_tensor(m["gam"][:, h, :], m["qk_g"][:, 0:DH], DH ** -0.5,
                                           m["qk_g"][:, DH:2 * DH], ALU.mult, ALU.mult)


def attend(nc, a, out, slot_rows, odd_sum, s, scattered, filled, m, plan, b):
    K, Kb, Kn, V, Vn, Q, Q1n, QL, QL1n = (m[n] for n in ("K", "Kb", "Kn", "V", "Vn", "Q", "Q1n", "QL", "QL1n"))
    ps_s, ps_o, ps_u, probs, oT, qbT = (m[n] for n in ("ps_s", "ps_o", "ps_u", "probs", "oT", "qbT"))
    ident, lnT, z, st, raw, sq = (m[n] for n in ("ident", "lnT", "z", "st", "raw", "sq"))
    xin, xres, rows, hnT = (m[n] for n in ("xin", "xres", "rows", "hnT"))

    QUAD_SCATTERS = 16 * QT * TOPK

    def unit_owner(u):
        return "vec" if u[0] in ("max", "max_ctx", "proj", "pos") else "act"

    units, steps, blocks = plan.units, plan.steps, plan.blocks
    unit_no = {u: i for i, u in enumerate(units)}
    step_no = {u: i for i, u in enumerate(steps)}
    block_no = {u: i for i, u in enumerate(blocks)}
    max_no = {u: i for i, u in enumerate([t[1:] for t in plan.tasks if t[0] == "qb"])}
    proj_units = [u for u in units if u[0] == "proj"]
    logit_units = [u for u in units if u[0] == "logits"]

    def bank(u):
        return ps_u[:, unit_no[u] % SIDE, :]

    def wait_full(eng, u):
        eng.wait_ge(s["unit_full"], unit_no[u] + 1)

    def count_empty(u):
        return sum(unit_owner(w) == unit_owner(u) for w in units[:unit_no[u] + 1])

    def wait_empty(eng, u):
        eng.wait_ge(s["emptied_" + unit_owner(u)], count_empty(u))

    def rows_of(j):
        return P if j < TPB else NCTX

    def q_place(j):
        return (Q[0], QL[0], j) if j < QT else (Q1n, QL1n, j - QT)

    x_dram = a["x"].rearrange("(b t p) d -> b p t d", b=B, p=P)
    out_dram = out[0:NTOK, :].rearrange("(b t p) d -> b p t d", b=B, p=P)

    def of_batch(ap, n):
        return ap[n] if isinstance(n, int) else ap[bass.ds(n, 1)][0]

    with nc.Block() as block:
        @block.sync
        def _(sp):
            if plan.keys:
                sp.dma_start(xin[:], of_batch(x_dram, b + 1)).then_inc(s["x_loaded"], 16)
                sp.dma_start(m["xctx"][:], of_batch(a["ctx"], b + 1)).then_inc(s["ctx_loaded"], 16)
            n_mask = 0
            for use, i, n in ((plan.first, 0, b), (plan.second, 1, b + 1)):
                if use:
                    n_mask += 2
                    sp.dma_start(m["mask_u8"][:, i:i + 1], of_batch(a["mask_col"], n)).then_inc(s["mask_loaded"], 16)
                    sp.dma_start(m["mask_row8"][:, i, :], of_batch(a["mask_row"], n)).then_inc(s["mask_loaded"], 16)

            def load_residual(x):
                sp.dma_start(xres[:], of_batch(x_dram, b)[:, QT * x:QT * x + QT, :]).then_inc(s["xres_loaded"], 16)

            if plan.route0:
                load_residual(0)

            if plan.keys and not plan.first:
                zero = rows[1][:, 0:2, 0:D]
                sp.dma_start(slot_rows.rearrange("(e p t) r -> p e (t r)", p=P, t=2),
                             rows[0][:, 0:2, :].rearrange("p t r -> p (t r)").unsqueeze(1).to_broadcast(
                                 [P, E, 2 * ROW])).then_inc(filled, 16)
                sp.dma_start(out[NTOK:NTOK + DUMP, :].rearrange("(p t) d -> p t d", t=2), zero).then_inc(filled, 16)
                sp.dma_start(odd_sum.rearrange("(p t) d -> p t d", p=P),
                             rows[1][:, 0:1, 0:D].to_broadcast([P, (NTOK + DUMP) // P, D])).then_inc(filled, 16)

            def copy_head(h):
                for dst, src in ((K[:, h, :], Kn[:, h, :]), (Kb[0:DH, h, :], Kn[0:DH, h, :]),
                                 (V[:, h, :, :], Vn[:, h, :, :]), (Q[1][:, h, :], Q1n[:, h, :]),
                                 (QL[1][:, h, :, :], QL1n[:, h, :, :])):
                    sp.dma_start(dst.bitcast(F32), src.bitcast(F32)).then_inc(s[f"head_copied{h}"], 16)

            def keys_made():
                wait_empty(sp, ("k_turn", NKT - 1))
                sp.wait_ge(s["lo_made"], (NKT + 1) // 2)

            stored = 0
            for t in plan.tasks:
                if t[0] == "kv_done":
                    keys_made()
                    if not plan.first:
                        for h in range(H):
                            copy_head(h)
                if t[0] == "o_copy" and t[1] == 1 and plan.second:
                    if t[2] == 0:
                        keys_made()
                    sp.wait_ge(s["values_done"], len(STEPS) * (block_no[t[1:]] + 1))
                    copy_head(t[2])
                if t[0] == "store":
                    stored += 1
                    x = t[1]
                    wait_empty(sp, ("proj", x, QT - 1, H - 1))
                    sp.dma_start(of_batch(out_dram, b)[:, QT * x:QT * x + QT, :], xres[:]).then_inc(s["x2_stored"], 16)
                if t == ("logits", 0, QT - 1):
                    sp.wait_ge(s["x2_stored"], 16)
                    sp.wait_ge(s["hn_made"], QT)
                    load_residual(1)
            if stored:
                sp.wait_ge(s["x2_stored"], 16 * stored)
            if plan.keys and not plan.first:
                sp.wait_ge(filled, 16 * 3)

        @block.gpsimd
        def _(pool):
            n = 0

            def add_bias(x):
                pool.wait_ge(s["xres_loaded"], 16 * (x + 1))
                for j in range(QT):
                    pool.tensor_tensor(xres[:, j, :], xres[:, j, :], m["bo"][:], ALU.add).then_inc(s["xres_based"], 1)
                    pool.wait_ge(s["xres_based"], QT * x + j + 1)

            def scatter(x):
                for q in range(QT):
                    for k in range(TOPK):
                        pool.indirect_dma_start(
                            out=slot_rows, out_offset=bass.IndirectOffsetOnAxis(
                                ap=m["slot_idx"][x][:, q, k:k + 1], axis=0),
                            in_=rows[x][:, q, :], in_offset=None, bounds_check=E * CAP - 1,
                            oob_is_err=False).then_inc(scattered, 16)

            if plan.route0:
                add_bias(0)
                scatter(1)
                pool.wait_ge(scattered, b * (2 * QUAD_SCATTERS) + QUAD_SCATTERS)
                pool.sem_inc(s["rows_free"], 1)
            for t in plan.tasks:
                if t[0] == "scatter" and (t[1] == 0 or not plan.second):
                    n += 1
                    pool.wait_ge(s["slots_made"], n)
                    pool.wait_ge(s["rows_made"], n)
                    pool.wait_ge(s["hn_made"], QT * n)
                    scatter(t[1])
                if t == ("logits", 0, QT - 1):
                    add_bias(1)

        @block.tensor
        def _(pe):
            def free_bank(u):
                if unit_no[u] >= SIDE:
                    wait_empty(pe, units[unit_no[u] - SIDE])

            for t in plan.tasks:
                kind = t[0]
                if t in unit_no:
                    free_bank(t)
                if kind == "ln_turn":
                    j = t[1]
                    w, rj = (P, rows_of(j)) if j < TPB else (DCTX // 2, NCTX)
                    pe.wait_ge(s["z_made"], j + 1)
                    for c in range(2):
                        i = pe.transpose(bank(t)[0:w, c * P:c * P + rj], z[0:rj, j % 2, c * w:(c + 1) * w],
                                         ident[0:rj, 0:rj])
                    i.then_inc(s["unit_full"], 1)
                elif kind in ("qk", "v"):
                    j = t[1]
                    rj = rows_of(j)
                    wait_empty(pe, ("ln_turn", j))
                    w = P if j < TPB else DCTX // 2
                    if kind == "qk":
                        dst = bank(t)[0:rj, 0:2 * D] if j < TPB else bank(t)[0:rj, D:2 * D]
                    else:
                        dst = bank(t)[0:rj, 0:D]
                    for c in range(2):
                        if j < TPB:
                            rhs = m["wqkv"][:, c, 0:2 * D] if kind == "qk" else m["wqkv"][:, c, 2 * D:3 * D]
                        else:
                            rhs = m["wkvx"][:, c, 0:D] if kind == "qk" else m["wkvx"][:, c, D:2 * D]
                        i = pe.matmul(dst, lnT[0:w, j % 2, c, 0:rj], rhs, start=(c == 0), stop=(c == 1))
                    i.then_inc(s["unit_full"], 1)
                elif kind in ("q_turn", "k_turn"):
                    j = t[1]
                    rj = rows_of(j)
                    pair = j // 2
                    pe.wait_ge(s["hi_made"], pair + 1)
                    pe.wait_ge(s["lo_made"], pair + 1)
                    h0 = 0 if kind == "q_turn" else H
                    for h in range(H):
                        i = pe.transpose(bank(t)[:, h * P:h * P + rj], st[0:rj, j % 2, h0 + h, :], ident[0:rj, 0:rj])
                    i.then_inc(s["unit_full"], 1)
                elif kind in ("max", "max_ctx", "qb"):
                    x, h = t[1:3]
                    keys = K if x == 1 else Kn
                    if x == 0:
                        wait_empty(pe, ("k_turn", NKT - 1))
                    if kind == "max":
                        tile, half = t[3:5]
                        i = pe.matmul(bank(t)[:, :], Q[x][:, h, tile * P:(tile + 1) * P],
                                      keys[:, h, half * 512:(half + 1) * 512], start=True, stop=True)
                    elif kind == "max_ctx":
                        pe.wait_ge(s["mask_made"], 4 if plan.first and plan.second else 2)
                        pe.matmul(bank(t)[:, 0:QT * NCP], m["one_row"][:],
                                  m["mask_row"][:, 1 - x, :, :].rearrange("o q k -> o (q k)"), start=True, stop=False,
                                  skip_group_check=True)
                        for tile in range(QT):
                            i = pe.matmul(bank(t)[:, tile * NCP:(tile + 1) * NCP],
                                          Q[x][:, h, tile * P:(tile + 1) * P], keys[:, h, S:NK],
                                          start=False, stop=(tile == QT - 1), skip_group_check=True)
                    else:
                        pe.wait_ge(s["neg_made"], max_no[(x, h)] + 1)
                        for tile in range(QT):
                            i = pe.transpose(bank(t)[0:VW, tile * P:(tile + 1) * P], QL[x][:, h, tile, :], ident[:])
                    i.then_inc(s["unit_full"], 1)
                elif kind == "scores":
                    x, h, st_ = t[1:]
                    n = step_no[t[1:]]
                    wait_empty(pe, ("qb", x, h))
                    if x == 0:
                        pe.wait_ge(s[f"head_copied{h}"], 16 * 5)
                    if n >= 2:
                        pe.wait_ge(s["probs_made"], n - 1)
                    for i_kt, kt in enumerate(STEPS[st_]):
                        rk = rows_of(kt)
                        dst = ps_s[0:rk, n % 2, i_kt, :]
                        pe.matmul(dst, K[:, h, kt * P:kt * P + rk], Q[x][:, h, :], start=True, stop=False)
                        i = pe.matmul(dst, Kb[:, h, kt * P:kt * P + rk], qbT[max_no[(x, h)] % 2][:],
                                      start=False, stop=True)
                    i.then_inc(s["scores_full"], 1)
                elif kind == "values":
                    x, h, st_ = t[1:]
                    n = step_no[t[1:]]
                    pe.wait_ge(s["probs_made"], n + 1)
                    if st_ == 0 and block_no[(x, h)] >= 1:
                        pe.wait_ge(s["o_copied"], block_no[(x, h)])
                    for i_kt, kt in enumerate(STEPS[st_]):
                        rk = rows_of(kt)
                        i = pe.matmul(ps_o[0:VW, :], V[0:rk, h, kt, :], probs[0:rk, n % 2, i_kt, :],
                                      start=(kt == 0), stop=(kt == NKT - 1))
                    i.then_inc(s["values_done"], 1)
                elif kind == "proj":
                    x, tile, h = t[1:]
                    if x == 1:
                        pe.wait_ge(s["o_copied"], H)
                    i = pe.matmul(bank(t)[:, 0:D + 1], oT[x][:, h, tile * P:(tile + 1) * P], m["wo"][:, h, :],
                                  start=True, stop=True)
                    i.then_inc(s["unit_full"], 1)
                elif kind == "hn_turn":
                    x, tile = t[1:]
                    n = [u for u in units if u[0] == "hn_turn"].index(t)
                    pe.wait_ge(s["hn_made"], n + 1)
                    for c in range(2):
                        i = pe.transpose(bank(t)[:, c * P:(c + 1) * P], rows[x][:, tile, c * P:(c + 1) * P], ident[:])
                    i.then_inc(s["unit_full"], 1)
                elif kind == "logits":
                    n = logit_units.index(t)
                    wait_empty(pe, ("hn_turn",) + t[1:])
                    for c in range(2):
                        i = pe.matmul(bank(t)[:, 0:E], hnT[:, n % 2, c, :], m["gate"][:, c, :],
                                      start=(c == 0), stop=(c == 1))
                    i.then_inc(s["unit_full"], 1)
                elif kind == "pos":
                    n = [u for u in units if u[0] == "pos"].index(t)
                    pe.wait_ge(s["sel_made"], n + 1)
                    for tile in range(QT):
                        dst = bank(t)[:, tile * E:(tile + 1) * E]
                        pe.matmul(dst, m["tri"][:], m["selb"][:, tile, :], start=(tile == 0), stop=False,
                                  skip_group_check=True)
                        i = pe.matmul(dst, m["ones"][:], m["carry"][:, tile, :], start=False, stop=(tile == QT - 1),
                                      skip_group_check=True)
                    i.then_inc(s["unit_full"], 1)

        @block.scalar
        def _(act):
            for t in plan.tasks:
                kind = t[0]
                if kind in ("ln_turn", "qk", "v", "q_turn", "k_turn", "qb", "hn_turn", "logits"):
                    wait_full(act, t)
                if kind == "z":
                    j = t[1]
                    rj, w = rows_of(j), (D if j < TPB else DCTX)
                    act.wait_ge(s["stats_done"], 1)
                    if j >= 2:
                        wait_full(act, ("ln_turn", j - 2))
                    src = xin[:, j, :] if j < TPB else m["xctx"][:]
                    act.activation(z[0:rj, j % 2, 0:w], src, ACT.Identity, scale=m["ln_s"][0:rj, j:j + 1],
                                   bias=m["ln_nb"][0:rj, j:j + 1]).then_inc(s["z_made"], 1)
                elif kind == "ln_turn":
                    j = t[1]
                    rj = rows_of(j)
                    w = P if j < TPB else DCTX // 2
                    g_, b_ = (m["ln_g"], m["ln_b"]) if j < TPB else (m["lx_g"], m["lx_b"])
                    if j >= 2:
                        wait_full(act, ("v", j - 2))
                    for c in range(2):
                        i = act.activation(lnT[0:w, j % 2, c, 0:rj], bank(t)[0:w, c * P:c * P + rj], ACT.Identity,
                                           scale=g_[:, c:c + 1], bias=b_[:, c:c + 1])
                    i.then_inc(s["emptied_act"], 1)
                elif kind == "qk":
                    j = t[1]
                    rj = rows_of(j)
                    h0 = 0 if j < TPB else H
                    if j >= 4:
                        act.wait_ge(s["lo_made"], (j - 4) // 2 + 1)
                    if j >= 2:
                        act.wait_ge(s["summed"], j - 1)
                    src = bank(t)[0:rj, h0 * DH:2 * D]
                    act.activation(raw[0:rj, j % 4, h0:2 * H, :], src, ACT.Copy)
                    act.activation(sq[0:rj, j % 2, h0:2 * H, :], src, ACT.Square).then_inc(s["emptied_act"], 1)
                elif kind == "v":
                    j = t[1]
                    rj = rows_of(j)
                    act.activation(Vn[0:rj, :, j, 0:DH], bank(t)[0:rj, 0:D].rearrange("p (h d) -> p h d", h=H),
                                   ACT.Copy).then_inc(s["emptied_act"], 1)
                elif kind == "hi":
                    pair = t[1]
                    n = min(2, NKT - 2 * pair)
                    act.wait_ge(s["normed"], pair + 1)
                    if pair >= 1:
                        wait_full(act, ("k_turn", 2 * pair - 1))
                    a0 = 2 * (pair % 2)
                    act.activation(st[:, 0:n, :, 0:DH].bitcast(F32R), raw[:, a0:a0 + n, :, :], ACT.Copy)
                    act.activation(st[:, 0:n, 0:H, DH:2 * DH].bitcast(F32R), raw[:, a0:a0 + n, 0:H, :], ACT.Copy
                                   ).then_inc(s["hi_made"], 1)
                elif kind == "q_turn":
                    j = t[1]
                    dst, _, at = q_place(j)
                    i = act.activation(dst[:, :, at * P:(at + 1) * P], bank(t).rearrange("p (h q) -> p h q", h=H),
                                       ACT.Copy)
                    i.then_inc(s["emptied_act"], 1)
                elif kind == "k_turn":
                    j = t[1]
                    rj = rows_of(j)
                    i = act.activation(Kn[:, :, j * P:j * P + rj],
                                       bank(t).rearrange("p (h q) -> p h q", h=H)[:, :, 0:rj], ACT.Copy)
                    i.then_inc(s["emptied_act"], 1)
                elif kind == "qb":
                    x, h = t[1:]
                    n = max_no[(x, h)]
                    if n >= 2:
                        act.wait_ge(s["scores_full"], step_no[blocks[n - 2] + (len(STEPS) - 1,)] + 1)
                    act.activation(qbT[n % 2][:], bank(t)[0:VW, :], ACT.Copy).then_inc(s["emptied_act"], 1)
                elif kind == "scores":
                    x, h, st_ = t[1:]
                    n = step_no[t[1:]]
                    act.wait_ge(s["scores_full"], n + 1)
                    if n >= 2:
                        act.wait_ge(s["values_done"], n - 1)
                    if len(STEPS[st_]) == 2:
                        act.activation(probs[:, n % 2, :, :], ps_s[:, n % 2, :, :], ACT.Exp
                                       ).then_inc(s["probs_made"], 1)
                    else:
                        act.wait_ge(s["mask_made"], 4 if plan.first and plan.second else 2)
                        act.activation(probs[0:NCTX, n % 2, 0, :], ps_s[0:NCTX, n % 2, 0, :], ACT.Exp,
                                       bias=m["mask_bias"][:, 1 - x:2 - x]).then_inc(s["probs_made"], 1)
                elif kind == "o_copy":
                    x, h = t[1:]
                    n = block_no[(x, h)]
                    act.wait_ge(s["values_done"], len(STEPS) * (n + 1))
                    act.activation(oT[x][:, h, :], ps_o[0:VW, :], ACT.Copy).then_inc(s["o_copied"], 1)
                elif kind == "hn":
                    x, tile = t[1:]
                    n = [u for u in plan.tasks if u[0] == "hn_scale"].index(("hn_scale", x)) + 1
                    act.wait_ge(s["hn_scaled"], n)
                    if x == 1 and plan.route0:
                        act.wait_ge(s["rows_free"], 1)
                    act.activation(rows[x][:, tile, 0:D], xres[:, tile, :], ACT.Identity,
                                   scale=m["c_y"][:, tile:tile + 1], bias=m["c_nb"][:, tile:tile + 1]
                                   ).then_inc(s["hn_made"], 1)
                elif kind == "hn_turn":
                    n = [u for u in units if u[0] == "hn_turn"].index(t)
                    if n >= 2:
                        wait_full(act, logit_units[n - 2])
                    act.activation(hnT[:, n % 2, :, :], bank(t)[:, 0:2 * P].rearrange("p (c q) -> p c q", c=2),
                                   ACT.Copy).then_inc(s["emptied_act"], 1)
                elif kind == "logits":
                    x, tile = t[1:]
                    n = logit_units.index(t)
                    if tile == 0 and n:
                        act.wait_ge(s["sel_made"], n // QT)

                    act.activation(m["th"][:, tile, :], bank(t)[:, 0:E], ACT.Tanh, scale=0.5
                                   ).then_inc(s["emptied_act"], 1)

        @block.vector
        def _(v):
            n_vec = 0

            def link(ins):
                nonlocal n_vec
                n_vec += 1
                ins.then_inc(s["vec_step"], 1)
                v.wait_ge(s["vec_step"], n_vec)

            made = 0
            for use, i in ((plan.first, 0), (plan.second, 1)):
                if use:
                    v.wait_ge(s["mask_loaded"], 64 if plan.first and plan.second else 32)
                    v.tensor_scalar(m["mask_bias"][:, i:i + 1], m["mask_u8"][:, i:i + 1], BIG, -BIG, ALU.mult,
                                    ALU.add).then_inc(s["mask_made"], 1)
                    v.tensor_scalar(m["mask_row"][:, i, :, 0:NCTX],
                                    m["mask_row8"][:, i, :].unsqueeze(1).to_broadcast([1, QT, NCTX]), BIG, -BIG,
                                    ALU.mult, ALU.add).then_inc(s["mask_made"], 1)

            n_quad = 0
            for t in plan.tasks:
                kind = t[0]
                if kind in ("max", "max_ctx", "proj", "pos"):
                    wait_full(v, t)
                if kind == "stats":
                    v.wait_ge(s["x_loaded"], 16)
                    v.wait_ge(s["ctx_loaded"], 16)
                    for j in range(NKT):
                        src = xin[:, j, :] if j < TPB else m["xctx"][:]
                        i = v.bn_stats(m["bn"][0:rows_of(j), j, :], src)
                    link(i)
                    for j in range(NKT):
                        i = v.bn_aggr(m["mv"][0:rows_of(j), j, :], m["bn"][0:rows_of(j), j, :])
                    link(i)
                    mean, var = m["mv"][:, :, 0], m["mv"][:, :, 1]
                    link(v.tensor_scalar(m["st_v"][:], var, LN_EPS, None, ALU.add))
                    rsqrt(v, link, m["st_v"][:], m["st_i"][:], m["ln_s"][:], m["st_t"][:])
                    lat = slice(0, TPB)
                    link(v.tensor_tensor(m["st_v"][:, lat], m["ln_s"][:, lat], m["ln_s"][:, lat], ALU.mult))
                    link(v.tensor_tensor(m["st_v"][:, lat], m["st_v"][:, lat], var[:, lat], ALU.mult))
                    link(v.tensor_scalar(m["st_v"][:, lat], m["st_v"][:, lat], LN_EPS, None, ALU.add))
                    rsqrt(v, link, m["st_v"][:, lat], m["st_i"][:, lat], m["st_r"][:, lat], m["st_t"][:, lat])
                    link(v.tensor_tensor(m["ln_s"][:, lat], m["ln_s"][:, lat], m["st_r"][:, lat], ALU.mult))
                    v.scalar_tensor_tensor(m["ln_nb"][:], mean, -1.0, m["ln_s"][:], ALU.mult, ALU.mult
                                           ).then_inc(s["stats_done"], 1)
                elif kind == "v":
                    j = t[1]
                    wait_empty(v, ("qk", j))
                    at = 2 * H * (j % 2)
                    v.tensor_reduce(m["rs_v"][:, j // 2 % 2, at:at + 2 * H], sq[:, j % 2, :, :], AX.X, ALU.add
                                    ).then_inc(s["summed"], 1)
                elif kind in ("rs", "norm", "lo"):
                    pair = t[1]
                    n = min(2, NKT - 2 * pair)
                    nr = n * 2 * H
                    r, y, half, shifted = (m[k][:, pair % 2, 0:nr] for k in ("rs_v", "rs_y", "rs_t", "rs_i"))
                    a0 = 2 * (pair % 2)
                    if kind == "rs":
                        v.wait_ge(s["summed"], min(2 * pair + 2, NKT))
                        link(v.tensor_scalar(r, r, 1.0 / DH, RMS_EPS ** 2, ALU.mult, ALU.max))
                        rsqrt(v, link, r, shifted, y, half)
                    elif kind == "norm":
                        flat = raw[:, a0:a0 + n, :, :].rearrange("p a h d -> p (a h) d")
                        link(v.tensor_tensor(flat, flat, y.unsqueeze(2).to_broadcast([P, nr, DH]), ALU.mult))
                        mine = raw[:, a0:a0 + n, 0:H, :]
                        v.tensor_tensor(mine, mine, m["gam"][:].unsqueeze(1).to_broadcast([P, n, H, DH]), ALU.mult
                                        ).then_inc(s["normed"], 1)
                    else:
                        v.wait_ge(s["hi_made"], pair + 1)
                        if 2 * pair < TPB:
                            _, ql, at = q_place(2 * pair)
                            for i in range(2):
                                v.tensor_tensor(ql[:, :, at + i, 0:DH], raw[:, a0 + i, 0:H, :], st[:, i, 0:H, 0:DH],
                                                ALU.subtract)
                        v.tensor_tensor(st[:, 0:n, H:2 * H, DH:2 * DH], raw[:, a0:a0 + n, H:2 * H, :],
                                        st[:, 0:n, H:2 * H, 0:DH], ALU.subtract).then_inc(s["lo_made"], 1)
                elif kind == "max":
                    x, h, tile, half = t[1:]
                    v.tensor_reduce(m["mp"][:, tile, half:half + 1], bank(t)[:, :], AX.X, ALU.max
                                    ).then_inc(s["emptied_vec"], 1)
                elif kind == "max_ctx":
                    v.tensor_reduce(m["mp"][:, :, 2:3], bank(t)[:, 0:QT * NCP].rearrange("p (q k) -> p q k", q=QT),
                                    AX.X, ALU.max).then_inc(s["emptied_vec"], 1)
                elif kind == "neg":
                    x, h = t[1:]
                    wait_empty(v, ("max_ctx", x, h))
                    link(v.tensor_reduce(m["mx"][:], m["mp"][:], AX.X, ALU.max))
                    v.tensor_scalar(QL[x][:, h, :, DH:VW], m["mx"][:].unsqueeze(2), -1.0, None, ALU.mult
                                    ).then_inc(s["neg_made"], 1)
                elif kind == "proj":
                    x, tile, h = t[1:]
                    v.wait_ge(s["xres_based"], QT * x + tile + 1)
                    link(v.reciprocal(m["rden"][:], bank(t)[:, D:D + 1]))
                    i = v.scalar_tensor_tensor(xres[:, tile, :], bank(t)[:, 0:D], m["rden"][:], xres[:, tile, :],
                                               ALU.mult, ALU.add)
                    i.then_inc(s["emptied_vec"], 1)
                    wait_empty(v, t)
                    if h == H - 1:
                        link(v.bn_stats(m["bnC"][:, tile, :], xres[:, tile, :]))
                        link(v.bn_aggr(m["mvC"][:, tile, :], m["bnC"][:, tile, :]))
                elif kind == "hn_scale":
                    if n_quad:
                        v.wait_ge(s["hn_made"], QT * n_quad)
                    link(v.tensor_scalar(m["c_v"][:], m["mvC"][:, :, 1], LN_EPS, None, ALU.add))
                    rsqrt(v, link, m["c_v"][:], m["c_i"][:], m["c_y"][:], m["c_t"][:])
                    v.scalar_tensor_tensor(m["c_nb"][:], m["mvC"][:, :, 0], -1.0, m["c_y"][:], ALU.mult, ALU.mult
                                           ).then_inc(s["hn_scaled"], 1)
                elif kind == "gates":
                    x = t[1]
                    n_quad += 1
                    sc, sfc, th, sel = m["sc"], m["sfc"], m["th"], m["sel"]
                    if x == 1 and plan.route0:
                        v.wait_ge(s["rows_free"], 1)
                    wait_empty(v, ("logits", x, QT - 1))
                    link(v.tensor_scalar(sc[:], th[:], 1.0, 0.5, ALU.add, ALU.mult))
                    link(v.tensor_tensor(sfc[:], sc[:], m["gate_bias"][:].unsqueeze(1).to_broadcast([P, QT, E]),
                                         ALU.add))
                    for q in range(QT):
                        for g in range(G):
                            i = v.max(m["g8"][:, q, g, :], sfc[:, q, g * EG:(g + 1) * EG])
                    link(i)
                    link(v.tensor_tensor(m["gs"][:], m["g8"][:, :, :, 0], m["g8"][:, :, :, 1], ALU.add))
                elif kind == "groups":
                    for q in range(QT):
                        i = v.max(m["gm8"][:, q, :], m["gs"][:, q, :])
                    link(i)
                    for q in range(QT):
                        i = v.max_index(m["gi"][:, q, :], m["gm8"][:, q, :], m["gs"][:, q, :])
                    link(i)
                    link(v.tensor_copy(m["gif"][:], m["gi"][:]))
                    for q in range(QT):
                        i = v.tensor_tensor(m["geq"][:, q, :, :],
                                            m["group_no"][:].unsqueeze(2).to_broadcast([P, G, TG]),
                                            m["gif"][:, q, 0:TG].unsqueeze(1).to_broadcast([P, G, TG]), ALU.is_equal)
                    link(i)
                    link(v.tensor_reduce(m["gmask"][:], m["geq"][:], AX.X, ALU.add))
                    link(v.tensor_scalar(m["pen"][:], m["gmask"][:], BIG, -BIG, ALU.mult, ALU.add))
                    sfg = sfc[:].rearrange("p q (g e) -> p q g e", g=G)
                    link(v.tensor_tensor(sfg, sfg, m["gmask"][:].unsqueeze(3).to_broadcast([P, QT, G, EG]), ALU.mult))
                    link(v.tensor_tensor(sfg, sfg, m["pen"][:].unsqueeze(3).to_broadcast([P, QT, G, EG]), ALU.add))
                elif kind == "best":
                    for q in range(QT):
                        i = v.max(m["v8"][:, q, :], sfc[:, q, :])
                    link(i)
                    for q in range(QT):
                        i = v.match_replace(m["rep"][:, q, :], m["v8"][:, q, :], sfc[:, q, :], -3e38)
                    link(i)
                    link(v.tensor_tensor(sel[:], m["rep"][:], sfc[:], ALU.not_equal))
                    link(v.tensor_copy(m["selb"][:], sel[:]))
                    for q in range(QT - 1):
                        link(v.tensor_tensor(m["carry"][:, q + 1, :], m["carry"][:, q, :], m["selb"][:, q, :],
                                             ALU.add))
                    v.tensor_tensor(m["carry"][:, QT, :], m["carry"][:, QT - 1, :], m["selb"][:, QT - 1, :], ALU.add
                                    ).then_inc(s["sel_made"], 1)
                elif kind == "weights":
                    x = t[1]
                    link(v.tensor_tensor(m["wsel"][:], sc[:], sel[:], ALU.mult))
                    link(v.tensor_reduce(m["wden"][:], m["wsel"][:], AX.X, ALU.add))
                    link(v.tensor_scalar(m["wden"][:], m["wden"][:], 1e-20, None, ALU.add))
                    link(v.reciprocal(m["wden"][:], m["wden"][:]))
                    link(v.tensor_tensor(m["wsel"][:], m["wsel"][:], m["wden"][:].unsqueeze(2).to_broadcast([P, QT, E]),
                                         ALU.mult))
                    link(v.tensor_scalar(rows[x][:, :, D + 1:ROW], m["wsel"][:], ROUTE_SCALE, None, ALU.mult))
                    v.tensor_copy(rows[x][:, :, D:D + 1], m["token_id"][:, QT * x:QT * x + QT].unsqueeze(2)
                                  ).then_inc(s["rows_made"], 1)
                    if x == 1:
                        v.wait_ge(s["rows_made"], n_quad)
                        link(v.tensor_scalar(m["token_id"][:], m["token_id"][:], float(S), None, ALU.add))
                elif kind == "pos":
                    x = t[1]
                    pos = bank(t)[:, 0:QT * E].rearrange("p (q e) -> p q e", q=QT)
                    key = m["key"]
                    link(v.tensor_tensor(key[:], pos, m["slot_base"][:].unsqueeze(1).to_broadcast([P, QT, E]),
                                         ALU.add))
                    v.scalar_tensor_tensor(m["rep"][:], pos, float(CAP), m["sel"][:], ALU.is_lt, ALU.mult
                                           ).then_inc(s["emptied_vec"], 1)
                elif kind == "slots":
                    x = t[1]
                    key = m["key"]
                    wait_empty(v, ("pos", x))
                    v.wait_ge(s["sel_made"], n_quad)
                    link(v.tensor_copy(m["carry"][:, 0, :], m["carry"][:, QT, :]))
                    link(v.tensor_tensor(key[:], key[:], m["rep"][:], ALU.mult))
                    for q in range(QT):
                        i = v.max(m["k8"][:, q, :], key[:, q, :])
                    link(i)
                    link(v.tensor_scalar(m["adj"][:], m["k8"][:], 0.0, 1e6, ALU.is_equal, ALU.mult))
                    v.scalar_tensor_tensor(m["slot_idx"][x][:], m["k8"][:], -1.0, m["adj"][:], ALU.add, ALU.add
                                           ).then_inc(s["slots_made"], 1)


def phase2(nc, a, out, slot_rows, odd_sum, s, added, fresh, ctx):
    def sb(name, shape, dt=F32):
        return ctx.enter_context(nc.sbuf_tensor(name, shape, dt))

    START = RING
    w = sb("w_exp", [P, RING, 3 * D])
    xr = sb("x_rows", [P, RING, 2, ROW])
    xT = sb("xT", [P, 2, 2, CAP])
    silu = sb("silu", [P, 2, CAP])
    hid = sb("hid", [P, 2, CAP])
    y = sb("y", [P, RING, 2, D])
    ids = sb("ids", [P, RING, 2], U32)
    ident = sb("ident2", [P, P])
    ps_x = ctx.enter_context(nc.psum_tensor("ps_x", [P, 2, 2, CAP], F32))
    ps_g = ctx.enter_context(nc.psum_tensor("ps_g", [P, 2, 2, CAP], F32))
    ps_y = ctx.enter_context(nc.psum_tensor("ps_y", [P, 2, 2, D], F32))
    rows_dram = slot_rows.rearrange("(e p t) r -> e p t r", p=P, t=2)
    PASSES = E // RING - 1

    def steps(eng, first, step):
        with eng.Fori(0, PASSES) as it:
            for r in range(RING):
                step(first + r, it)
        for c in range(first + RING * PASSES, E):
            step(c, 0)

    def at(c, it, n=0, k=1):
        return k * (c + n) + (it * (k * RING) if not isinstance(it, int) else 0)

    with nc.Block() as block:
        @block.sync
        def _(sp):
            def load(c, it):
                r = c % RING
                e = at(c, it)
                sp.dma_start(w[:, r, :], a["wexp"][e] if isinstance(e, int) else a["wexp"][bass.ds(e, 1)][0]
                             ).then_inc(s[f"w_loaded{r}"], 16)
                sp.dma_start(xr[:, r, :, :], rows_dram[e] if isinstance(e, int) else rows_dram[bass.ds(e, 1)][0]
                             ).then_inc(s[f"x_in{r}"], 16)

            def reload(c, it):
                sp.wait_ge(s["y_full"], at(c, it, 1 - RING + START))
                sp.wait_ge(s["y_made"], at(c, it, 1 - RING + START))
                load(c, it)

            for c in range(RING):
                load(c, 0)
            steps(sp, RING, reload)

        @block.tensor
        def _(pe):
            def turn(c, it):
                pe.wait_ge(s[f"x_in{c % RING}"], 16 * (c // RING + 1) + (it * 16 if not isinstance(it, int) else 0))
                pe.wait_ge(s["turned_copied"], at(c, it, START - 1))
                for k in range(2):
                    for t in range(2):
                        i = pe.transpose(ps_x[:, c % 2, k, t * P:(t + 1) * P],
                                         xr[:, c % RING, t, k * P:(k + 1) * P], ident[:])
                i.then_inc(s["rows_turned"], 1)

            def gate_up(c, it):
                pe.wait_ge(s[f"w_loaded{c % RING}"], 16 * (c // RING + 1) + (it * 16 if not isinstance(it, int) else 0))
                pe.wait_ge(s["turned_copied"], at(c, it, START + 1))
                pe.wait_ge(s["h_made"], at(c, it, START - 1))
                for part in range(2):
                    for k in range(2):
                        o = (2 * part + k) * I
                        i = pe.matmul(ps_g[:, c % 2, part, :], w[:, c % RING, o:o + I], xT[:, c % 2, k, :],
                                      start=(k == 0), stop=(k == 1))
                i.then_inc(s["gate_up"], 1)

            def down(c, it):
                pe.wait_ge(s["h_made"], at(c, it, START + 1))
                pe.wait_ge(s["y_made"], at(c, it, START - 1))
                for t in range(2):
                    i = pe.matmul(ps_y[:, c % 2, t, :], hid[:, c % 2, t * P:(t + 1) * P],
                                  w[:, c % RING, 4 * I:4 * I + D], start=True, stop=True)
                i.then_inc(s["y_full"], 1)

            pe.sem_inc(s["gate_up"], START)
            pe.sem_inc(s["y_full"], START)
            pe.wait_ge(s["const_made"], 1)
            turn(0, 0)
            turn(1, 0)
            gate_up(0, 0)

            def step(c, it):
                if c < E - 1:
                    turn(c + 1, it)
                gate_up(c, it)
                down(c - 1, it)

            steps(pe, 1, step)
            down(E - 1, 0)

        @block.scalar
        def _(act):
            def copy(c, it):
                act.wait_ge(s["rows_turned"], at(c, it, 1))
                act.wait_ge(s["gate_up"], at(c, it, START - 1))
                act.activation(xT[:, c % 2, :, :], ps_x[:, c % 2, :, :], ACT.Copy).then_inc(s["turned_copied"], 1)

            def gate(c, it):
                act.wait_ge(s["gate_up"], at(c, it, START + 1))
                act.wait_ge(s["h_made"], at(c, it, START - 1))
                act.activation(silu[:, c % 2, :], ps_g[:, c % 2, 0, :], ACT.Silu).then_inc(s["silu_made"], 1)

            act.sem_inc(s["turned_copied"], START)
            copy(0, 0)
            copy(1, 0)
            gate(0, 0)

            def step(c, it):
                if c < E - 1:
                    copy(c + 1, it)
                gate(c, it)

            steps(act, 1, step)

        @block.vector
        def _(v):
            def hidden(c, it):
                v.wait_ge(s["silu_made"], at(c, it, 1))
                v.wait_ge(s["y_full"], at(c, it, START - 1))
                v.tensor_tensor(hid[:, c % 2, :], silu[:, c % 2, :], ps_g[:, c % 2, 1, :], ALU.mult
                                ).then_inc(s["h_made"], 1)

            def weigh(c, it):
                r = c % RING
                v.wait_ge(s["y_full"], at(c, it, START + 1))
                v.wait_ge(s["add_done"], at(c, it, START - RING + 1))
                for t in range(2):
                    col = at(c, it, D + 1)
                    v.tensor_scalar(y[:, r, t, :], ps_y[:, c % 2, t, :],
                                    xr[:, r, t, col:col + 1] if isinstance(col, int) else xr[:, r, t, bass.ds(col, 1)],
                                    None, ALU.mult)
                v.tensor_copy(ids[:, r, :].unsqueeze(2), xr[:, r, :, D:D + 1]).then_inc(s["y_made"], 1)

            v.sem_inc(s["h_made"], START)
            v.sem_inc(s["y_made"], START)
            hidden(0, 0)

            def step(c, it):
                hidden(c, it)
                weigh(c - 1, it)

            steps(v, 1, step)
            weigh(E - 1, 0)

        @block.gpsimd
        def _(pool):
            def add(c, it):
                r = c % RING
                for t in range(2):
                    pool.indirect_dma_start(
                        out=(out, odd_sum)[c % 2], out_offset=bass.IndirectOffsetOnAxis(ap=ids[:, r, t:t + 1], axis=0),
                        in_=y[:, r, t, :], in_offset=None, bounds_check=NTOK + DUMP - 1, oob_is_err=True,
                        compute_op=ALU.add).then_inc(added[c % 2], 16)

            def step(c, it):
                pool.wait_ge(s["y_made"], at(c, it, START + 1))
                pool.wait_ge(added[c % 2], 32 * (c // 2) + (it * (16 * RING) if not isinstance(it, int) else 0))
                pool.sem_inc(s["add_done"], 1)
                add(c, it)

            pool.memset(ident[:], 0.0).then_inc(s["pool_step"], 1)
            pool.wait_ge(s["pool_step"], 1)
            pool.affine_select(out=ident[:], in_=ident[:], compare_op=ALU.not_equal, fill=1.0,
                               base=0, pattern=[[-1, P]], channel_multiplier=1).then_inc(s["const_made"], 1)
            pool.sem_inc(s["add_done"], START)
            for c in range(2):
                pool.wait_ge(s["y_made"], at(c, 0, START + 1))
                add(c, 0)
            steps(pool, 2, step)
            for parity in range(2):
                pool.wait_ge(added[parity], 16 * E)
    fresh()
    join(nc, out, odd_sum, s, ctx)


def join(nc, out, odd_sum, s, ctx):
    PARTS, BUFS, T = 8, 4, NTOK // P // 8
    even = ctx.enter_context(nc.sbuf_tensor("even_rows", [P, BUFS, T, D], F32))
    odd = ctx.enter_context(nc.sbuf_tensor("odd_rows", [P, BUFS, T, D], F32))
    out_v = out[0:NTOK, :].rearrange("(n p t) d -> n p t d", p=P, t=T)
    odd_v = odd_sum[0:NTOK, :].rearrange("(n p t) d -> n p t d", p=P, t=T)
    with nc.Block() as block:
        @block.sync
        def _(sp):
            for n in range(PARTS):
                if n >= BUFS:
                    sp.wait_ge(s[f"w_loaded{n % BUFS}"], 16 * (n // BUFS))
                sp.dma_start(even[:, n % BUFS, :, :], out_v[n]).then_inc(s[f"x_in{n % BUFS}"], 16)
                sp.dma_start(odd[:, n % BUFS, :, :], odd_v[n]).then_inc(s[f"x_in{n % BUFS}"], 16)

        @block.vector
        def _(v):
            for n in range(PARTS):
                v.wait_ge(s[f"x_in{n % BUFS}"], 32 * (n // BUFS + 1))
                v.tensor_tensor(even[:, n % BUFS, :, :], even[:, n % BUFS, :, :], odd[:, n % BUFS, :, :], ALU.add
                                ).then_inc(s["y_made"], 1)

        @block.scalar
        def _(act):
            for n in range(PARTS):
                act.wait_ge(s["y_made"], n + 1)
                act.dma_start(out_v[n], even[:, n % BUFS, :, :]).then_inc(s[f"w_loaded{n % BUFS}"], 16)
            for n in range(BUFS):
                act.wait_ge(s[f"w_loaded{n}"], 16 * (PARTS // BUFS))


def kernel(x, ctx_768, mask_BxS2_bk0, L0_xattn_ln_x_g, L0_xattn_ln_x_b, L0_xattn_ln_l_g, L0_xattn_ln_l_b,
           L0_xattn_qn_g, L0_xattn_kn_g, L0_xattn_Wq, L0_xattn_Wkv, L0_xattn_Wlkv, L0_xattn_Wo, L0_xattn_bo,
           L0_ffn_gate_w, L0_ffn_gate_bias, L0_ffn_w_gate, L0_ffn_w_up, L0_ffn_w_down):
    import concourse.bacc as bacc
    from concourse.bass_utils import run_bass_kernel_spmd

    def chunks(wt, rows):
        return wt.reshape(-1, rows, wt.shape[-1]).transpose(1, 0, 2)

    arr = np.asarray
    mask = arr(mask_BxS2_bk0)
    wg = arr(L0_ffn_w_gate).reshape(E, 2, P, I).transpose(0, 2, 1, 3).reshape(E, P, 2 * I)
    wu = arr(L0_ffn_w_up).reshape(E, 2, P, I).transpose(0, 2, 1, 3).reshape(E, P, 2 * I)
    data = {
        "x": arr(x).reshape(NTOK, D),
        "ctx": arr(ctx_768),
        "mask_col": mask.reshape(B, NCTX, 1),
        "mask_row": mask.reshape(B, 1, NCTX),
        "wqkv": chunks(np.concatenate([arr(L0_xattn_Wq).T, arr(L0_xattn_Wlkv).T], axis=1), P),
        "wkvx": chunks(arr(L0_xattn_Wkv).T, DCTX // 2),
        "wo": arr(L0_xattn_Wo).T.reshape(H, DH, D).transpose(1, 0, 2),
        "gate": chunks(arr(L0_ffn_gate_w).T, P),
        "gate_bias": arr(L0_ffn_gate_bias).reshape(1, E),
        "bo": arr(L0_xattn_bo).reshape(1, D),
        "ln_g": arr(L0_xattn_ln_l_g).reshape(2, P).T,
        "ln_b": arr(L0_xattn_ln_l_b).reshape(2, P).T,
        "lx_g": arr(L0_xattn_ln_x_g).reshape(2, DCTX // 2).T,
        "lx_b": arr(L0_xattn_ln_x_b).reshape(2, DCTX // 2).T,
        "qk_g": np.concatenate([arr(L0_xattn_qn_g), arr(L0_xattn_kn_g)]).reshape(1, 2 * DH),
        "wexp": np.concatenate([wg, wu, arr(L0_ffn_w_down)], axis=2),
    }
    nc = bacc.Bacc("TRN2", target_bir_lowering=False, num_devices=1, dynamic_dma_scratch_size=4096)
    arrays, aps = {}, {}
    for name, value in data.items():
        arrays[f"in_{name}"] = np.ascontiguousarray(value)
        aps[name] = nc.dram_tensor(f"in_{name}", value.shape, mybir.dt.from_np(value.dtype),
                                   kind="ExternalInput").ap()
    out = nc.dram_tensor("out_rows", (NTOK + DUMP, D), F32, kind="ExternalOutput").ap()
    build(nc, aps, out)
    r = run_bass_kernel_spmd(nc, [arrays], core_ids=[0])
    return r.results[0]["out_rows"][:NTOK].reshape(B, S, D)
```

```python
from contextlib import ExitStack

import numpy as np

import concourse.bass as bass
from concourse import mybir

F32 = mybir.dt.float32
F32R = mybir.dt.float32r
BF16 = mybir.dt.bfloat16
U32 = mybir.dt.uint32
I32 = mybir.dt.int32
U8 = mybir.dt.uint8
ALU = mybir.AluOpType
ACT = mybir.ActivationFunctionType
AX = mybir.AxisListType

P = 128
B, S, D = 4, 1024, 256
NCTX, DCTX = 77, 192
H, DH = 4, 64
TPB = S // P
QT = 4
QW = QT * P
NKT = TPB + 1
NCP = NCTX + 1
NK = S + NCP
STEPS = [(0, 1), (2, 3), (4, 5), (6, 7), (8,)]
VW = DH + 1
E, TOPK, G, TG, CAP = 64, 8, 8, 4, 256
EG = E // G
I = 128
ROUTE_SCALE = 2.5
NTOK = B * S
DUMP = CAP
ROW = D + 1 + E
LN_EPS = 1e-5
RMS_EPS = 1e-8
BIG = 1e30
MAGIC = 0x5F3759DF
SIDE = 3
RING = 8


COST = {"lag": 2.5, "z": 0.3, "ln_turn": 0.8, "qk": 1.4, "v": 0.9, "rs": 0.7, "norm": 1.2, "norm_q": 0.7,
        "stats": 0.9, "x_next": 0.0, "residual_next": 0.0, "hi": 2.0, "lo": 2.2,
        "q_turn": 0.7, "k_turn": 0.7, "kv_done": 0.0, "max": 0.7, "max_ctx": 0.9, "neg": 0.5, "qb": 0.6,
        "proj": 1.0, "store": 0.0, "hn_scale": 0.7, "hn": 0.4, "hn_turn": 0.6, "logits": 0.6, "gates": 0.9,
        "group_sums": 0.8, "groups": 0.8, "group_ids": 0.8, "mask_groups": 1.0, "bar_groups": 0.9, "best": 0.8,
        "replace": 0.8, "chosen": 0.8, "count": 1.2, "pos": 0.8, "slots": 1.2, "slot_ids": 0.5, "weights": 1.4,
        "scale_weights": 1.2, "scatter": 0.0}
STATS_PIECES = 9
CHOICE = ("gates", "group_sums", "groups", "group_ids", "mask_groups", "bar_groups", "best", "replace", "chosen",
          "count", "pos", "slots", "slot_ids", "weights", "scale_weights")
FILLS = 4


class Plan:

    def __init__(self, first, second, keys, route0, route1):
        self.tasks = []
        self.units = []
        self.steps = []
        self.blocks = []
        self.first, self.second, self.keys = first, second, keys
        self.route0, self.route1 = route0, route1
        key_tasks = self.key_tasks() if keys else []
        route = self.route_tasks(1) if route1 else []
        todo = []
        if first:
            pinned = [self.max_tasks(1, h) for h in range(1, H)] + [self.max_tasks(0, 0) if second else []]
            if second:
                sides = self.spread(self.mix(self.route_tasks(0), key_tasks), pinned)
            else:
                sides = self.last_sides(route)
                route = sides.pop()
            for h in range(H):
                if h == H - 1 and second:
                    todo.append((1, h, sides[h] + pinned[h]))
                else:
                    todo.append((1, h, self.mix(sides[h], pinned[h])))
        else:
            for t in key_tasks + self.max_tasks(0, 0):
                self.add(*t)
        if second:
            pinned = [self.max_tasks(0, h) for h in range(1, H)] + [self.max_tasks(2, 0)]
            stats = [("lag",)] * 4 + [("stats", n) for n in range(STATS_PIECES)]
            sides = self.spread([("x_next",), *self.mix(route or [("residual_next",)], stats)], pinned)
            todo += [(0, h, self.mix(sides[h], pinned[h])) for h in range(H)]
            route = []
        self.attention(todo)
        for t in route:
            self.add(*t)

    def last_sides(self, route1):
        route0 = self.route_tasks(0)
        proj = [[t for t in route1 if t[0] == "proj" and t[3] == h] for h in range(H)]
        norm = route0.index(("hn_scale", 0, 0))
        choice = route0.index(("logits", 0, QT - 1)) + 1
        by_tile = self.route_tasks(1, parts=[(q, q + 1) for q in range(QT)])
        return [route0[:norm], route0[norm:choice], self.mix(route0[choice:], proj[0]), proj[1] + proj[2],
                proj[3] + [t for t in by_tile if t[0] != "proj"]]

    def cost(self, tasks):
        return sum(COST[t[0]] for t in tasks)

    def spread(self, tasks, pinned):
        share = (self.cost(tasks) + sum(self.cost(p) for p in pinned)) / len(pinned)
        out, i = [], 0
        for n, p in enumerate(pinned):
            room = share - self.cost(p)
            mine = []
            while i < len(tasks) and (room > 0 or n == len(pinned) - 1):
                room -= self.cost(tasks[i:i + 1])
                mine.append(tasks[i])
                i += 1
            out.append(mine)
        return out

    def mix(self, a, b):
        out, i, j, done_a, done_b = [], 0, 0, 0.0, 0.0
        all_a, all_b = max(self.cost(a), 0.1), max(self.cost(b), 0.1)
        while i < len(a) or j < len(b):
            if j >= len(b) or (i < len(a) and done_a / all_a <= done_b / all_b):
                done_a += self.cost(a[i:i + 1])
                out.append(a[i])
                i += 1
            else:
                done_b += self.cost(b[j:j + 1])
                out.append(b[j])
                j += 1
        return out

    def add(self, kind, *args):
        if kind in ("ln_turn", "qk", "v", "q_turn", "k_turn", "max", "max_ctx", "qb", "proj", "hn_turn", "logits",
                    "pos"):
            self.units.append((kind, *args))
        if kind == "scores":
            self.steps.append(args)
            if args[2] == 0:
                self.blocks.append(args[:2])
        self.tasks.append((kind, *args))

    def key_tasks(self):
        out = [("z", 0), ("z", 1), ("ln_turn", 0)]
        behind = []
        for j in range(NKT):
            for t in (("ln_turn", j + 1), ("qk", j), ("v", j)):
                if t[0] == "ln_turn":
                    if j + 2 < NKT:
                        out.append(("z", j + 2))
                    if j + 1 == NKT:
                        continue
                out.append(t)
                for _ in range(3):
                    if behind:
                        out.append(behind.pop(0))
            if j % 2 == 1 or j == NKT - 1:
                pair = j // 2
                behind += [("rs", pair, n) for n in range(4)]
                behind += [("norm", pair), ("norm_q", pair), ("hi", pair), ("lo", pair)] + [("lag",)] * 4
                for k in range(2 * pair, j + 1):
                    if k < TPB:
                        behind.append(("q_turn", k))
                    behind.append(("k_turn", k))
        return out + behind + [("kv_done",)]

    def max_tasks(self, x, h):
        out = [("max", x, h, t, half) for t in range(QT) for half in range(2)]
        return out + [("max_ctx", x, h), ("neg", x, h), ("lag",), ("qb", x, h)]

    def route_tasks(self, x, parts=((0, QT),)):
        out = [("proj", x, t, h) for t in range(QT) for h in range(H)]
        out += [("store", x)] + [("hn_scale", x, n) for n in range(4)] + [("lag",)]
        out += [("hn", x, t) for t in range(QT)]
        for t in range(QT):
            out.append(("hn_turn", x, t))
            if t:
                out.append(("logits", x, t - 1))
        out.append(("logits", x, QT - 1))
        if x == 1:
            out.append(("residual_next",))
        for part in parts:
            out += [("gates", x, *part), *[("group_sums", x, q) for q in range(*part)]]
            out += [(kind, x, *part) for kind in ("groups", "group_ids", "mask_groups", "bar_groups", "best", "replace",
                                                  "chosen", "count")]
            out += [("lag",)]
            out += [(kind, x, *part) for kind in ("pos", "slots", "slot_ids", "weights", "scale_weights", "scatter")]
        return out

    def attention(self, todo):
        order = [(x, h, s) for x, h, _ in todo for s in range(len(STEPS))]
        self.add("scores", *order[0])
        for n, (x, h, s) in enumerate(order):
            if s == 0:
                side = list(todo[n // len(STEPS)][2])
                whole, done, at = self.cost(side), 0.0, 0
                slots = 2 * len(STEPS) - 2
            for kind in ("scores", "values"):
                if kind == "values":
                    self.add("values", x, h, s)
                elif n + 1 < len(order):
                    self.add("scores", *order[n + 1])
                at += 1
                while side and (at >= slots or done < whole * at / slots):
                    done += self.cost(side[:1])
                    self.add(*side.pop(0))
            if s == len(STEPS) - 1:
                self.add("o_copy", x, h)


def build(nc, a, out):
    with ExitStack() as ctx:
        def sem(name):
            return ctx.enter_context(nc.semaphore(name))

        slot_rows = nc.dram_tensor("slot_rows", [E * CAP, ROW], F32).ap()
        odd_sum = nc.dram_tensor("odd_sum", [NTOK + DUMP, D], F32).ap()

        first_sem = sem("loaded")
        s = {"loaded": first_sem}
        names = ["const_made", "rows_free", "vec_step", "pool_step", "x_loaded", "xres_loaded", "xres_based",
                 "ctx_loaded", "mask_loaded", "mask_made", "stats_done", "z_made", "unit_full", "emptied_act",
                 "emptied_vec", "summed", "normed", "hi_made", "lo_made", "head_copied0", "head_copied1",
                 "head_copied2", "head_copied3", "neg_made", "scores_full", "probs_made", "values_done", "o_copied",
                 "x2_stored", "hn_scaled", "hn_made", "sel_made", "slots_made",
                 "rows_made",
                 *[f"w_loaded{n}" for n in range(RING)], *[f"x_in{n}" for n in range(RING)],
                 "rows_turned", "turned_copied", "gate_up", "silu_made", "h_made", "y_full", "y_made", "add_done"]
        for n in names:
            s[n] = sem(n)
        last = s[names[-1]]
        scattered, added, filled = sem("scattered"), [sem("added_even"), sem("added_odd")], sem("filled")

        def fresh():
            nc.all_engine_barrier(sems_to_clear=range(first_sem.num, last.num + 1))

        with ExitStack() as p1:
            phase1(nc, a, out, slot_rows, odd_sum, s, scattered, filled, fresh, p1)
        with ExitStack() as p2:
            phase2(nc, a, out, slot_rows, odd_sum, s, added, fresh, p2)


def rsqrt(v, link, x, shifted, y, t, pieces=range(4)):
    if 0 in pieces:
        link(v.tensor_scalar(shifted, x.bitcast(U32), 1, None, ALU.logical_shift_right))
        link(v.tensor_scalar(y.bitcast(I32), shifted, -1.0, float(MAGIC), ALU.mult, ALU.add))
    for n in pieces:
        if n > 0:
            link(v.scalar_tensor_tensor(t, y, -0.5, y, ALU.mult, ALU.mult))
            link(v.tensor_tensor(t, t, x, ALU.mult))
            link(v.scalar_tensor_tensor(y, t, 1.5, y, ALU.add, ALU.mult))


def layernorm_stats(v, link, s, m, piece):
    eps_v, scale, scale2, half, shifted = (m[n] for n in ("st_v", "ln_s", "st_r", "st_t", "st_i"))
    mean, var = m["mv"][:, :, 0], m["mv"][:, :, 1]
    lat = slice(0, TPB)
    if piece < 3:
        if piece == 0:
            v.wait_ge(s["x_loaded"], 16)
            v.wait_ge(s["ctx_loaded"], 16)
        for j in range(3 * piece, 3 * piece + 3):
            src = m["xin"][:, j, :] if j < TPB else m["xctx"][:]
            rj = P if j < TPB else NCTX
            i = v.bn_stats(m["bn"][0:rj, j, :], src)
        link(i)
    elif piece == 3:
        for j in range(NKT):
            rj = P if j < TPB else NCTX
            i = v.bn_aggr(m["mv"][0:rj, j, :], m["bn"][0:rj, j, :])
        link(i)
    elif piece == 4:
        link(v.tensor_scalar(eps_v[:], var, LN_EPS, None, ALU.add))
        rsqrt(v, link, eps_v[:], shifted[:], scale[:], half[:], (0, 1))
    elif piece == 5:
        rsqrt(v, link, eps_v[:], shifted[:], scale[:], half[:], (2, 3))
    elif piece == 6:
        link(v.tensor_tensor(eps_v[:, lat], scale[:, lat], scale[:, lat], ALU.mult))
        link(v.tensor_tensor(eps_v[:, lat], eps_v[:, lat], var[:, lat], ALU.mult))
        link(v.tensor_scalar(eps_v[:, lat], eps_v[:, lat], LN_EPS, None, ALU.add))
        rsqrt(v, link, eps_v[:, lat], shifted[:, lat], scale2[:, lat], half[:, lat], (0,))
    elif piece == 7:
        rsqrt(v, link, eps_v[:, lat], shifted[:, lat], scale2[:, lat], half[:, lat], (1, 2))
    else:
        rsqrt(v, link, eps_v[:, lat], shifted[:, lat], scale2[:, lat], half[:, lat], (3,))
        link(v.tensor_tensor(scale[:, lat], scale[:, lat], scale2[:, lat], ALU.mult))
        v.scalar_tensor_tensor(m["ln_nb"][:], mean, -1.0, scale[:], ALU.mult, ALU.mult).then_inc(s["stats_done"], 1)


def phase1(nc, a, out, slot_rows, odd_sum, s, scattered, filled, fresh, ctx):
    def sb(name, shape, dt=F32):
        return ctx.enter_context(nc.sbuf_tensor(name, shape, dt))

    wqkv = sb("wqkv_s", [P, 2, 3 * D])
    wkvx = sb("wkvx_s", [DCTX // 2, 2, 2 * D])
    wo = sb("wo_s", [VW, H, D + 1])
    gate = sb("gate_s", [P, 2, E])
    gate_bias = sb("gate_bias_s", [P, E])
    bo = sb("bo_s", [P, D])
    ln_g, ln_b = sb("ln_g_s", [P, 2]), sb("ln_b_s", [P, 2])
    lx_g, lx_b = sb("lx_g_s", [DCTX // 2, 2]), sb("lx_b_s", [DCTX // 2, 2])
    qk_g = sb("qk_g_s", [P, 2 * DH])
    gam = sb("gam", [P, H, DH])
    ident = sb("ident", [P, P])
    tri = sb("tri", [P, P], BF16)
    ones = sb("ones_b", [P, P], BF16)
    one_row = sb("one_row", [1, P], F32R)
    slot_base = sb("slot_base", [P, E])
    group_no = sb("group_no", [P, G])
    token_id = sb("token_id", [P, TPB])

    K = sb("K", [P, H, NK], F32R)
    Kb = sb("Kb", [VW, H, NK], F32R)
    Kn = sb("Kn", [P, H, NK], F32R)
    V = sb("V", [P, H, NKT, VW])
    Vn = sb("Vn", [P, H, NKT, VW])
    Q = [sb("Q0", [P, H, QW], F32R), sb("Q1", [P, H, QW], F32R)]
    Q1n = sb("Q1n", [P, H, QW], F32R)
    QL = [sb("QL0", [P, H, QT, VW]), sb("QL1", [P, H, QT, VW])]
    QL1n = sb("QL1n", [P, H, QT, VW])
    oT = [sb("oT0", [VW, H, QW]), sb("oT1", [VW, H, QW])]
    qbT = [sb("qbT0", [VW, QW], F32R), sb("qbT1", [VW, QW], F32R)]
    probs = sb("probs", [P, 2, 2, QW])

    xin = sb("xin", [P, TPB, D])
    xctx = sb("xctx", [NCTX, DCTX])
    xres = sb("xres", [P, QT, D])
    mask_u8 = sb("mask_u8", [NCTX, 2], U8)
    mask_bias = sb("mask_bias", [NCTX, 2])
    mask_row8 = sb("mask_row8", [1, 2, NCTX], U8)
    mask_row = sb("mask_row", [1, 2, QT, NCP], F32R)
    bn = sb("bn", [P, NKT, 6])
    mv = sb("mv", [P, NKT, 2])
    st_v, st_y, st_t, st_r = (sb(n, [P, NKT]) for n in ("st_v", "st_y", "st_t", "st_r"))
    st_i = sb("st_i", [P, NKT], U32)
    ln_s, ln_nb = sb("ln_s", [P, NKT]), sb("ln_nb", [P, NKT])
    z = sb("z", [P, 2, D])
    lnT = sb("lnT", [P, 2, 2, P])
    raw = sb("raw", [P, 4, 2 * H, DH])
    sq = sb("sq", [P, 2, 2 * H, DH])
    NR = 2 * 2 * H
    rs_v, rs_y, rs_t = (sb(n, [P, 2, NR]) for n in ("rs_v", "rs_y", "rs_t"))
    rs_i = sb("rs_i", [P, 2, NR], U32)
    st = sb("st", [P, 2, 2 * H, 2 * DH])
    mp = sb("mp", [P, QT, 3])
    mx = sb("mx", [P, QT])
    bnC, mvC = sb("bnC", [P, QT, 6]), sb("mvC", [P, QT, 2])
    c_v, c_y, c_t, c_nb = (sb(n, [P, QT]) for n in ("c_v", "c_y", "c_t", "c_nb"))
    c_i = sb("c_i", [P, QT], U32)
    rden = sb("rden", [P, 1])
    rows = [sb("rows0", [P, QT, ROW]), sb("rows1", [P, QT, ROW])]
    hnT = sb("hnT", [P, 2, 2, P])
    th = sb("th", [P, QT, E])
    sc, sfc, rep, sel, wsel, key = (sb(n, [P, QT, E]) for n in ("sc", "sfc", "rep", "sel", "wsel", "key"))
    g8 = sb("g8", [P, QT, G, 8])
    gs, gmask, pen = (sb(n, [P, QT, G]) for n in ("gs", "gmask", "pen"))
    gm8, v8, k8, adj = (sb(n, [P, QT, 8]) for n in ("gm8", "v8", "k8", "adj"))
    gi = sb("gi", [P, QT, 8], U32)
    gif = sb("gif", [P, QT, 8])
    geq = sb("geq", [P, QT, G, TG])
    selb = sb("selb", [P, QT, E], BF16)
    carry = sb("carry", [P, QT + 1, E], BF16)
    wden = sb("wden", [P, QT])
    slot_idx = [sb("slot_idx0", [P, QT, 8], U32), sb("slot_idx1", [P, QT, 8], U32)]

    ps_s = ctx.enter_context(nc.psum_tensor("ps_s", [P, 2, 2, QW], F32))
    ps_o = ctx.enter_context(nc.psum_tensor("ps_o", [P, QW], F32))
    ps_u = ctx.enter_context(nc.psum_tensor("ps_u", [P, SIDE, 512], F32))

    setup(nc, a, out, slot_rows, s, locals())
    main = locals()
    fresh()
    attend(nc, a, out, slot_rows, odd_sum, s, scattered, filled, main, Plan(False, True, True, False, False), -1)
    fresh()
    with nc.Fori(0, B - 1) as b:
        attend(nc, a, out, slot_rows, odd_sum, s, scattered, filled, main, Plan(True, True, True, True, True), b)
        fresh()
    attend(nc, a, out, slot_rows, odd_sum, s, scattered, filled, main, Plan(True, False, False, True, True), B - 1)
    fresh()


def setup(nc, a, out, slot_rows, s, m):
    with ExitStack() as ctx:
        empty = m["rows"][0][:, 0:2, :]
        ctx.enter_context(nc.allow_non_contiguous_dma(reason="small constants"))
        with nc.Block() as block:
            LOADS = 11

            @block.sync
            def _(sp):
                sp.dma_start(m["xin"][:], a["x"].rearrange("(b t p) d -> b p t d", b=B, p=P)[0]
                             ).then_inc(s["x_loaded"], 16)
                sp.dma_start(m["xctx"][:], a["ctx"][0]).then_inc(s["ctx_loaded"], 16)
                for dst, src in ((m["wqkv"], a["wqkv"]), (m["wkvx"], a["wkvx"]), (m["gate"], a["gate"]),
                                 (m["ln_g"], a["ln_g"]), (m["ln_b"], a["ln_b"]), (m["lx_g"], a["lx_g"]),
                                 (m["lx_b"], a["lx_b"])):
                    sp.dma_start(dst[:], src).then_inc(s["loaded"], 16)
                sp.dma_start(m["gate_bias"][:], a["gate_bias"].to_broadcast([P, E])).then_inc(s["loaded"], 16)
                sp.dma_start(m["bo"][:], a["bo"].to_broadcast([P, D])).then_inc(s["loaded"], 16)
                sp.dma_start(m["qk_g"][:], a["qk_g"].to_broadcast([P, 2 * DH])).then_inc(s["loaded"], 16)
                sp.wait_ge(s["const_made"], 2)
                sp.dma_start(m["wo"][0:DH, :, 0:D], a["wo"]).then_inc(s["loaded"], 16)
                sp.wait_ge(s["loaded"], 16 * LOADS)

            @block.gpsimd
            def _(pool):
                n = 0

                def link(ins):
                    nonlocal n
                    n += 1
                    ins.then_inc(s["pool_step"], 1)
                    pool.wait_ge(s["pool_step"], n)

                link(pool.memset(m["wo"][:], 0.0))
                pool.memset(m["wo"][DH:VW, :, D:D + 1], 1.0).then_inc(s["const_made"], 2)
                pool.wait_ge(s["const_made"], 2)
                link(pool.memset(empty, 0.0))
                link(pool.iota(empty[:, :, D:D + 1], pattern=[[P, 2], [0, 1]], base=NTOK, channel_multiplier=1,
                               allow_small_or_imprecise_dtypes=True))
                link(pool.memset(m["ident"][:], 0.0))
                link(pool.affine_select(out=m["ident"][:], in_=m["ident"][:], compare_op=ALU.not_equal, fill=1.0,
                                        base=0, pattern=[[-1, P]], channel_multiplier=1))
                link(pool.memset(m["ones"][:], 1.0))
                link(pool.affine_select(out=m["tri"][:], in_=m["ones"][:], compare_op=ALU.is_gt, fill=0.0,
                                        base=0, pattern=[[1, P]], channel_multiplier=-1))
                link(pool.iota(m["slot_base"][:], pattern=[[CAP, E]], base=1, channel_multiplier=0,
                               allow_small_or_imprecise_dtypes=True))
                link(pool.iota(m["group_no"][:], pattern=[[1, G]], base=0, channel_multiplier=0,
                               allow_small_or_imprecise_dtypes=True))
                link(pool.iota(m["token_id"][:], pattern=[[P, TPB]], base=0, channel_multiplier=1,
                               allow_small_or_imprecise_dtypes=True))
                link(pool.memset(m["rows"][1][:], 0.0))
                link(pool.memset(m["slot_idx"][1][:], 1 << 20))
                link(pool.memset(m["Kb"][DH:VW, :, :].bitcast(F32), 1.0))
                link(pool.memset(m["Kn"][:, :, NK - 1:NK].bitcast(F32), 0.0))

            @block.vector
            def _(v):
                v.memset(m["one_row"][:].bitcast(F32), 1.0)
                v.memset(m["Vn"][:, :, 0:TPB, DH:VW], 1.0)
                v.memset(m["Vn"][:, :, TPB, :], 1.0)
                v.memset(m["carry"][:], 0.0)
                v.memset(m["QL1n"][:, :, :, DH:VW], 0.0)
                v.memset(m["K"][:, :, NK - 1:NK].bitcast(F32), 0.0)
                v.memset(m["mask_row"][:].bitcast(F32), -BIG)
                n_vec = 0

                def link(ins):
                    nonlocal n_vec
                    n_vec += 1
                    ins.then_inc(s["vec_step"], 1)
                    v.wait_ge(s["vec_step"], n_vec)

                link(v.memset(m["mv"][:], 1.0))
                for piece in range(STATS_PIECES):
                    layernorm_stats(v, link, s, m, piece)
                v.wait_ge(s["loaded"], 16 * LOADS)
                for h in range(H):
                    v.scalar_tensor_tensor(m["gam"][:, h, :], m["qk_g"][:, 0:DH], DH ** -0.5,
                                           m["qk_g"][:, DH:2 * DH], ALU.mult, ALU.mult)


def attend(nc, a, out, slot_rows, odd_sum, s, scattered, filled, m, plan, b):
    K, Kb, Kn, V, Vn, Q, Q1n, QL, QL1n = (m[n] for n in ("K", "Kb", "Kn", "V", "Vn", "Q", "Q1n", "QL", "QL1n"))
    ps_s, ps_o, ps_u, probs, oT, qbT = (m[n] for n in ("ps_s", "ps_o", "ps_u", "probs", "oT", "qbT"))
    ident, lnT, z, st, raw, sq = (m[n] for n in ("ident", "lnT", "z", "st", "raw", "sq"))
    xin, xres, rows, hnT = (m[n] for n in ("xin", "xres", "rows", "hnT"))

    QUAD_SCATTERS = 16 * QT * TOPK

    def unit_owner(u):
        return "vec" if u[0] in ("max", "max_ctx", "proj", "pos") else "act"

    units, steps, blocks = plan.units, plan.steps, plan.blocks
    unit_no = {u: i for i, u in enumerate(units)}
    step_no = {u: i for i, u in enumerate(steps)}
    block_no = {u: i for i, u in enumerate(blocks)}
    neg_no = {u: i for i, u in enumerate([t[1:] for t in plan.tasks if t[0] == "qb"])}
    max_no = {u: i for i, u in enumerate(([(1, 0)] if plan.first else []) + list(neg_no))}
    logit_units = [u for u in units if u[0] == "logits"]

    def bank(u):
        return ps_u[:, unit_no[u] % SIDE, :]

    def wait_full(eng, u):
        eng.wait_ge(s["unit_full"], unit_no[u] + 1)

    def count_empty(u):
        return sum(unit_owner(w) == unit_owner(u) for w in units[:unit_no[u] + 1])

    def wait_empty(eng, u):
        eng.wait_ge(s["emptied_" + unit_owner(u)], count_empty(u))

    def rows_of(j):
        return P if j < TPB else NCTX

    def q_place(j):
        return (Q[0], QL[0], j) if j < QT else (Q1n, QL1n, j - QT)

    x_dram = a["x"].rearrange("(b t p) d -> b p t d", b=B, p=P)
    out_dram = out[0:NTOK, :].rearrange("(b t p) d -> b p t d", b=B, p=P)

    def of_batch(ap, n):
        return ap[n] if isinstance(n, int) else ap[bass.ds(n, 1)][0]

    with nc.Block() as block:
        @block.sync
        def _(sp):
            for use, i, n in ((plan.first, 0, b), (plan.second, 1, b + 1)):
                if use:
                    sp.dma_start(m["mask_u8"][:, i:i + 1], of_batch(a["mask_col"], n)).then_inc(s["mask_loaded"], 16)
                    sp.dma_start(m["mask_row8"][:, i, :], of_batch(a["mask_row"], n)).then_inc(s["mask_loaded"], 16)

            def load_residual(x, n):
                sp.dma_start(xres[:], of_batch(x_dram, n)[:, QT * x:QT * x + QT, :]).then_inc(s["xres_loaded"], 16)

            def fill_slots(half):
                mine = slice(half * E // 2, (half + 1) * E // 2)
                sp.dma_start(slot_rows.rearrange("(e p t) r -> p e (t r)", p=P, t=2)[:, mine, :],
                             rows[0][:, 0:2, :].rearrange("p t r -> p (t r)").unsqueeze(1).to_broadcast(
                                 [P, E // 2, 2 * ROW])).then_inc(filled, 16)

            if plan.keys and not plan.first:
                fill_slots(0)

            def copy_head(h):
                for dst, src in ((K[:, h, :], Kn[:, h, :]), (Kb[0:DH, h, :], Kn[0:DH, h, :]),
                                 (V[:, h, :, :], Vn[:, h, :, :]), (Q[1][:, h, :], Q1n[:, h, :]),
                                 (QL[1][:, h, :, :], QL1n[:, h, :, :])):
                    sp.dma_start(dst.bitcast(F32), src.bitcast(F32)).then_inc(s[f"head_copied{h}"], 16)

            def keys_made():
                wait_empty(sp, ("k_turn", NKT - 1))
                sp.wait_ge(s["lo_made"], (NKT + 1) // 2)

            stored = 0
            for t in plan.tasks:
                if t[0] == "kv_done":
                    keys_made()
                    if not plan.first:
                        for h in range(H):
                            copy_head(h)
                if t[0] == "o_copy" and t[1] == 1 and plan.second:
                    if t[2] == 0:
                        keys_made()
                    sp.wait_ge(s["values_done"], len(STEPS) * (block_no[t[1:]] + 1))
                    copy_head(t[2])
                if t[0] == "store":
                    stored += 1
                    x = t[1]
                    wait_empty(sp, ("proj", x, QT - 1, H - 1))
                    sp.dma_start(of_batch(out_dram, b)[:, QT * x:QT * x + QT, :], xres[:]).then_inc(s["x2_stored"], 16)
                if t == ("logits", 0, QT - 1):
                    sp.wait_ge(s["x2_stored"], 16)
                    sp.wait_ge(s["hn_made"], QT)
                    load_residual(1, b)
                if t[0] == "residual_next":
                    if plan.second:
                        if stored:
                            sp.wait_ge(s["x2_stored"], 16 * stored)
                            sp.wait_ge(s["hn_made"], 2 * QT)
                        load_residual(0, b + 1)
                if t[0] == "x_next":
                    sp.wait_ge(s["z_made"], NKT)
                    after = (b + 2) % B
                    sp.dma_start(xin[:], of_batch(x_dram, after)).then_inc(s["x_loaded"], 16)
                    sp.dma_start(m["xctx"][:], of_batch(a["ctx"], after)).then_inc(s["ctx_loaded"], 16)
            if stored:
                sp.wait_ge(s["x2_stored"], 16 * stored)
            if plan.keys and not plan.first:
                fill_slots(1)
                zero = rows[1][:, 0:2, 0:D]
                sp.dma_start(out[NTOK:NTOK + DUMP, :].rearrange("(p t) d -> p t d", t=2), zero).then_inc(filled, 16)
                sp.dma_start(odd_sum.rearrange("(p t) d -> p t d", p=P),
                             rows[1][:, 0:1, 0:D].to_broadcast([P, (NTOK + DUMP) // P, D])).then_inc(filled, 16)

        @block.gpsimd
        def _(pool):
            n = 0

            def add_bias(x):
                pool.wait_ge(s["xres_loaded"], 16 * (x + 1))
                for j in range(QT):
                    pool.tensor_tensor(xres[:, j, :], xres[:, j, :], m["bo"][:], ALU.add).then_inc(s["xres_based"], 1)
                    pool.wait_ge(s["xres_based"], QT * x + j + 1)

            def scatter(x, first, end):
                for q in range(first, end):
                    for k in range(TOPK):
                        pool.indirect_dma_start(
                            out=slot_rows, out_offset=bass.IndirectOffsetOnAxis(
                                ap=m["slot_idx"][x][:, q, k:k + 1], axis=0),
                            in_=rows[x][:, q, :], in_offset=None, bounds_check=E * CAP - 1,
                            oob_is_err=False).then_inc(scattered, 16)

            if plan.route0:
                pool.wait_ge(filled, 16 * FILLS)
                scatter(1, 0, QT)
                pool.wait_ge(scattered, b * (2 * QUAD_SCATTERS) + QUAD_SCATTERS)
                pool.sem_inc(s["rows_free"], 1)
            for t in plan.tasks:
                if t[0] == "scatter" and (t[1] == 0 or not plan.second):
                    n += 1
                    pool.wait_ge(s["slots_made"], n)
                    pool.wait_ge(s["rows_made"], n)
                    pool.wait_ge(s["hn_made"], QT * (t[1] + 1 if plan.route0 else 1))
                    scatter(*t[1:])
                if t == ("logits", 0, QT - 1):
                    add_bias(0)
                if t[0] == "residual_next" and plan.second:
                    add_bias(1 if plan.first else 0)

        @block.tensor
        def _(pe):
            def free_bank(u):
                if unit_no[u] >= SIDE:
                    wait_empty(pe, units[unit_no[u] - SIDE])

            for t in plan.tasks:
                kind = t[0]
                if t in unit_no:
                    free_bank(t)
                if kind == "ln_turn":
                    j = t[1]
                    w, rj = (P, rows_of(j)) if j < TPB else (DCTX // 2, NCTX)
                    pe.wait_ge(s["z_made"], j + 1)
                    for c in range(2):
                        i = pe.transpose(bank(t)[0:w, c * P:c * P + rj], z[0:rj, j % 2, c * w:(c + 1) * w],
                                         ident[0:rj, 0:rj])
                    i.then_inc(s["unit_full"], 1)
                elif kind in ("qk", "v"):
                    j = t[1]
                    rj = rows_of(j)
                    wait_empty(pe, ("ln_turn", j))
                    w = P if j < TPB else DCTX // 2
                    if kind == "qk":
                        dst = bank(t)[0:rj, 0:2 * D] if j < TPB else bank(t)[0:rj, D:2 * D]
                    else:
                        dst = bank(t)[0:rj, 0:D]
                    for c in range(2):
                        if j < TPB:
                            rhs = m["wqkv"][:, c, 0:2 * D] if kind == "qk" else m["wqkv"][:, c, 2 * D:3 * D]
                        else:
                            rhs = m["wkvx"][:, c, 0:D] if kind == "qk" else m["wkvx"][:, c, D:2 * D]
                        i = pe.matmul(dst, lnT[0:w, j % 2, c, 0:rj], rhs, start=(c == 0), stop=(c == 1))
                    i.then_inc(s["unit_full"], 1)
                elif kind in ("q_turn", "k_turn"):
                    j = t[1]
                    rj = rows_of(j)
                    pair = j // 2
                    pe.wait_ge(s["hi_made"], pair + 1)
                    pe.wait_ge(s["lo_made"], pair + 1)
                    h0 = 0 if kind == "q_turn" else H
                    for h in range(H):
                        i = pe.transpose(bank(t)[:, h * P:h * P + rj], st[0:rj, j % 2, h0 + h, :], ident[0:rj, 0:rj])
                    i.then_inc(s["unit_full"], 1)
                elif kind in ("max", "max_ctx", "qb"):
                    x, h = t[1:3]
                    keys, quad = (Kn, 0) if x == 0 else (K, 1)
                    ctx = 0 if x == 1 else 1
                    if x == 2:
                        pe.wait_ge(s["head_copied0"], 16 * 5)
                    if x == 0:
                        wait_empty(pe, ("k_turn", NKT - 1))
                    if kind == "max":
                        tile, half = t[3:5]
                        i = pe.matmul(bank(t)[:, :], Q[quad][:, h, tile * P:(tile + 1) * P],
                                      keys[:, h, half * 512:(half + 1) * 512], start=True, stop=True)
                    elif kind == "max_ctx":
                        pe.wait_ge(s["mask_made"], 4 if plan.first and plan.second else 2)
                        pe.matmul(bank(t)[:, 0:QT * NCP], m["one_row"][:],
                                  m["mask_row"][:, ctx, :, :].rearrange("o q k -> o (q k)"), start=True, stop=False,
                                  skip_group_check=True)
                        for tile in range(QT):
                            i = pe.matmul(bank(t)[:, tile * NCP:(tile + 1) * NCP],
                                          Q[quad][:, h, tile * P:(tile + 1) * P], keys[:, h, S:NK],
                                          start=False, stop=(tile == QT - 1), skip_group_check=True)
                    else:
                        pe.wait_ge(s["neg_made"], neg_no[(x, h)] + 1)
                        for tile in range(QT):
                            i = pe.transpose(bank(t)[0:VW, tile * P:(tile + 1) * P], QL[quad][:, h, tile, :], ident[:])
                    i.then_inc(s["unit_full"], 1)
                elif kind == "scores":
                    x, h, st_ = t[1:]
                    n = step_no[t[1:]]
                    if (x, h) in neg_no:
                        wait_empty(pe, ("qb", x, h))
                    if x == 0:
                        pe.wait_ge(s[f"head_copied{h}"], 16 * 5)
                    if n >= 2:
                        pe.wait_ge(s["probs_made"], n - 1)
                    for i_kt, kt in enumerate(STEPS[st_]):
                        rk = rows_of(kt)
                        dst = ps_s[0:rk, n % 2, i_kt, :]
                        pe.matmul(dst, K[:, h, kt * P:kt * P + rk], Q[x][:, h, :], start=True, stop=False)
                        i = pe.matmul(dst, Kb[:, h, kt * P:kt * P + rk], qbT[max_no[(x, h)] % 2][:],
                                      start=False, stop=True)
                    i.then_inc(s["scores_full"], 1)
                elif kind == "values":
                    x, h, st_ = t[1:]
                    n = step_no[t[1:]]
                    pe.wait_ge(s["probs_made"], n + 1)
                    if st_ == 0 and block_no[(x, h)] >= 1:
                        pe.wait_ge(s["o_copied"], block_no[(x, h)])
                    for i_kt, kt in enumerate(STEPS[st_]):
                        rk = rows_of(kt)
                        i = pe.matmul(ps_o[0:VW, :], V[0:rk, h, kt, :], probs[0:rk, n % 2, i_kt, :],
                                      start=(kt == 0), stop=(kt == NKT - 1))
                    i.then_inc(s["values_done"], 1)
                elif kind == "proj":
                    x, tile, h = t[1:]
                    if x == 1:
                        pe.wait_ge(s["o_copied"], h + 1)
                    i = pe.matmul(bank(t)[:, 0:D + 1], oT[x][:, h, tile * P:(tile + 1) * P], m["wo"][:, h, :],
                                  start=True, stop=True)
                    i.then_inc(s["unit_full"], 1)
                elif kind == "hn_turn":
                    x, tile = t[1:]
                    n = [u for u in units if u[0] == "hn_turn"].index(t)
                    pe.wait_ge(s["hn_made"], n + 1)
                    for c in range(2):
                        i = pe.transpose(bank(t)[:, c * P:(c + 1) * P], rows[x][:, tile, c * P:(c + 1) * P], ident[:])
                    i.then_inc(s["unit_full"], 1)
                elif kind == "logits":
                    n = logit_units.index(t)
                    wait_empty(pe, ("hn_turn",) + t[1:])
                    for c in range(2):
                        i = pe.matmul(bank(t)[:, 0:E], hnT[:, n % 2, c, :], m["gate"][:, c, :],
                                      start=(c == 0), stop=(c == 1))
                    i.then_inc(s["unit_full"], 1)
                elif kind == "pos":
                    n = [u for u in units if u[0] == "pos"].index(t)
                    pe.wait_ge(s["sel_made"], n + 1)
                    first, end = t[2:]
                    for tile in range(first, end):
                        dst = bank(t)[:, tile * E:(tile + 1) * E]
                        pe.matmul(dst, m["tri"][:], m["selb"][:, tile, :], start=(tile == first), stop=False,
                                  skip_group_check=True)
                        i = pe.matmul(dst, m["ones"][:], m["carry"][:, tile, :], start=False, stop=(tile == end - 1),
                                      skip_group_check=True)
                    i.then_inc(s["unit_full"], 1)

        @block.scalar
        def _(act):
            for t in plan.tasks:
                kind = t[0]
                if kind in ("ln_turn", "qk", "v", "q_turn", "k_turn", "qb", "hn_turn", "logits"):
                    wait_full(act, t)
                if kind == "z":
                    j = t[1]
                    rj, w = rows_of(j), (D if j < TPB else DCTX)
                    if j >= 2:
                        wait_full(act, ("ln_turn", j - 2))
                    src = xin[:, j, :] if j < TPB else m["xctx"][:]
                    act.activation(z[0:rj, j % 2, 0:w], src, ACT.Identity, scale=m["ln_s"][0:rj, j:j + 1],
                                   bias=m["ln_nb"][0:rj, j:j + 1]).then_inc(s["z_made"], 1)
                elif kind == "ln_turn":
                    j = t[1]
                    rj = rows_of(j)
                    w = P if j < TPB else DCTX // 2
                    g_, b_ = (m["ln_g"], m["ln_b"]) if j < TPB else (m["lx_g"], m["lx_b"])
                    if j >= 2:
                        wait_full(act, ("v", j - 2))
                    for c in range(2):
                        i = act.activation(lnT[0:w, j % 2, c, 0:rj], bank(t)[0:w, c * P:c * P + rj], ACT.Identity,
                                           scale=g_[:, c:c + 1], bias=b_[:, c:c + 1])
                    i.then_inc(s["emptied_act"], 1)
                elif kind == "qk":
                    j = t[1]
                    rj = rows_of(j)
                    h0 = 0 if j < TPB else H
                    if j >= 4:
                        act.wait_ge(s["lo_made"], (j - 4) // 2 + 1)
                    if j >= 2:
                        act.wait_ge(s["summed"], j - 1)
                    src = bank(t)[0:rj, h0 * DH:2 * D]
                    act.activation(raw[0:rj, j % 4, h0:2 * H, :], src, ACT.Copy)
                    act.activation(sq[0:rj, j % 2, h0:2 * H, :], src, ACT.Square).then_inc(s["emptied_act"], 1)
                elif kind == "v":
                    j = t[1]
                    rj = rows_of(j)
                    act.activation(Vn[0:rj, :, j, 0:DH], bank(t)[0:rj, 0:D].rearrange("p (h d) -> p h d", h=H),
                                   ACT.Copy).then_inc(s["emptied_act"], 1)
                elif kind == "hi":
                    pair = t[1]
                    n = min(2, NKT - 2 * pair)
                    act.wait_ge(s["normed"], pair + 1)
                    if pair >= 1:
                        wait_full(act, ("k_turn", 2 * pair - 1))
                    a0 = 2 * (pair % 2)
                    act.activation(st[:, 0:n, :, 0:DH].bitcast(F32R), raw[:, a0:a0 + n, :, :], ACT.Copy)
                    act.activation(st[:, 0:n, 0:H, DH:2 * DH].bitcast(F32R), raw[:, a0:a0 + n, 0:H, :], ACT.Copy
                                   ).then_inc(s["hi_made"], 1)
                elif kind == "q_turn":
                    j = t[1]
                    dst, _, at = q_place(j)
                    i = act.activation(dst[:, :, at * P:(at + 1) * P], bank(t).rearrange("p (h q) -> p h q", h=H),
                                       ACT.Copy)
                    i.then_inc(s["emptied_act"], 1)
                elif kind == "k_turn":
                    j = t[1]
                    rj = rows_of(j)
                    i = act.activation(Kn[:, :, j * P:j * P + rj],
                                       bank(t).rearrange("p (h q) -> p h q", h=H)[:, :, 0:rj], ACT.Copy)
                    i.then_inc(s["emptied_act"], 1)
                elif kind == "qb":
                    x, h = t[1:]
                    n = max_no[(x, h)]
                    if n >= 2:
                        act.wait_ge(s["scores_full"], step_no[blocks[n - 2] + (len(STEPS) - 1,)] + 1)
                    act.activation(qbT[n % 2][:], bank(t)[0:VW, :], ACT.Copy).then_inc(s["emptied_act"], 1)
                elif kind == "scores":
                    x, h, st_ = t[1:]
                    n = step_no[t[1:]]
                    act.wait_ge(s["scores_full"], n + 1)
                    if n >= 2:
                        act.wait_ge(s["values_done"], n - 1)
                    if len(STEPS[st_]) == 2:
                        act.activation(probs[:, n % 2, :, :], ps_s[:, n % 2, :, :], ACT.Exp
                                       ).then_inc(s["probs_made"], 1)
                    else:
                        act.wait_ge(s["mask_made"], 4 if plan.first and plan.second else 2)
                        act.activation(probs[0:NCTX, n % 2, 0, :], ps_s[0:NCTX, n % 2, 0, :], ACT.Exp,
                                       bias=m["mask_bias"][:, 1 - x:2 - x]).then_inc(s["probs_made"], 1)
                elif kind == "o_copy":
                    x, h = t[1:]
                    n = block_no[(x, h)]
                    act.wait_ge(s["values_done"], len(STEPS) * (n + 1))
                    act.activation(oT[x][:, h, :], ps_o[0:VW, :], ACT.Copy).then_inc(s["o_copied"], 1)
                elif kind == "hn":
                    x, tile = t[1:]
                    n = [u[1] for u in plan.tasks if u[0] == "hn_scale" and u[2] == 3].index(x) + 1
                    act.wait_ge(s["hn_scaled"], n)
                    if x == 0:
                        act.wait_ge(filled, 16 * FILLS)
                    if x == 1 and plan.route0:
                        act.wait_ge(s["rows_free"], 1)
                    act.activation(rows[x][:, tile, 0:D], xres[:, tile, :], ACT.Identity,
                                   scale=m["c_y"][:, tile:tile + 1], bias=m["c_nb"][:, tile:tile + 1]
                                   ).then_inc(s["hn_made"], 1)
                elif kind == "hn_turn":
                    n = [u for u in units if u[0] == "hn_turn"].index(t)
                    if n >= 2:
                        wait_full(act, logit_units[n - 2])
                    act.activation(hnT[:, n % 2, :, :], bank(t)[:, 0:2 * P].rearrange("p (c q) -> p c q", c=2),
                                   ACT.Copy).then_inc(s["emptied_act"], 1)
                elif kind == "logits":
                    x, tile = t[1:]
                    n = logit_units.index(t)
                    if tile == 0 and n:
                        act.wait_ge(s["sel_made"], n // QT)
                    act.activation(m["th"][:, tile, :], bank(t)[:, 0:E], ACT.Tanh, scale=0.5
                                   ).then_inc(s["emptied_act"], 1)

        @block.vector
        def _(v):
            n_vec = 0

            def link(ins):
                nonlocal n_vec
                n_vec += 1
                ins.then_inc(s["vec_step"], 1)
                v.wait_ge(s["vec_step"], n_vec)

            made = 0
            for use, i in ((plan.first, 0), (plan.second, 1)):
                if use:
                    v.wait_ge(s["mask_loaded"], 64 if plan.first and plan.second else 32)
                    v.tensor_scalar(m["mask_bias"][:, i:i + 1], m["mask_u8"][:, i:i + 1], BIG, -BIG, ALU.mult,
                                    ALU.add).then_inc(s["mask_made"], 1)
                    v.tensor_scalar(m["mask_row"][:, i, :, 0:NCTX],
                                    m["mask_row8"][:, i, :].unsqueeze(1).to_broadcast([1, QT, NCTX]), BIG, -BIG,
                                    ALU.mult, ALU.add).then_inc(s["mask_made"], 1)

            n_part = 0
            for t in plan.tasks:
                kind = t[0]
                if kind in ("max", "max_ctx", "proj", "pos"):
                    wait_full(v, t)
                if kind in CHOICE:
                    x = t[1]
                    tiles = slice(*t[2:]) if kind != "group_sums" else slice(t[2], t[2] + 1)
                    n_tiles = tiles.stop - tiles.start
                    sc, sfc, sel, rep, key, wsel = (m[k][:, tiles, :] for k in
                                                    ("sc", "sfc", "sel", "rep", "key", "wsel"))
                    wden = m["wden"][:, tiles]
                if kind == "stats":
                    layernorm_stats(v, link, s, m, t[1])
                elif kind == "v":
                    j = t[1]
                    wait_empty(v, ("qk", j))
                    at = 2 * H * (j % 2)
                    v.tensor_reduce(m["rs_v"][:, j // 2 % 2, at:at + 2 * H], sq[:, j % 2, :, :], AX.X, ALU.add
                                    ).then_inc(s["summed"], 1)
                elif kind in ("rs", "norm", "norm_q", "lo"):
                    pair = t[1]
                    n = min(2, NKT - 2 * pair)
                    nr = n * 2 * H
                    r, y, half, shifted = (m[k][:, pair % 2, 0:nr] for k in ("rs_v", "rs_y", "rs_t", "rs_i"))
                    a0 = 2 * (pair % 2)
                    if kind == "rs":
                        if t[2] == 0:
                            v.wait_ge(s["summed"], min(2 * pair + 2, NKT))
                            link(v.tensor_scalar(r, r, 1.0 / DH, RMS_EPS ** 2, ALU.mult, ALU.max))
                        rsqrt(v, link, r, shifted, y, half, t[2:])
                    elif kind == "norm":
                        flat = raw[:, a0:a0 + n, :, :].rearrange("p a h d -> p (a h) d")
                        link(v.tensor_tensor(flat, flat, y.unsqueeze(2).to_broadcast([P, nr, DH]), ALU.mult))
                    elif kind == "norm_q":
                        mine = raw[:, a0:a0 + n, 0:H, :]
                        v.tensor_tensor(mine, mine, m["gam"][:].unsqueeze(1).to_broadcast([P, n, H, DH]), ALU.mult
                                        ).then_inc(s["normed"], 1)
                    else:
                        v.wait_ge(s["hi_made"], pair + 1)
                        if 2 * pair < TPB:
                            _, ql, at = q_place(2 * pair)
                            for i in range(2):
                                v.tensor_tensor(ql[:, :, at + i, 0:DH], raw[:, a0 + i, 0:H, :], st[:, i, 0:H, 0:DH],
                                                ALU.subtract)
                        v.tensor_tensor(st[:, 0:n, H:2 * H, DH:2 * DH], raw[:, a0:a0 + n, H:2 * H, :],
                                        st[:, 0:n, H:2 * H, 0:DH], ALU.subtract).then_inc(s["lo_made"], 1)
                elif kind == "max":
                    x, h, tile, half = t[1:]
                    v.tensor_reduce(m["mp"][:, tile, half:half + 1], bank(t)[:, :], AX.X, ALU.max
                                    ).then_inc(s["emptied_vec"], 1)
                elif kind == "max_ctx":
                    v.tensor_reduce(m["mp"][:, :, 2:3], bank(t)[:, 0:QT * NCP].rearrange("p (q k) -> p q k", q=QT),
                                    AX.X, ALU.max).then_inc(s["emptied_vec"], 1)
                elif kind == "neg":
                    x, h = t[1:]
                    wait_empty(v, ("max_ctx", x, h))
                    link(v.tensor_reduce(m["mx"][:], m["mp"][:], AX.X, ALU.max))
                    v.tensor_scalar(QL[1 if x else 0][:, h, :, DH:VW], m["mx"][:].unsqueeze(2), -1.0, None, ALU.mult
                                    ).then_inc(s["neg_made"], 1)
                elif kind == "proj":
                    x, tile, h = t[1:]
                    if x == 1:
                        v.wait_ge(s["xres_based"], tile + 1)
                    link(v.reciprocal(m["rden"][:], bank(t)[:, D:D + 1]))
                    i = v.scalar_tensor_tensor(xres[:, tile, :], bank(t)[:, 0:D], m["rden"][:], xres[:, tile, :],
                                               ALU.mult, ALU.add)
                    i.then_inc(s["emptied_vec"], 1)
                    wait_empty(v, t)
                    if h == H - 1:
                        link(v.bn_stats(m["bnC"][:, tile, :], xres[:, tile, :]))
                        link(v.bn_aggr(m["mvC"][:, tile, :], m["bnC"][:, tile, :]))
                elif kind == "hn_scale":
                    if t[2] == 0:
                        if n_part:
                            v.wait_ge(s["hn_made"], QT)
                        link(v.tensor_scalar(m["c_v"][:], m["mvC"][:, :, 1], LN_EPS, None, ALU.add))
                    rsqrt(v, link, m["c_v"][:], m["c_i"][:], m["c_y"][:], m["c_t"][:], t[2:])
                    if t[2] == 3:
                        v.scalar_tensor_tensor(m["c_nb"][:], m["mvC"][:, :, 0], -1.0, m["c_y"][:], ALU.mult, ALU.mult
                                               ).then_inc(s["hn_scaled"], 1)
                elif kind == "gates":
                    n_part += 1
                    if x == 1 and plan.route0:
                        v.wait_ge(s["rows_free"], 1)
                    wait_empty(v, ("logits", x, tiles.stop - 1))
                    link(v.tensor_scalar(sc, m["th"][:, tiles, :], 1.0, 0.5, ALU.add, ALU.mult))
                    link(v.tensor_tensor(sfc, sc, m["gate_bias"][:].unsqueeze(1).to_broadcast([P, n_tiles, E]),
                                         ALU.add))
                elif kind == "group_sums":
                    for g in range(G):
                        i = v.max(m["g8"][:, t[2], g, :], m["sfc"][:, t[2], g * EG:(g + 1) * EG])
                    link(i)
                elif kind == "groups":
                    link(v.tensor_tensor(m["gs"][:, tiles, :], m["g8"][:, tiles, :, 0], m["g8"][:, tiles, :, 1],
                                         ALU.add))
                    for q in range(*t[2:]):
                        i = v.max(m["gm8"][:, q, :], m["gs"][:, q, :])
                    link(i)
                elif kind == "group_ids":
                    for q in range(*t[2:]):
                        i = v.max_index(m["gi"][:, q, :], m["gm8"][:, q, :], m["gs"][:, q, :])
                    link(i)
                    link(v.tensor_copy(m["gif"][:, tiles, :], m["gi"][:, tiles, :]))
                elif kind == "mask_groups":
                    for q in range(*t[2:]):
                        i = v.tensor_tensor(m["geq"][:, q, :, :],
                                            m["group_no"][:].unsqueeze(2).to_broadcast([P, G, TG]),
                                            m["gif"][:, q, 0:TG].unsqueeze(1).to_broadcast([P, G, TG]), ALU.is_equal)
                    link(i)
                    link(v.tensor_reduce(m["gmask"][:, tiles, :], m["geq"][:, tiles, :, :], AX.X, ALU.add))
                    link(v.tensor_scalar(m["pen"][:, tiles, :], m["gmask"][:, tiles, :], BIG, -BIG, ALU.mult, ALU.add))
                elif kind == "bar_groups":
                    by_group = sfc.rearrange("p q (g e) -> p q g e", g=G)
                    link(v.tensor_tensor(by_group, by_group, m["gmask"][:, tiles, :].unsqueeze(3).to_broadcast(
                        [P, n_tiles, G, EG]), ALU.mult))
                    link(v.tensor_tensor(by_group, by_group, m["pen"][:, tiles, :].unsqueeze(3).to_broadcast(
                        [P, n_tiles, G, EG]), ALU.add))
                elif kind == "best":
                    for q in range(*t[2:]):
                        i = v.max(m["v8"][:, q, :], m["sfc"][:, q, :])
                    link(i)
                elif kind == "replace":
                    for q in range(*t[2:]):
                        i = v.match_replace(m["rep"][:, q, :], m["v8"][:, q, :], m["sfc"][:, q, :], -3e38)
                    link(i)
                elif kind == "chosen":
                    link(v.tensor_tensor(sel, rep, sfc, ALU.not_equal))
                    link(v.tensor_copy(m["selb"][:, tiles, :], sel))
                elif kind == "count":
                    for q in range(*t[2:]):
                        i = v.tensor_tensor(m["carry"][:, q + 1, :], m["carry"][:, q, :], m["selb"][:, q, :], ALU.add)
                        if q < tiles.stop - 1:
                            link(i)
                    i.then_inc(s["sel_made"], 1)
                elif kind == "pos":
                    pos = bank(t).rearrange("p (q e) -> p q e", e=E)[:, tiles, :]
                    link(v.tensor_tensor(key, pos, m["slot_base"][:].unsqueeze(1).to_broadcast([P, n_tiles, E]),
                                         ALU.add))
                    v.scalar_tensor_tensor(rep, pos, float(CAP), sel, ALU.is_lt, ALU.mult
                                           ).then_inc(s["emptied_vec"], 1)
                elif kind == "slots":
                    wait_empty(v, ("pos", *t[1:]))
                    v.wait_ge(s["sel_made"], n_part)
                    if tiles.stop == QT:
                        link(v.tensor_copy(m["carry"][:, 0, :], m["carry"][:, QT, :]))
                    link(v.tensor_tensor(key, key, rep, ALU.mult))
                    for q in range(*t[2:]):
                        i = v.max(m["k8"][:, q, :], m["key"][:, q, :])
                    link(i)
                elif kind == "slot_ids":
                    link(v.tensor_scalar(m["adj"][:, tiles, :], m["k8"][:, tiles, :], 0.0, 1e6, ALU.is_equal, ALU.mult))
                    v.scalar_tensor_tensor(m["slot_idx"][x][:, tiles, :], m["k8"][:, tiles, :], -1.0,
                                           m["adj"][:, tiles, :], ALU.add, ALU.add).then_inc(s["slots_made"], 1)
                elif kind == "weights":
                    link(v.tensor_tensor(wsel, sc, sel, ALU.mult))
                    link(v.tensor_reduce(wden, wsel, AX.X, ALU.add))
                    link(v.tensor_scalar(wden, wden, 1e-20, None, ALU.add))
                    link(v.reciprocal(wden, wden))
                elif kind == "scale_weights":
                    link(v.tensor_tensor(wsel, wsel, wden.unsqueeze(2).to_broadcast([P, n_tiles, E]), ALU.mult))
                    link(v.tensor_scalar(rows[x][:, tiles, D + 1:ROW], wsel, ROUTE_SCALE, None, ALU.mult))
                    ids = slice(QT * x + tiles.start, QT * x + tiles.stop)
                    v.tensor_copy(rows[x][:, tiles, D:D + 1], m["token_id"][:, ids].unsqueeze(2)
                                  ).then_inc(s["rows_made"], 1)
                    if x == 1 and tiles.stop == QT:
                        v.wait_ge(s["rows_made"], n_part)
                        link(v.tensor_scalar(m["token_id"][:], m["token_id"][:], float(S), None, ALU.add))


def phase2(nc, a, out, slot_rows, odd_sum, s, added, fresh, ctx):
    def sb(name, shape, dt=F32):
        return ctx.enter_context(nc.sbuf_tensor(name, shape, dt))

    START = RING
    w = sb("w_exp", [P, RING, 3 * D])
    xr = sb("x_rows", [P, RING, 2, ROW])
    xT = sb("xT", [P, 2, 2, CAP])
    silu = sb("silu", [P, 2, CAP])
    hid = sb("hid", [P, 2, CAP])
    y = sb("y", [P, RING, 2, D])
    ids = sb("ids", [P, RING, 2], U32)
    ident = sb("ident2", [P, P])
    ps_x = ctx.enter_context(nc.psum_tensor("ps_x", [P, 2, 2, CAP], F32))
    ps_g = ctx.enter_context(nc.psum_tensor("ps_g", [P, 2, 2, CAP], F32))
    ps_y = ctx.enter_context(nc.psum_tensor("ps_y", [P, 2, 2, D], F32))
    rows_dram = slot_rows.rearrange("(e p t) r -> e p t r", p=P, t=2)
    PASSES = E // RING - 1

    def steps(eng, first, step):
        with eng.Fori(0, PASSES) as it:
            for r in range(RING):
                step(first + r, it)
        for c in range(first + RING * PASSES, E):
            step(c, 0)

    def at(c, it, n=0, k=1):
        return k * (c + n) + (it * (k * RING) if not isinstance(it, int) else 0)

    with nc.Block() as block:
        @block.sync
        def _(sp):
            def load(c, it):
                r = c % RING
                e = at(c, it)
                sp.dma_start(w[:, r, :], a["wexp"][e] if isinstance(e, int) else a["wexp"][bass.ds(e, 1)][0]
                             ).then_inc(s[f"w_loaded{r}"], 16)
                sp.dma_start(xr[:, r, :, :], rows_dram[e] if isinstance(e, int) else rows_dram[bass.ds(e, 1)][0]
                             ).then_inc(s[f"x_in{r}"], 16)

            def reload(c, it):
                sp.wait_ge(s["y_full"], at(c, it, 1 - RING + START))
                sp.wait_ge(s["y_made"], at(c, it, 1 - RING + START))
                load(c, it)

            for c in range(RING):
                load(c, 0)
            steps(sp, RING, reload)

        @block.tensor
        def _(pe):
            def turn(c, it):
                pe.wait_ge(s[f"x_in{c % RING}"], 16 * (c // RING + 1) + (it * 16 if not isinstance(it, int) else 0))
                pe.wait_ge(s["turned_copied"], at(c, it, START - 1))
                for k in range(2):
                    for t in range(2):
                        i = pe.transpose(ps_x[:, c % 2, k, t * P:(t + 1) * P],
                                         xr[:, c % RING, t, k * P:(k + 1) * P], ident[:])
                i.then_inc(s["rows_turned"], 1)

            def gate_up(c, it):
                pe.wait_ge(s[f"w_loaded{c % RING}"], 16 * (c // RING + 1) + (it * 16 if not isinstance(it, int) else 0))
                pe.wait_ge(s["turned_copied"], at(c, it, START + 1))
                pe.wait_ge(s["h_made"], at(c, it, START - 1))
                for part in range(2):
                    for k in range(2):
                        o = (2 * part + k) * I
                        i = pe.matmul(ps_g[:, c % 2, part, :], w[:, c % RING, o:o + I], xT[:, c % 2, k, :],
                                      start=(k == 0), stop=(k == 1))
                i.then_inc(s["gate_up"], 1)

            def down(c, it):
                pe.wait_ge(s["h_made"], at(c, it, START + 1))
                pe.wait_ge(s["y_made"], at(c, it, START - 1))
                for t in range(2):
                    i = pe.matmul(ps_y[:, c % 2, t, :], hid[:, c % 2, t * P:(t + 1) * P],
                                  w[:, c % RING, 4 * I:4 * I + D], start=True, stop=True)
                i.then_inc(s["y_full"], 1)

            pe.sem_inc(s["gate_up"], START)
            pe.sem_inc(s["y_full"], START)
            pe.wait_ge(s["const_made"], 1)
            turn(0, 0)
            turn(1, 0)
            gate_up(0, 0)

            def step(c, it):
                if c < E - 1:
                    turn(c + 1, it)
                gate_up(c, it)
                down(c - 1, it)

            steps(pe, 1, step)
            down(E - 1, 0)

        @block.scalar
        def _(act):
            def copy(c, it):
                act.wait_ge(s["rows_turned"], at(c, it, 1))
                act.wait_ge(s["gate_up"], at(c, it, START - 1))
                act.activation(xT[:, c % 2, :, :], ps_x[:, c % 2, :, :], ACT.Copy).then_inc(s["turned_copied"], 1)

            def gate(c, it):
                act.wait_ge(s["gate_up"], at(c, it, START + 1))
                act.wait_ge(s["h_made"], at(c, it, START - 1))
                act.activation(silu[:, c % 2, :], ps_g[:, c % 2, 0, :], ACT.Silu).then_inc(s["silu_made"], 1)

            act.sem_inc(s["turned_copied"], START)
            copy(0, 0)
            copy(1, 0)
            gate(0, 0)

            def step(c, it):
                if c < E - 1:
                    copy(c + 1, it)
                gate(c, it)

            steps(act, 1, step)

        @block.vector
        def _(v):
            def hidden(c, it):
                v.wait_ge(s["silu_made"], at(c, it, 1))
                v.wait_ge(s["y_full"], at(c, it, START - 1))
                v.tensor_tensor(hid[:, c % 2, :], silu[:, c % 2, :], ps_g[:, c % 2, 1, :], ALU.mult
                                ).then_inc(s["h_made"], 1)

            def weigh(c, it):
                r = c % RING
                v.wait_ge(s["y_full"], at(c, it, START + 1))
                v.wait_ge(s["add_done"], at(c, it, START - RING + 1))
                for t in range(2):
                    col = at(c, it, D + 1)
                    v.tensor_scalar(y[:, r, t, :], ps_y[:, c % 2, t, :],
                                    xr[:, r, t, col:col + 1] if isinstance(col, int) else xr[:, r, t, bass.ds(col, 1)],
                                    None, ALU.mult)
                v.tensor_copy(ids[:, r, :].unsqueeze(2), xr[:, r, :, D:D + 1]).then_inc(s["y_made"], 1)

            v.sem_inc(s["h_made"], START)
            v.sem_inc(s["y_made"], START)
            hidden(0, 0)

            def step(c, it):
                hidden(c, it)
                weigh(c - 1, it)

            steps(v, 1, step)
            weigh(E - 1, 0)

        @block.gpsimd
        def _(pool):
            def add(c, it):
                r = c % RING
                for t in range(2):
                    pool.indirect_dma_start(
                        out=(out, odd_sum)[c % 2], out_offset=bass.IndirectOffsetOnAxis(ap=ids[:, r, t:t + 1], axis=0),
                        in_=y[:, r, t, :], in_offset=None, bounds_check=NTOK + DUMP - 1, oob_is_err=True,
                        compute_op=ALU.add).then_inc(added[c % 2], 16)

            def step(c, it):
                pool.wait_ge(s["y_made"], at(c, it, START + 1))
                pool.wait_ge(added[c % 2], 32 * (c // 2) + (it * (16 * RING) if not isinstance(it, int) else 0))
                pool.sem_inc(s["add_done"], 1)
                add(c, it)

            pool.memset(ident[:], 0.0).then_inc(s["pool_step"], 1)
            pool.wait_ge(s["pool_step"], 1)
            pool.affine_select(out=ident[:], in_=ident[:], compare_op=ALU.not_equal, fill=1.0,
                               base=0, pattern=[[-1, P]], channel_multiplier=1).then_inc(s["const_made"], 1)
            pool.sem_inc(s["add_done"], START)
            for c in range(2):
                pool.wait_ge(s["y_made"], at(c, 0, START + 1))
                add(c, 0)
            steps(pool, 2, step)
            for parity in range(2):
                pool.wait_ge(added[parity], 16 * E)
    fresh()
    join(nc, out, odd_sum, s, ctx)


def join(nc, out, odd_sum, s, ctx):
    PARTS, BUFS, T = 8, 4, NTOK // P // 8
    even = ctx.enter_context(nc.sbuf_tensor("even_rows", [P, BUFS, T, D], F32))
    odd = ctx.enter_context(nc.sbuf_tensor("odd_rows", [P, BUFS, T, D], F32))
    out_v = out[0:NTOK, :].rearrange("(n p t) d -> n p t d", p=P, t=T)
    odd_v = odd_sum[0:NTOK, :].rearrange("(n p t) d -> n p t d", p=P, t=T)
    with nc.Block() as block:
        @block.sync
        def _(sp):
            for n in range(PARTS):
                if n >= BUFS:
                    sp.wait_ge(s[f"w_loaded{n % BUFS}"], 16 * (n // BUFS))
                sp.dma_start(even[:, n % BUFS, :, :], out_v[n]).then_inc(s[f"x_in{n % BUFS}"], 16)
                sp.dma_start(odd[:, n % BUFS, :, :], odd_v[n]).then_inc(s[f"x_in{n % BUFS}"], 16)

        @block.vector
        def _(v):
            for n in range(PARTS):
                v.wait_ge(s[f"x_in{n % BUFS}"], 32 * (n // BUFS + 1))
                v.tensor_tensor(even[:, n % BUFS, :, :], even[:, n % BUFS, :, :], odd[:, n % BUFS, :, :], ALU.add
                                ).then_inc(s["y_made"], 1)

        @block.scalar
        def _(act):
            for n in range(PARTS):
                act.wait_ge(s["y_made"], n + 1)
                act.dma_start(out_v[n], even[:, n % BUFS, :, :]).then_inc(s[f"w_loaded{n % BUFS}"], 16)
            for n in range(BUFS):
                act.wait_ge(s[f"w_loaded{n}"], 16 * (PARTS // BUFS))


def kernel(x, ctx_768, mask_BxS2_bk0, L0_xattn_ln_x_g, L0_xattn_ln_x_b, L0_xattn_ln_l_g, L0_xattn_ln_l_b,
           L0_xattn_qn_g, L0_xattn_kn_g, L0_xattn_Wq, L0_xattn_Wkv, L0_xattn_Wlkv, L0_xattn_Wo, L0_xattn_bo,
           L0_ffn_gate_w, L0_ffn_gate_bias, L0_ffn_w_gate, L0_ffn_w_up, L0_ffn_w_down):
    import concourse.bacc as bacc
    from concourse.bass_utils import run_bass_kernel_spmd

    def chunks(wt, rows):
        return wt.reshape(-1, rows, wt.shape[-1]).transpose(1, 0, 2)

    arr = np.asarray
    mask = arr(mask_BxS2_bk0)
    wg = arr(L0_ffn_w_gate).reshape(E, 2, P, I).transpose(0, 2, 1, 3).reshape(E, P, 2 * I)
    wu = arr(L0_ffn_w_up).reshape(E, 2, P, I).transpose(0, 2, 1, 3).reshape(E, P, 2 * I)
    data = {
        "x": arr(x).reshape(NTOK, D),
        "ctx": arr(ctx_768),
        "mask_col": mask.reshape(B, NCTX, 1),
        "mask_row": mask.reshape(B, 1, NCTX),
        "wqkv": chunks(np.concatenate([arr(L0_xattn_Wq).T, arr(L0_xattn_Wlkv).T], axis=1), P),
        "wkvx": chunks(arr(L0_xattn_Wkv).T, DCTX // 2),
        "wo": arr(L0_xattn_Wo).T.reshape(H, DH, D).transpose(1, 0, 2),
        "gate": chunks(arr(L0_ffn_gate_w).T, P),
        "gate_bias": arr(L0_ffn_gate_bias).reshape(1, E),
        "bo": arr(L0_xattn_bo).reshape(1, D),
        "ln_g": arr(L0_xattn_ln_l_g).reshape(2, P).T,
        "ln_b": arr(L0_xattn_ln_l_b).reshape(2, P).T,
        "lx_g": arr(L0_xattn_ln_x_g).reshape(2, DCTX // 2).T,
        "lx_b": arr(L0_xattn_ln_x_b).reshape(2, DCTX // 2).T,
        "qk_g": np.concatenate([arr(L0_xattn_qn_g), arr(L0_xattn_kn_g)]).reshape(1, 2 * DH),
        "wexp": np.concatenate([wg, wu, arr(L0_ffn_w_down)], axis=2),
    }
    nc = bacc.Bacc("TRN2", target_bir_lowering=False, num_devices=1, dynamic_dma_scratch_size=4096)
    arrays, aps = {}, {}
    for name, value in data.items():
        arrays[f"in_{name}"] = np.ascontiguousarray(value)
        aps[name] = nc.dram_tensor(f"in_{name}", value.shape, mybir.dt.from_np(value.dtype),
                                   kind="ExternalInput").ap()
    out = nc.dram_tensor("out_rows", (NTOK + DUMP, D), F32, kind="ExternalOutput").ap()
    build(nc, aps, out)
    r = run_bass_kernel_spmd(nc, [arrays], core_ids=[0])
    return r.results[0]["out_rows"][:NTOK].reshape(B, S, D)
```
